# Optimizing a Trainium2 kernel written in Bass

```python
import numpy as np
import jax
import jax.numpy as jnp

def _softmax(x, axis=-1):
    return jax.nn.softmax(x, axis=axis)

def _gelu(x):
    return jax.nn.gelu(x, approximate=True)

def _silu(x):
    return jax.nn.silu(x)

def _sigmoid(x):
    return jax.nn.sigmoid(x)

def _layernorm(x, axis=-1, eps=1e-05):
    m = jnp.mean(x, axis=axis, keepdims=True)
    v = jnp.var(x, axis=axis, keepdims=True)
    return (x - m) / jnp.sqrt(v + eps)

def _scatter_add(tgt, idx, src, axis=0):
    return tgt.at[idx].add(src)

def _segment_sum(src, seg, n):
    return jax.ops.segment_sum(src, seg, n)
kernel_name = 'mk_adj_preln_d4_adj_r2_5a9217'

def setup_inputs(seed: int=0):
    np.random.seed(seed)
    _w = jnp.asarray

    def _rec_inputs():
        import jax
        import jax.numpy as jnp
        _gk = jax.random.key(seed)
        x = 0.0002141 + 1 * jax.random.normal(jax.random.fold_in(_gk, 1), (2048, 128), jnp.float32)
        _a = jax.random.bernoulli(jax.random.fold_in(_gk, 2), 0.000976562, (2048, 2048))
        _af = _a.astype(jnp.float32)
        adj = _af
        return (x, adj)
    x, adj = _rec_inputs()

    def _L0_gnn_setup():
        import jax, jax.numpy as jnp
        import numpy as np
        N = 3072
        IN_F = 128
        OUT_F = 128
        H = 4
        OUT_PER_HEAD = OUT_F // H
        ALPHA = 0.2
        NEG_BIG = -9000000000000000.0
        key = jax.random.key(seed)
        k1, k2, k3, k4 = jax.random.split(key, 4)
        h_mat = jax.random.normal(k1, (N, IN_F), dtype=jnp.float32)
        adj = (jax.random.uniform(k2, (N, N)) < 0.05).astype(jnp.float32)
        weight = jax.random.normal(k3, (IN_F, H * OUT_PER_HEAD), dtype=jnp.float32) * (1.0 / np.sqrt(IN_F))
        att_weight = jax.random.normal(k4, (H, 2 * OUT_PER_HEAD), dtype=jnp.float32) * (1.0 / np.sqrt(OUT_PER_HEAD))
        return {'h_mat': h_mat, 'adj': adj, 'weight': weight, 'att_weight': att_weight}
    _L0_gnn_all = _L0_gnn_setup()
    _L0_gnn_in = {k: v for k, v in _L0_gnn_all.items() if k in ('weight', 'att_weight')}
    del _L0_gnn_all

    def _L1_gnn_setup():
        import jax, jax.numpy as jnp
        import numpy as np
        N, E, D = (4096, 4096, 128)
        key = jax.random.key(seed)
        k1, k2 = jax.random.split(key)
        X = jax.random.normal(k1, (N, D), dtype=jnp.float32)
        H = jax.random.uniform(k2, (N, E), dtype=jnp.float32)
        return {'X': X, 'H': H}
    _L1_gnn_all = _L1_gnn_setup()
    _L1_gnn_in = {k: v for k, v in _L1_gnn_all.items() if k in ()}
    del _L1_gnn_all

    def _L2_gnn_setup():
        import jax, jax.numpy as jnp
        import numpy as np
        N, C_IN, C_OUT, K = (4096, 128, 128, 3)
        key = jax.random.key(seed)
        k1, k2, k3 = jax.random.split(key, 3)
        x = jax.random.normal(k1, (N, C_IN), dtype=jnp.float32)
        L = jax.random.normal(k2, (N, N), dtype=jnp.float32) / np.sqrt(N).astype(np.float32)
        W = jax.random.normal(k3, (K, C_OUT, C_IN), dtype=jnp.float32) / np.sqrt(C_IN).astype(np.float32)
        return {'x': x, 'L': L, 'W': W}
    _L2_gnn_all = _L2_gnn_setup()
    _L2_gnn_in = {k: v for k, v in _L2_gnn_all.items() if k in ('W',)}
    del _L2_gnn_all

    def _L3_gnn_setup():
        import jax, jax.numpy as jnp
        import numpy as np
        N_NODE = 2048
        N_FEA_IN = 128
        N_FEA_OUT = 128
        key = jax.random.key(seed)
        k_x, k_a, k_w, k_att = jax.random.split(key, 4)
        stdv_w = 1.0 / np.sqrt(N_FEA_OUT)
        stdv_a = 1.0 / np.sqrt(2 * N_FEA_OUT)
        X = jax.random.normal(k_x, (N_NODE, N_FEA_IN), dtype=jnp.float32)
        A = jax.random.uniform(k_a, (N_NODE, N_NODE), dtype=jnp.float32)
        W = jax.random.uniform(k_w, (N_FEA_IN, N_FEA_OUT), minval=-stdv_w, maxval=stdv_w, dtype=jnp.float32)
        a = jax.random.uniform(k_att, (1, 2 * N_FEA_OUT), minval=-stdv_a, maxval=stdv_a, dtype=jnp.float32)
        return {'X': X, 'A': A, 'W': W, 'a': a}
    _L3_gnn_all = _L3_gnn_setup()
    _L3_gnn_in = {k: v for k, v in _L3_gnn_all.items() if k in ('W', 'a')}
    del _L3_gnn_all
    return {'x': x, 'adj': adj, 'L0_gnn_weight': _L0_gnn_in['weight'], 'L0_gnn_att_weight': _L0_gnn_in['att_weight'], 'L2_gnn_W': _L2_gnn_in['W'], 'L3_gnn_W': _L3_gnn_in['W'], 'L3_gnn_a': _L3_gnn_in['a']}

def reference(x, adj, L0_gnn_weight, L0_gnn_att_weight, L2_gnn_W, L3_gnn_W, L3_gnn_a):
    import jax
    import jax.numpy as jnp

    def _L0_gnn_ref(h_mat, adj, weight, att_weight):
        import jax, jax.numpy as jnp
        import numpy as np
        N = 3072
        IN_F = 128
        OUT_F = 128
        H = 4
        OUT_PER_HEAD = OUT_F // H
        ALPHA = 0.2
        NEG_BIG = -9000000000000000.0
        n = h_mat.shape[0]
        wh = jnp.matmul(h_mat, weight).reshape(n, H, OUT_PER_HEAD)
        a_src = att_weight[:, :OUT_PER_HEAD]
        a_dst = att_weight[:, OUT_PER_HEAD:]
        logit_parent = jnp.einsum('nhf,hf->nh', wh, a_src)
        logit_child = jnp.einsum('nhf,hf->nh', wh, a_dst)
        e = jax.nn.leaky_relu(logit_parent[:, None, :] + logit_child[None, :, :], ALPHA)
        att = jnp.where(adj[..., None] > 0, e, NEG_BIG)
        att = jax.nn.softmax(att, axis=1)
        h_prime = jnp.einsum('njh,jhf->nhf', att, wh)
        return h_prime.reshape(n, -1)

    def _L1_gnn_ref(X, H):
        import jax, jax.numpy as jnp
        import numpy as np
        N, E, D = (4096, 4096, 128)
        msg = jnp.matmul(H.T, X)
        inv_deg = 1.0 / H.sum(axis=0)
        inv_deg = jnp.where(jnp.isinf(inv_deg), 0.0, inv_deg)
        return msg * inv_deg[:, None]

    def _L2_gnn_ref(x, L, W):
        import jax, jax.numpy as jnp
        import numpy as np
        N, C_IN, C_OUT, K = (4096, 128, 128, 3)
        k = W.shape[0]
        T0 = x
        T1 = L @ x
        out = T0 @ W[0].T
        if k > 1:
            out = out + T1 @ W[1].T
        for j in range(2, k):
            T2 = 2.0 * (L @ T1) - T0
            out = out + T2 @ W[j].T
            T0, T1 = (T1, T2)
        return out

    def _L3_gnn_ref(X, A, W, a):
        import jax, jax.numpy as jnp
        import numpy as np
        N_NODE = 2048
        N_FEA_IN = 128
        N_FEA_OUT = 128
        XW = jnp.matmul(X, W)
        f = W.shape[1]
        s_col = jnp.matmul(XW, a[0, :f])
        s_row = jnp.matmul(XW, a[0, f:])
        Z1 = jax.nn.leaky_relu(s_row[:, None] + s_col[None, :], negative_slope=0.01)
        den = jnp.exp(Z1)
        num = jnp.matmul(A, den)
        att = jnp.where(num != 0, den / jnp.where(num != 0, num, 1.0), 0.0)
        H = jnp.matmul(A, jnp.matmul(att, XW))
        return H
    h = jnp.maximum(_layernorm(x, axis=-1), 0.0)
    x = x + _L0_gnn_ref(h, adj, L0_gnn_weight, L0_gnn_att_weight)
    h = jnp.maximum(_layernorm(x, axis=-1), 0.0)
    x = x + _L1_gnn_ref(h, adj)
    h = jnp.maximum(_layernorm(x, axis=-1), 0.0)
    x = x + _L2_gnn_ref(h, adj, L2_gnn_W)
    h = jnp.maximum(_layernorm(x, axis=-1), 0.0)
    x = x + _L3_gnn_ref(h, adj, L3_gnn_W, L3_gnn_a)
    return x

_drawn_inputs = setup_inputs


def setup_inputs(seed=0):
    import zlib

    import numpy as np

    out = dict(_drawn_inputs(seed))
    spreads = {}
    factors = {'L0_gnn_att_weight': 3.122}
    for name, (base, spread) in spreads.items():
        noise = np.random.default_rng([zlib.crc32(name.encode()), seed]).standard_normal(out[name].shape)
        drawn = base * np.exp(spread * noise) if base else spread * noise
        out[name] = jnp.asarray(drawn.astype(out[name].dtype))
    for name, factor in factors.items():
        out[name] = (out[name] * factor).astype(out[name].dtype)
    return out
```

```python
import concourse.bass as bass
from concourse import mybir
from contextlib import ExitStack

F32 = mybir.dt.float32
F32R = mybir.dt.float32r
BF16 = mybir.dt.bfloat16
ALU = mybir.AluOpType
ACT = mybir.ActivationFunctionType
AX_X = mybir.AxisListType.X

P = 128
N = 2048
T = N // P
D = 128
H = 4
F = D // H
F1 = F + 1
HALF = N // 2
HT = T // 2
BANK = 512
PW = 3 * D + 2
PC = 3 * D + 1
EPS = 1e-5
TINY = 1.2e-38
KB = 1024
LOW = 1.25


def gnn_stack(nc, x, adj, w0, att0, w2, w3, a3, out):
    ctx = ExitStack()
    with ctx:
        def at(name, kb, shape, dt=F32):
            return nc.alloc_sbuf_tensor_at(name, shape, dt, offset=int((kb + LOW) * KB))

        def sem(name):
            return ctx.enter_context(nc.semaphore(name))

        A = at("A", 0, [P, T, N], BF16)
        ATr = at("ATr", 0, [P, T, HALF], F32R)
        AT = at("AT", 64, [P, T, N], BF16)
        X = at("X", 128, [P, T, D])
        WH = at("WH", 136, [P, T, H, F1])
        B = 144.5
        a32 = [at(f"a32_{b}", B + 8 * b, [P, N]) for b in range(2)]
        cB = [at(f"cB_{h}", B + 16 + 8 * h, [P, N]) for h in range(H)]
        junk = at("junk", B + 48, [P, N], BF16)
        attB = at("attB", B + 48, [P, H, 2 * F])
        W0 = at("W0", B + 49, [P, D])
        h0 = at("h0", B + 52, [P, T, D])
        hT0 = at("hT0", B + 60, [P, N])
        whc = [at(f"whc_{e}", B + 2.25 * e, [P, T, F1]) for e in range(2)]
        oT = [at(f"oT_{e}", B + 5 + 4 * e, [F1, HALF]) for e in range(2)]
        pmB = at("pmB", B + 13, [P, N])
        p2B = at("p2B", B + 21, [P, N])
        ub = [at(f"ub_{b}", B + 29 + 4 * b, [P, HALF]) for b in range(2)]
        vb = [at(f"vb_{b}", B + 37 + 4 * b, [P, HALF]) for b in range(2)]
        pb = [at(f"pb_{b}", B + 45 + 4 * b, [P, HALF]) for b in range(2)]
        diag = [at(f"diag_{b}", B + 53 + 2 * b, [P, BANK]) for b in range(2)]
        O = at("O", B + 57, [P, T, H, F1])
        Os = at("Os", B + 29, [P, T, H, F1])
        acc = at("acc", B + 15, [P, T, PC])
        pcs = at("pcs", B + 39.5, [P, T, PW], BF16)
        h1 = at("h1", B + 52, [P, T, D])
        s1 = at("s1", B + 60, [P, T, D])
        hT2 = at("hT2", B + 60, [P, N])
        ys = at("ys", 136, [P, T, 3 * D])
        den_hi = [at(f"den_hi_{b}", 136 + 8 * b, [P, T, P], F32R) for b in range(2)]
        den_lo = [at(f"den_lo_{b}", 152 + 8 * b, [P, T, P], F32R) for b in range(2)]
        h3 = at("h3", 152, [P, T, D])
        hT3 = at("hT3", 160, [P, N])
        pr3 = at("pr3", 136, [P, T, D])
        zb = [at(f"zb_{b}", 168 + 4 * b, [P, HT, P]) for b in range(2)]
        dv = [at(f"dv_{b}", 176 + 2 * b, [P, BANK]) for b in range(2)]
        diag3 = [at(f"diag3_{b}", 168 + 2 * b, [P, BANK]) for b in range(2)]
        cB3 = at("cB3", 180, [P, N])
        rB3 = at("rB3", 188, [P, N])
        dT = [at(f"dT_{b}", 196 + 2 * b, [P, BANK]) for b in range(2)]
        mx = [at(f"mx_{b}", 200 + 2 * b, [P, BANK]) for b in range(2)]
        XW = at("XW", 204, [P, T, D])
        uT = at("uT", 136, [P, N])
        Un = at("Un", 144, [P, T, D])
        acc3 = at("acc3", 152, [P, T, PC])
        pcs3 = at("pcs3", 176.5, [P, T, PW], BF16)
        s3 = [at("s3_0", 189, [P, T, D]), at("s3_1", 197, [P, T, D])]

        top = [(LOW + 212.5) * KB]

        def const(name, shape, dt=F32):
            size = 1
            for n in shape[1:]:
                size *= n
            size = -(-size * (2 if dt == BF16 else 4) // 32) * 32
            t = nc.alloc_sbuf_tensor_at(name, shape, dt, offset=int(top[0]))
            top[0] += size
            return t

        ident = const("ident", [P, P])
        identb = const("identb", [P, P], BF16)
        ones = const("ones", [P, P])
        zeros = const("zeros", [P, P], BF16)
        W3 = const("W3", [P, D])
        a3B = const("a3B", [P, 2, D])
        W2 = const("W2", [P, 3, D])
        stats = const("stats", [P, T, 6])
        mv = const("mv", [P, T, 2])
        var = const("var", [P, T])
        power = const("power", [P, T])
        rstd = const("rstd", [P, T])
        pcol = const("pcol", [P, T, H])
        ccol = const("ccol", [P, T, H])
        cmax = const("cmax", [P, T, H])
        mcol = const("mcol", [P, T, H])
        tcol = const("tcol", [P, T, H])
        cmin = const("cmin", [P, H])
        pmcol = const("pmcol", [P, H, T])
        p2col = const("p2col", [P, H, T])
        c2col = const("c2col", [P, H, T])
        c1col = const("c1col", [P, H, T])
        cc = [const(f"cc_{e}", [P, T]) for e in range(2)]
        cc2 = [const(f"cc2_{e}", [P, T]) for e in range(2)]
        wsum = const("wsum", [P, H, F1])
        xwc = [const(f"xwc_{b}", [P, D]) for b in range(2)]
        c3 = const("c3", [P, T])
        c3s = const("c3s", [P, T])
        r3 = const("r3", [P, T])
        inv = const("inv", [P, T])
        deg = const("deg", [P, T])

        bank = [ctx.enter_context(nc.psum_tensor(f"bank{i}", [P, BANK], F32)) for i in range(8)]
        bankb = [b[:, :].bitcast(BF16) for b in bank]

        x_loaded = sem("x_loaded")
        w_loaded = sem("w_loaded")
        a_loaded = [sem(f"a_loaded{b}") for b in range(2)]
        a_ready = sem("a_ready")
        const_ready = sem("const_ready")
        vec = sem("vec")
        h_ready = sem("h_ready")
        var_ready = sem("var_ready")
        rstd_ready = sem("rstd_ready")
        hT_banks = sem("hT_banks")
        hT_ready = sem("hT_ready")
        w2T_banks = sem("w2T_banks")
        w2_ready = sem("w2_ready")
        proj_banks = sem("proj_banks")
        proj_ready = sem("proj_ready")
        wsum_bank = sem("wsum_bank")
        wsum_ready = sem("wsum_ready")
        logits_ready = sem("logits_ready")
        diag_ready = sem("diag_ready")
        bc_bank = sem("bc_bank")
        bc_copied = sem("bc_copied")
        at_bank = sem("at_bank")
        at_copied = sem("at_copied")
        guard_ready = sem("guard_ready")
        cur_ready = sem("cur_ready")
        uv_ready = sem("uv_ready")
        uv_free = sem("uv_free")
        p_ready = sem("p_ready")
        p_free = sem("p_free")
        oT_ready = sem("oT_ready")
        o_turned = sem("o_turned")
        o_kept = sem("o_kept")
        pieces_ready = sem("pieces_ready")
        mm_bank = sem("mm_bank")
        mm_copied = sem("mm_copied")
        atr_ready = sem("atr_ready")
        half_done = sem("half_done")
        xw_cur = sem("xw_cur")
        z_ready = sem("z_ready")
        den_ready = sem("den_ready")
        lo_ready = sem("lo_ready")
        num_bank = sem("num_bank")
        num_free = sem("num_free")
        dT_ready = sem("dT_ready")
        rec_ready = sem("rec_ready")
        att_ready = sem("att_ready")
        att_free = sem("att_free")
        u_bank = sem("u_bank")
        uT_ready = sem("uT_ready")
        u_turned = sem("u_turned")
        un_ready = sem("un_ready")
        pmax = sem("pmax")
        rec_seq = sem("rec_seq")
        act_seq = sem("act_seq")
        leaky_ready = sem("leaky_ready")
        dmax = sem("dmax")
        x_final = sem("x_final")
        passed = sem("passed")
        stored = sem("stored")

        CREDIT = {uv_free: 2, p_free: 2, oT_ready: 4, o_turned: 2, o_kept: 2, at_copied: 4, mm_copied: 2,
                  num_bank: 4, num_free: 4, att_ready: 2, att_free: 2}

        def apart(engine):
            engine.sem_inc(passed, 1)

        def steps(engine, lead, follow, turn=None):
            lead(0, 0, 0)
            for half in range(2):
                s0 = T * half
                with engine.Fori(0, HT - 1) as g:
                    for b in range(2):
                        lead(s0 + 2 * g + b + 1, 2 * g + b + 1, (b + 1) % 2)
                        follow(s0 + 2 * g + b, 2 * g + b, b, half)
                lead(s0 + T - 1, T - 1, 1)
                follow(s0 + T - 2, T - 2, 0, half)
                if half == 0:
                    if turn is not None:
                        turn()
                    lead(T, 0, 0)
                follow(s0 + T - 1, T - 1, 1, half)

        block = ctx.enter_context(nc.Block())

        @block.sync
        def _(sp):
            sp.dma_start(X[:, :, :], x.rearrange("(t p) f -> p t f", p=P)).then_inc(x_loaded, 16)

            def load(it, b):
                sp.dma_start(a32[b][:, :], adj[bass.ds(it * P, P), :]).then_inc(a_loaded[b], 16)

            load(0, 0)
            load(1, 1)
            with sp.Fori(1, HT) as g:
                for b in range(2):
                    sp.wait_ge(a_ready, 2 * g + b - 1)
                    load(2 * g + b, b)
            sp.wait_ge(x_final, 1)
            sp.dma_start(out.rearrange("(t p) f -> p t f", p=P), X[:, :, :]).then_inc(stored, 16)
            sp.wait_ge(stored, 16)

        @block.gpsimd
        def _(pool):
            for free, count in CREDIT.items():
                pool.sem_inc(free, count)
            nc.gpsimd.memset(ones[:, :], 1.0).then_inc(const_ready, 1)
            nc.gpsimd.memset(zeros[:, :], 0.0).then_inc(const_ready, 1)
            nc.gpsimd.memset(power[:, :], -0.5).then_inc(const_ready, 1)
            nc.gpsimd.memset(WH[:, :, :, F:F1], 1.0).then_inc(const_ready, 1)
            pool.wait_ge(const_ready, 4)
            nc.gpsimd.affine_select(out=ident[:, :], in_=ones[:, :], compare_op=ALU.is_equal, fill=0.0, base=0,
                                    pattern=[[-1, P]], channel_multiplier=1).then_inc(const_ready, 1)
            pool.wait_ge(const_ready, 5)
            nc.gpsimd.tensor_copy(identb[:, :], ident[:, :]).then_inc(const_ready, 1)

            def rstd_of(layer):
                pool.wait_ge(var_ready, layer + 1)
                nc.gpsimd.tensor_tensor(rstd[:, :], var[:, :], power[:, :], ALU.pow).then_inc(rstd_ready, 1)

            def diagonal(dst, col, n):
                if not isinstance(n, int) or n >= 2:
                    pool.wait_ge(bc_bank, n - 1)
                if not isinstance(n, int):
                    apart(pool)
                nc.gpsimd.tensor_tensor(dst[:, :].rearrange("p (t q) -> p t q", q=P),
                                        ident[:, :].unsqueeze(1).to_broadcast([P, 4, P]),
                                        col.unsqueeze(2).to_broadcast([P, 4, P]), ALU.mult).then_inc(diag_ready, 1)

            rstd_of(0)
            pool.wait_ge(logits_ready, 1)
            for n in range(16):
                diagonal(diag[n % 2], c1col[:, n // 4, 4 * (n % 4):4 * (n % 4) + 4], n)
            pool.wait_ge(guard_ready, 1)
            pool.wait_ge(bc_copied, 16)
            with pool.Fori(0, 2) as g:
                for e in range(2):
                    h = 2 * g + e
                    pool.wait_ge(oT_ready, 4 * g + 2 * e + 2)
                    nc.gpsimd.tensor_copy(whc[e][:, :, :], WH[:, :, bass.ds(h, 1), :].rearrange("p t o f -> p t (o f)")).then_inc(cur_ready, 1)
                    nc.gpsimd.tensor_copy(cc[e][:, :], c1col[:, bass.ds(h, 1), :].rearrange("p o t -> p (o t)")).then_inc(cur_ready, 1)
                    nc.gpsimd.tensor_copy(cc2[e][:, :], c2col[:, bass.ds(h, 1), :].rearrange("p o t -> p (o t)")).then_inc(cur_ready, 1)
                    for half in range(2):
                        for k in range(4):
                            col = (pmcol, p2col)[k // 2]
                            t0 = HT * half + 4 * (k % 2)
                            diagonal(diag[k % 2], col[:, bass.ds(h, 1), t0:t0 + 4].rearrange("p o t -> p (o t)"),
                                     16 + 16 * g + 8 * e + 4 * half + k)
            rstd_of(1)
            rstd_of(2)
            rstd_of(3)
            pool.wait_ge(logits_ready, 2)
            n0 = 48
            for k in range(8):
                diagonal(diag3[k % 2], (c3, r3)[k // 4][:, 4 * (k % 4):4 * (k % 4) + 4], n0 + k)
            pool.wait_ge(bc_bank, n0 + 8)
            pool.wait_ge(bc_copied, n0 + 8)

            def z_step(jt, s=None):
                for q in range(2):
                    if s is not None:
                        pool.wait_ge(lo_ready, 2 * s + q + 1)
                        if not isinstance(s, int):
                            apart(pool)
                    nc.gpsimd.tensor_tensor(zb[q][:, :, :],
                                            cB3[:, bass.ds(jt * P, P)].unsqueeze(1).to_broadcast([P, HT, P]),
                                            r3[:, HT * q:HT * q + HT].unsqueeze(2).to_broadcast([P, HT, P]),
                                            ALU.add).then_inc(z_ready, 1)

            def lo_step(s, jt, b):
                for q in range(2):
                    pool.wait_ge(den_ready, 2 * s + q + 1)
                    qs = slice(HT * q, HT * q + HT)
                    nc.gpsimd.tensor_tensor(den_lo[b][:, qs, :], zb[q][:, :, :], den_hi[b][:, qs, :].bitcast(F32),
                                            ALU.subtract).then_inc(lo_ready, 1)
                if isinstance(jt, int) and jt == T - 1:
                    if s == T - 1:
                        z_step(0, s)
                else:
                    z_step(jt + 1, s)

            def att_step(s, jt, b, half):
                for c in range(2):
                    pool.wait_ge(rec_ready, 2 * s + c + 1)
                    nc.gpsimd.tensor_tensor(mx[c][:, :], dT[c][:, :], mx[c][:, :], ALU.mult).then_inc(att_ready, 1)

            z_step(0)
            steps(pool, lo_step, att_step)

        @block.scalar
        def _(act):
            act.dma_start(W0[:, :], w0).then_inc(w_loaded, 16)
            act.dma_start(attB[:, :, :].rearrange("p h f -> p (h f)"),
                          att0.rearrange("h f -> (h f)").partition_broadcast(P)).then_inc(w_loaded, 16)
            act.dma_start(W2[:, :, :], w2.rearrange("k o c -> o k c")).then_inc(w_loaded, 16)
            act.dma_start(W3[:, :], w3).then_inc(w_loaded, 16)
            act.dma_start(a3B[:, :, :].rearrange("p k f -> p (k f)"),
                          a3.rearrange("o f -> (o f)").partition_broadcast(P)).then_inc(w_loaded, 16)

            def turn_h(dst, use):
                for q in range(4):
                    act.wait_ge(hT_banks, 4 * use + q + 1)
                    nc.scalar.copy(dst[:, q * BANK:(q + 1) * BANK], bank[q][:, :]).then_inc(hT_ready, 1)

            turn_h(hT0, 0)
            for n in range(16):
                act.wait_ge(bc_bank, n + 1)
                nc.scalar.copy(cB[n // 4][:, (n % 4) * BANK:(n % 4 + 1) * BANK], bank[4 + n % 2][:, :]).then_inc(bc_copied, 1)
            with act.Fori(0, HT) as g:
                for b in range(2):
                    act.wait_ge(a_loaded[b], 16 * g + 16)
                    nc.scalar.copy(A[:, bass.ds(2 * g + b, 1), :].rearrange("p o n -> p (o n)"), a32[b][:, :]).then_inc(a_ready, 1)

            with act.Fori(0, 2) as g:
                for e in range(2):
                    for half in range(2):
                        u = 4 * g + 2 * e + half
                        for k in range(4):
                            n = 16 + 4 * u + k
                            lo = HALF * half + BANK * (k % 2)
                            act.wait_ge(bc_bank, n + 1)
                            nc.scalar.copy((pmB, p2B)[k // 2][:, lo:lo + BANK], bank[4 + k % 2][:, :]).then_inc(bc_copied, 1)
                        act.wait_ge(bc_copied, 16 + 4 * u + 4)
                        act.wait_ge(cur_ready, 6 * g + 3 * e + 3)
                        hs = slice(HALF * half, HALF * half + HALF)
                        for jt in range(T):
                            act.wait_ge(uv_free, T * u + jt + 1)
                            nc.scalar.activation(ub[jt % 2][:, :], pmB[:, hs], ACT.Exp, bias=cc[e][:, jt:jt + 1]).then_inc(uv_ready, 1)
                            nc.scalar.activation(vb[jt % 2][:, :], p2B[:, hs], ACT.Exp, bias=cc2[e][:, jt:jt + 1]).then_inc(uv_ready, 1)
                        act.wait_ge(p_free, T * u + T + 2)
                        act.wait_ge(o_turned, u + 1)
                        nc.scalar.copy(oT[half][:, 0:BANK], bank[2 * half][0:F1, :])
                        nc.scalar.copy(oT[half][:, BANK:HALF], bank[2 * half + 1][0:F1, :]).then_inc(oT_ready, 1)

            def products(dst, base):
                with act.Fori(0, HT) as g:
                    for b in range(2):
                        act.wait_ge(mm_bank, base + 2 * g + b + 1)
                        nc.scalar.copy(dst[:, bass.ds(2 * g + b, 1), :].rearrange("p o n -> p (o n)"),
                                       bank[b][:, 0:PC]).then_inc(mm_copied, 1)

            products(acc, 0)
            turn_h(hT2, 1)
            for t in range(T):
                act.wait_ge(proj_banks, 4 + t + 1)
                nc.scalar.copy(ys[:, t, :], bank[4 + t % 4][:, 0:3 * D]).then_inc(proj_ready, 1)
            products(acc, T)
            products(acc, 2 * T)
            turn_h(hT3, 2)
            for q in range(4):
                act.wait_ge(proj_banks, 4 + T + q + 1)
                nc.scalar.copy(XW[:, 4 * q:4 * q + 4, :].rearrange("p t f -> p (t f)"), bank[4 + q][:, :]).then_inc(proj_ready, 1)
            for k in range(8):
                act.wait_ge(bc_bank, 48 + k + 1)
                nc.scalar.copy((cB3, rB3)[k // 4][:, (k % 4) * BANK:(k % 4 + 1) * BANK], bank[4 + k % 2][:, :]).then_inc(bc_copied, 1)
            act.wait_ge(bc_copied, 56)

            def den_step(s, jt, b):
                act.wait_ge(num_bank, 2 * s + 2)
                for q in range(2):
                    z = zb[q][:, :, :]
                    act.wait_ge(leaky_ready, 2 * s + q + 1)
                    nc.scalar.activation(z, z, ACT.Exp).then_inc(act_seq, 1)
                    act.wait_ge(act_seq, 2 * s + q + 1)
                    nc.scalar.copy(den_hi[b][:, HT * q:HT * q + HT, :], z).then_inc(den_ready, 1)

            def dT_step(s, jt, b, half):
                for c in range(2):
                    act.wait_ge(att_ready, 2 * s + c + 1)
                    apart(act)
                    lo = HALF * half + BANK * c
                    nc.scalar.activation(dT[c][:, :], rB3[:, lo:lo + BANK], ACT.Exp, bias=c3[:, bass.ds(jt, 1)])
                    nc.scalar.activation(dv[c][:, :], rB3[:, lo:lo + BANK], ACT.Exp, bias=c3s[:, bass.ds(jt, 1)],
                                         scale=0.01).then_inc(dT_ready, 1)
                act.wait_ge(att_free, s + 1)
                nc.scalar.copy(xwc[b][:, :], XW[:, bass.ds(jt, 1), :].rearrange("p o f -> p (o f)")).then_inc(xw_cur, 1)

            steps(act, den_step, dT_step)
            for q in range(4):
                act.wait_ge(u_bank, q + 1)
                nc.scalar.copy(uT[:, q * BANK:(q + 1) * BANK], bank[4 + q][:, :]).then_inc(uT_ready, 1)
            for q in range(4):
                act.wait_ge(u_turned, q + 1)
                nc.scalar.copy(Un[:, 4 * q:4 * q + 4, :].rearrange("p t f -> p (t f)"), bank[q][:, :]).then_inc(un_ready, 1)
            products(acc3, 3 * T)

        @block.tensor
        def _(pe):
            def turn_h(src, layer, use):
                pe.wait_ge(h_ready, layer + 1)
                for t in range(T):
                    last = nc.tensor.transpose(bank[t // 4][:, P * (t % 4):P * (t % 4) + P], src[:, t, :], ident[:, :])
                    if t % 4 == 3:
                        last.then_inc(hT_banks, 1)

            def broadcast(dg, n, b):
                pe.wait_ge(diag_ready, n + 1)
                if not isinstance(n, int) or n >= 2:
                    pe.wait_ge(bc_copied, n - 1)
                nc.tensor.matmul(bank[4 + b][:, :], ones[:, :], dg[b][:, :], start=True, stop=True).then_inc(bc_bank, 1)

            pe.wait_ge(const_ready, 6)
            turn_h(h0, 0, 0)
            pe.wait_ge(w_loaded, 80)
            for k in range(3):
                last = nc.tensor.transpose(bank[6][:, P * k:P * k + P], W2[:, k, :], ident[:, :])
            last.then_inc(w2T_banks, 1)
            pe.wait_ge(w2_ready, 1)
            for t in range(T):
                pe.wait_ge(hT_ready, t // 4 + 1)
                last = nc.tensor.matmul(bank[4 + t // 4][:, P * (t % 4):P * (t % 4) + P], hT0[:, P * t:P * t + P],
                                        W0[:, :], start=True, stop=True)
                if t % 4 == 3:
                    last.then_inc(proj_banks, 1)
            pe.wait_ge(proj_ready, 4)
            for t in range(T):
                last = nc.tensor.matmul(bank[7][:, 0:H * F1], ones[:, :], WH[:, t, :, :].rearrange("p h f -> p (h f)"),
                                        start=t == 0, stop=t == T - 1)
            last.then_inc(wsum_bank, 1)
            for n in range(16):
                broadcast(diag, n, n % 2)

            pe.wait_ge(hT_ready, 4)
            with pe.Fori(0, HT) as g:
                for b in range(2):
                    it = 2 * g + b
                    pe.wait_ge(a_ready, it + 1)
                    for grp in range(2):
                        pe.wait_ge(at_copied, 2 * it + grp + 1)
                        for k in range(8):
                            jt = 8 * grp + k
                            last = nc.tensor.transpose(
                                bankb[2 * b + grp][:, P * k:P * k + P],
                                A[:, bass.ds(it, 1), P * jt:P * jt + P].rearrange("p o n -> p (o n)"), identb[:, :])
                        last.then_inc(at_bank, 1)

            pe.wait_ge(at_copied, 2 * T + 4)
            pe.wait_ge(wsum_ready, 1)
            with pe.Fori(0, 2) as g:
                for e in range(2):
                    for half in range(2):
                        u = 4 * g + 2 * e + half
                        for k in range(4):
                            broadcast(diag, 16 + 4 * u + k, k % 2)
                        pe.wait_ge(cur_ready, 6 * g + 3 * e + 3)
                        pe.wait_ge(oT_ready, u + 3)
                        for jt in range(T):
                            pe.wait_ge(p_ready, T * u + jt + 1)
                            for c in range(2):
                                last = nc.tensor.matmul(bank[2 * half + c][0:F1, :], whc[e][:, jt, :],
                                                        pb[jt % 2][:, BANK * c:BANK * c + BANK],
                                                        start=jt == 0, stop=jt == T - 1)
                            last.then_inc(p_free, 1)
                        pe.wait_ge(oT_ready, u + 5)
                        pe.wait_ge(o_kept, u + 1)
                        for t in range(HT):
                            last = nc.tensor.matmul(bank[6 + half][:, F1 * t:F1 * t + F1], oT[half][:, P * t:P * t + P],
                                                    ident[0:F1, 0:F1], start=True, stop=True)
                        last.then_inc(o_turned, 1)

            def product(adjacency, pieces, number):
                pe.wait_ge(pieces_ready, number + 1)
                base = T * number
                with pe.Fori(0, HT) as g:
                    for b in range(2):
                        i = 2 * g + b
                        pe.wait_ge(mm_copied, base + i + 1)
                        for kt in range(T):
                            last = nc.tensor.matmul(bank[b][:, 0:PC], adjacency[:, kt, bass.ds(i * P, P)],
                                                    pieces[:, kt, 0:PC], start=kt == 0, stop=kt == T - 1)
                        last.then_inc(mm_bank, 1)

            product(A, pcs, 0)
            pe.wait_ge(mm_copied, T + 2)
            turn_h(h1, 2, 1)
            for t in range(T):
                pe.wait_ge(hT_ready, 4 + t // 4 + 1)
                if t >= 4:
                    pe.wait_ge(proj_ready, 4 + t - 3)
                nc.tensor.matmul(bank[4 + t % 4][:, 0:3 * D], hT2[:, P * t:P * t + P],
                                 W2[:, :, :].rearrange("p k o -> p (k o)"), start=True, stop=True).then_inc(proj_banks, 1)
            product(AT, pcs, 1)
            product(AT, pcs, 2)
            pe.wait_ge(mm_copied, 3 * T + 2)
            turn_h(h3, 3, 2)
            for t in range(T):
                pe.wait_ge(hT_ready, 8 + t // 4 + 1)
                last = nc.tensor.matmul(bank[4 + t // 4][:, P * (t % 4):P * (t % 4) + P], hT3[:, P * t:P * t + P],
                                        W3[:, :], start=True, stop=True)
                if t % 4 == 3:
                    last.then_inc(proj_banks, 1)
            pe.wait_ge(proj_ready, 8 + T)
            for k in range(8):
                broadcast(diag3, 48 + k, k % 2)
            pe.wait_ge(bc_copied, 56)
            for c in range(4):
                last = nc.tensor.matmul(bank[4 + c][:, :], zeros[:, :], zeros[:, 0:1].to_broadcast([P, BANK]),
                                        start=True, stop=False)

            def num_step(s, jt, b):
                pe.wait_ge(lo_ready, 2 * s + 2)
                pe.wait_ge(num_free, 2 * s + 2)
                for kt in range(T):
                    if isinstance(s, int) and s % T == 0:
                        pe.wait_ge(atr_ready, s + kt + 1)
                    for part, den in enumerate((den_hi, den_lo)):
                        for c in range(2):
                            last = nc.tensor.matmul(bank[2 * b + c][:, :], den[b][:, kt, :],
                                                    ATr[:, kt, BANK * c:BANK * c + BANK],
                                                    start=kt == 0 and part == 0, stop=kt == T - 1 and part == 1)
                            if kt == T - 1 and part == 1:
                                last.then_inc(num_bank, 1)

            def u_step(s, jt, b, half):
                pe.wait_ge(xw_cur, s + 1)
                for c in range(2):
                    pe.wait_ge(att_ready, 2 * s + c + 3)
                    last = nc.tensor.matmul(bank[4 + 2 * half + c][:, :], xwc[b][:, :], mx[c][:, :], start=False,
                                            stop=False)
                last.then_inc(att_free, 1)

            steps(pe, num_step, u_step)
            for c in range(4):
                nc.tensor.matmul(bank[4 + c][:, :], zeros[:, :], zeros[:, 0:1].to_broadcast([P, BANK]),
                                 start=False, stop=True).then_inc(u_bank, 1)
            pe.wait_ge(num_free, 4 * T + 4)
            for t in range(T):
                pe.wait_ge(uT_ready, t // 4 + 1)
                last = nc.tensor.transpose(bank[t // 4][:, P * (t % 4):P * (t % 4) + P], uT[:, P * t:P * t + P],
                                           ident[:, :])
                if t % 4 == 3:
                    last.then_inc(u_turned, 1)
            product(AT, pcs3, 3)

        @block.vector
        def _(dve):
            done = [0]

            def then(instruction):
                done[0] += 1
                instruction.then_inc(vec, 1)
                dve.wait_ge(vec, done[0])

            def layernorm(layer, dst):
                for t in range(T):
                    last = nc.vector.bn_stats(stats[:, t, :], X[:, t, :])
                then(last)
                for t in range(T):
                    last = nc.vector.bn_aggr(mv[:, t, :], stats[:, t, :])
                then(last)
                nc.vector.tensor_scalar(var[:, :], mv[:, :, 1:2].rearrange("p t o -> p (t o)"), EPS, None,
                                        ALU.add).then_inc(var_ready, 1)
                dve.wait_ge(rstd_ready, layer + 1)
                for t in range(T):
                    last = nc.vector.tensor_scalar(dst[:, t, :], X[:, t, :], mv[:, t, 0:1], rstd[:, t:t + 1],
                                                   ALU.subtract, ALU.mult)
                then(last)
                done[0] += 1
                nc.vector.tensor_scalar(dst[:, :, :], dst[:, :, :], 0.0, None, ALU.max).then_inc(vec, 1)
                dve.wait_ge(vec, done[0])
                dve.sem_inc(h_ready, 1)

            def split(src, dst, rest):
                then(nc.vector.tensor_copy(dst[:, :, 0:D], src))
                then(nc.vector.tensor_tensor(rest[:, :, :], src, dst[:, :, 0:D], ALU.subtract))
                then(nc.vector.tensor_copy(dst[:, :, D:2 * D], rest[:, :, :]))
                nc.vector.tensor_tensor(dst[:, :, 2 * D:3 * D], rest[:, :, :], dst[:, :, D:2 * D],
                                        ALU.subtract).then_inc(pieces_ready, 1)

            def join(src, dst):
                then(nc.vector.tensor_tensor(dst[:, :, :], src[:, :, 2 * D:3 * D], src[:, :, D:2 * D], ALU.add))
                then(nc.vector.tensor_tensor(dst[:, :, :], dst[:, :, :], src[:, :, 0:D], ALU.add))

            dve.wait_ge(x_loaded, 16)
            layernorm(0, h0)
            dve.wait_ge(w2T_banks, 1)
            then(nc.vector.tensor_copy(W2[:, :, :].rearrange("p k o -> p (k o)"), bank[6][:, 0:3 * D]))
            nc.vector.tensor_tensor(W2[:, 0, :], W2[:, 0, :], W2[:, 2, :], ALU.subtract).then_inc(w2_ready, 1)
            for q in range(4):
                dve.wait_ge(proj_banks, q + 1)
                nc.vector.tensor_copy(WH[:, 4 * q:4 * q + 4, :, 0:F],
                                      bank[4 + q][:, :].rearrange("p (t h f) -> p t h f", t=4, h=H)).then_inc(proj_ready, 1)
            dve.wait_ge(proj_ready, 4)
            pr = h0[:, :, :].rearrange("p t (h f) -> p t h f", h=H)
            for k, col in enumerate((pcol, ccol)):
                then(nc.vector.tensor_tensor(pr, WH[:, :, :, 0:F],
                                             attB[:, :, F * k:F * k + F].unsqueeze(1).to_broadcast([P, T, H, F]), ALU.mult))
                then(nc.vector.tensor_reduce(col[:, :, :], pr, AX_X, ALU.add))
            then(nc.vector.tensor_copy(c1col[:, :, :].rearrange("p h t -> p t h"), ccol[:, :, :]))
            nc.vector.tensor_scalar(c2col[:, :, :], c1col[:, :, :], 0.2, None, ALU.mult).then_inc(logits_ready, 1)
            dve.wait_ge(wsum_bank, 1)
            nc.vector.tensor_copy(wsum[:, :, :].rearrange("p h f -> p (h f)"), bank[7][:, 0:H * F1]).then_inc(wsum_ready, 1)
            for h in range(H):
                dve.wait_ge(bc_copied, 4 * h + 4)
                then(nc.vector.tensor_reduce(cmin[:, h:h + 1], cB[h][:, :], AX_X, ALU.min))
                then(nc.vector.tensor_scalar(cmin[:, h:h + 1], cmin[:, h:h + 1], 1.0, None, ALU.subtract))
                then(nc.vector.tensor_scalar(cB[h][:, :], cB[h][:, :], cmin[:, h:h + 1], None, ALU.subtract))

            for it in range(T):
                for grp in range(2):
                    dve.wait_ge(at_bank, 2 * it + grp + 1)
                    nc.vector.tensor_copy(AT[:, 8 * grp:8 * grp + 8, P * it:P * it + P],
                                          bankb[2 * (it % 2) + grp][:, :].rearrange("p (j i) -> p j i", j=8)
                                          ).then_inc(at_copied, 1)
                for h in range(H):
                    last = nc.vector.tensor_tensor_reduce(out=junk[:, :], in0=A[:, it, :], in1=cB[h][:, :], scale=1.0,
                                                          scalar=0.0, op0=ALU.mult, op1=ALU.max,
                                                          accum_out=cmax[:, it, h:h + 1])
                    then(last)
            then(nc.vector.tensor_tensor(cmax[:, :, :], cmax[:, :, :],
                                         cmin[:, :].unsqueeze(1).to_broadcast([P, T, H]), ALU.add))
            then(nc.vector.tensor_tensor(cmax[:, :, :], cmax[:, :, :], pcol[:, :, :], ALU.add))
            then(nc.vector.tensor_scalar(tcol[:, :, :], cmax[:, :, :], 0.2, None, ALU.mult))
            then(nc.vector.tensor_tensor(mcol[:, :, :], cmax[:, :, :], tcol[:, :, :], ALU.max))
            then(nc.vector.tensor_tensor(pmcol[:, :, :].rearrange("p h t -> p t h"), pcol[:, :, :], mcol[:, :, :],
                                         ALU.subtract))
            then(nc.vector.tensor_scalar(tcol[:, :, :], pcol[:, :, :], 0.2, None, ALU.mult))
            nc.vector.tensor_tensor(p2col[:, :, :].rearrange("p h t -> p t h"), tcol[:, :, :], mcol[:, :, :],
                                    ALU.subtract).then_inc(guard_ready, 1)

            dve.wait_ge(at_copied, 2 * T + 4)
            with dve.Fori(0, 2) as g:
                for e in range(2):
                    for half in range(2):
                        u = 4 * g + 2 * e + half
                        for jt in range(T):
                            n = T * u + jt
                            b = jt % 2
                            dve.wait_ge(uv_ready, 2 * n + 2)
                            nc.vector.tensor_tensor(ub[b][:, :], ub[b][:, :], vb[b][:, :], ALU.max).then_inc(pmax, 1)
                            dve.wait_ge(pmax, n + 1)
                            dve.wait_ge(p_free, n + 1)
                            nc.vector.tensor_tensor(pb[b][:, :], ub[b][:, :], AT[:, jt, HALF * half:HALF * half + HALF],
                                                    ALU.min).then_inc(p_ready, 1)
                            dve.wait_ge(p_ready, n + 1)
                            dve.sem_inc(uv_free, 1)
                        dve.wait_ge(o_turned, u + 3)
                        nc.vector.tensor_copy(O[:, HT * half:HT * half + HT, bass.ds(2 * g + e, 1), :].rearrange("p t o f -> p t (o f)"),
                                              bank[6 + half][:, 0:HT * F1].rearrange("p (t f) -> p t f", f=F1)
                                              ).then_inc(o_kept, 1)
            dve.wait_ge(o_kept, 8 + 2)
            Ow, Osw = (t[:, :, :, :].rearrange("p t h f -> p t (h f)") for t in (O, Os))
            then(nc.vector.tensor_scalar(tcol[:, :, :].unsqueeze(3), O[:, :, :, F:F1], 0.0, None, ALU.is_equal))
            then(nc.vector.tensor_tensor(Os[:, :, :, :], tcol[:, :, :].unsqueeze(3).to_broadcast([P, T, H, F1]),
                                         wsum[:, :, :].unsqueeze(1).to_broadcast([P, T, H, F1]), ALU.mult))
            then(nc.vector.tensor_tensor(Ow, Ow, Osw, ALU.add))
            then(nc.vector.reciprocal(tcol[:, :, :].unsqueeze(3), O[:, :, :, F:F1]))
            then(nc.vector.tensor_tensor(O[:, :, :, 0:F], O[:, :, :, 0:F],
                                         tcol[:, :, :].unsqueeze(3).to_broadcast([P, T, H, F]), ALU.mult))
            X4 = X[:, :, :].rearrange("p t (h f) -> p t h f", h=H)
            then(nc.vector.tensor_tensor(X4, X4, O[:, :, :, 0:F], ALU.add))

            layernorm(1, h1)
            then(nc.vector.memset(pcs[:, :, 3 * D:PW], 1.0))
            split(h1[:, :, :], pcs, s1)
            dve.wait_ge(mm_copied, T + 2)
            dg = acc[:, :, 3 * D:PC].rearrange("p t o -> p (t o)")
            then(nc.vector.tensor_scalar(inv[:, :], dg, 0.0, None, ALU.is_equal))
            then(nc.vector.tensor_tensor(deg[:, :], dg, inv[:, :], ALU.add))
            then(nc.vector.reciprocal(deg[:, :], deg[:, :]))
            then(nc.vector.tensor_scalar(inv[:, :], dg, 0.0, None, ALU.not_equal))
            then(nc.vector.tensor_tensor(inv[:, :], inv[:, :], deg[:, :], ALU.mult))
            join(acc, s1)
            then(nc.vector.tensor_tensor(s1[:, :, :], s1[:, :, :], inv[:, :].unsqueeze(2).to_broadcast([P, T, D]),
                                         ALU.mult))
            then(nc.vector.tensor_tensor(X[:, :, :], X[:, :, :], s1[:, :, :], ALU.add))

            layernorm(2, h1)

            def narrow(half, tiles):
                for kt in tiles:
                    nc.vector.tensor_copy(ATr[:, kt, :], AT[:, kt, HALF * half:HALF * half + HALF]).then_inc(atr_ready, 1)

            dve.wait_ge(proj_ready, 4 + T)
            split(ys[:, :, 2 * D:3 * D], pcs, s1)
            narrow(0, range(T))
            dve.wait_ge(mm_copied, 2 * T + 2)
            join(acc, s1)
            then(nc.vector.scalar_tensor_tensor(s1[:, :, :], s1[:, :, :], 2.0, ys[:, :, D:2 * D], ALU.mult, ALU.add))
            split(s1[:, :, :], pcs, h1)
            dve.wait_ge(mm_copied, 3 * T + 2)
            join(acc, s1)
            then(nc.vector.tensor_tensor(s1[:, :, :], s1[:, :, :], ys[:, :, 0:D], ALU.add))
            then(nc.vector.tensor_tensor(X[:, :, :], X[:, :, :], s1[:, :, :], ALU.add))

            layernorm(3, h3)
            dve.wait_ge(proj_ready, 8 + T)
            for k, col in enumerate((c3, r3)):
                then(nc.vector.tensor_tensor(pr3[:, :, :], XW[:, :, :],
                                             a3B[:, k:k + 1, :].to_broadcast([P, T, D]), ALU.mult))
                last = nc.vector.tensor_reduce(col[:, :], pr3[:, :, :], AX_X, ALU.add)
                then(last)
            nc.vector.tensor_scalar(c3s[:, :], c3[:, :], 0.01, None, ALU.mult).then_inc(logits_ready, 1)

            def leaky_step(s, jt, b):
                for q in range(2):
                    dve.wait_ge(z_ready, 2 * s + q + 1)
                    nc.vector.scalar_tensor_tensor(zb[q][:, :, :], zb[q][:, :, :], 0.01, zb[q][:, :, :], ALU.mult,
                                                   ALU.max).then_inc(leaky_ready, 1)

            def rec_step(s, jt, b, half):
                dve.wait_ge(att_free, s + 2)
                for c in range(2):
                    dve.wait_ge(num_bank, 2 * s + c + 5)
                    nc.vector.tensor_scalar(mx[c][:, :], bank[2 * b + c][:, :], TINY, None, ALU.max).then_inc(rec_seq, 1)
                    dve.wait_ge(dT_ready, 2 * s + c + 1)
                    nc.vector.tensor_tensor(dT[c][:, :], dT[c][:, :], dv[c][:, :], ALU.max).then_inc(dmax, 1)
                    dve.wait_ge(dmax, 2 * s + c + 1)
                    nc.vector.scalar_tensor_tensor(dT[c][:, :], bank[2 * b + c][:, :], 0.0, dT[c][:, :],
                                                   ALU.not_equal, ALU.mult).then_inc(num_free, 1)
                    dve.wait_ge(rec_seq, 2 * s + c + 1)
                    dve.wait_ge(num_free, 2 * s + c + 5)
                    nc.vector.reciprocal(mx[c][:, :], mx[c][:, :]).then_inc(rec_ready, 1)

            def second_half():
                dve.wait_ge(num_bank, 2 * T + 4)
                narrow(1, range(T))

            steps(dve, leaky_step, rec_step, second_half)
            dve.wait_ge(un_ready, 4)
            then(nc.vector.memset(pcs3[:, :, 3 * D:PW], 1.0))
            split(Un[:, :, :], pcs3, s3[0])
            dve.wait_ge(mm_copied, 4 * T + 2)
            join(acc3, s3[1])
            nc.vector.tensor_tensor(X[:, :, :], X[:, :, :], s3[1][:, :, :], ALU.add).then_inc(x_final, 1)


_INS = ["x", "adj", "L0_gnn_weight", "L0_gnn_att_weight", "L2_gnn_W", "L3_gnn_W", "L3_gnn_a"]


def kernel(**inputs):
    import numpy as np
    import concourse.bacc as bacc
    from concourse import mybir as mb
    from concourse.bass_utils import run_bass_kernel_spmd

    nc = bacc.Bacc("TRN2", target_bir_lowering=False, num_devices=1, dynamic_dma_scratch_size=1024)
    arrays, args = {}, []
    for name in _INS:
        a = np.ascontiguousarray(inputs[name])
        arrays[f"in_{name}"] = a
        args.append(nc.dram_tensor(f"in_{name}", a.shape, mb.dt.from_np(a.dtype), kind="ExternalInput").ap())
    args.append(nc.dram_tensor("out_0", (N, D), mb.dt.float32, kind="ExternalOutput").ap())
    gnn_stack(nc, *args)
    r = run_bass_kernel_spmd(nc, [arrays], core_ids=[0])
    return r.results[0]["out_0"]
```

```python
import concourse.bass as bass
from concourse import mybir
from contextlib import ExitStack

F32 = mybir.dt.float32
F32R = mybir.dt.float32r
I32 = mybir.dt.int32
BF16 = mybir.dt.bfloat16
ALU = mybir.AluOpType
ACT = mybir.ActivationFunctionType
AX_X = mybir.AxisListType.X

P = 128
N = 2048
T = N // P
D = 128
H = 4
F = D // H
F1 = F + 1
HALF = N // 2
HT = T // 2
BANK = 512
PW = 3 * D + 2
PC = 3 * D + 1
WC = H * F1 + H
CHUNKS = ((0, 5), (5, 10), (10, 16))
NC = len(CHUNKS)
EPS = 1e-5
TINY = 1.2e-38
KB = 1024
LOW = 1.25


def gnn_stack(nc, x, adj, w0, att0, w2, w3, a3, out):
    ctx = ExitStack()
    with ctx:
        def at(name, kb, shape, dt=F32):
            return nc.alloc_sbuf_tensor_at(name, shape, dt, offset=int((kb + LOW) * KB))

        def sem(name):
            return ctx.enter_context(nc.semaphore(name))

        A = at("A", 0, [P, T, N], BF16)
        ATr = at("ATr", 0, [P, T, HALF], F32R)
        AT = at("AT", 64, [P, T, N], BF16)
        X = at("X", 128, [P, T, D])
        WX = at("WX", 136, [P, T, WC])
        WH = WX[:, :, 0:H * F1].rearrange("p t (h f) -> p t h f", f=F1)
        B = 144.5
        a32 = [at(f"a32_{b}", B + 8 * b, [P, N]) for b in range(2)]
        cB = [at(f"cB_{h}", B + 16 + 8 * h, [P, N]) for h in range(H)]
        junk = at("junk", B + 48, [P, N], BF16)
        attB = at("attB", B + 48, [P, H, 2 * F])
        W0 = at("W0", B + 49, [P, D])
        h0 = at("h0", B + 52, [P, T, D])
        hT0 = at("hT0", B + 60, [P, N])
        ext = at("ext", B + 50, [P, 2 * H])
        exm = at("exm", B + 50.125, [2 * H, 1])
        exd = at("exd", B + 50.25, [2 * H, 2 * H])
        whc = [at(f"whc_{e}", B + 2.25 * e, [P, T, F1]) for e in range(2)]
        oT = [at(f"oT_{e}", B + 5 + 4 * e, [F1, HALF]) for e in range(2)]
        pmB = at("pmB", B + 13, [P, N])
        p2B = at("p2B", B + 21, [P, N])
        ub = [at(f"ub_{b}", B + 29 + 4 * b, [P, HALF]) for b in range(2)]
        vb = [at(f"vb_{b}", B + 37 + 4 * b, [P, HALF]) for b in range(2)]
        pb = [at(f"pb_{b}", B + 45 + 4 * b, [P, HALF]) for b in range(2)]
        diag = [at(f"diag_{b}", B + 53 + 2 * b, [P, BANK]) for b in range(2)]
        O = at("O", B + 57, [P, T, H, F1])
        pmcol, p2col, c2col = (at(name, B + 65.5 + 0.25 * k, [P, H, T]) for k, name in enumerate(("pmcol", "p2col", "c2col")))
        Oc = at("Oc", 136, [P, T, H, F1])
        slots = at("slots", B + 48, [P, T, T])
        G = [at(f"G_{b}", B + 4 * b, [P, T, P], BF16) for b in range(2)]
        zc = [at(f"zc_{b}", B + 8 + 6 * b, [P, NC, H, P]) for b in range(4)]
        wc = [at(f"wc_{b}", B + 32 + 1.75 * b, [P, NC, WC]) for b in range(4)]
        ATc = [at(f"ATc_{b}", B + 39 + 0.75 * b, [P, NC, P], BF16) for b in range(2)]
        mB = [at(f"mB_{b}", [B + 42, B + 52][b], [P, H * P]) for b in range(2)]
        rows = [at(f"rows_{b}", B + 44 + 4 * b, [P, 2, H, P]) for b in range(2)]
        rest0 = at("rest0", B + 52, [P, 4, WC])
        tri = at("tri", B + 54.25, [P, P], BF16)
        some = at("some", B + 54.75, [P, T, T], BF16)
        whp = at("whp", B + 55.25, [P, T, 3, WC], BF16)
        Os = at("Os", B + 29, [P, T, H, F1])
        acc = at("acc", B + 15, [P, T, PC])
        pcs = at("pcs", B + 39.5, [P, T, PW], BF16)
        h1 = at("h1", B + 52, [P, T, D])
        s1 = at("s1", B + 60, [P, T, D])
        hT2 = at("hT2", B + 60, [P, N])
        ys = at("ys", 136, [P, T, 3 * D])
        den_hi = [at(f"den_hi_{b}", 136 + 8 * b, [P, T, P], F32R) for b in range(2)]
        den_lo = [at(f"den_lo_{b}", 152 + 8 * b, [P, T, P], F32R) for b in range(2)]
        h3 = at("h3", 152, [P, T, D])
        hT3 = at("hT3", 160, [P, N])
        pr3 = at("pr3", 136, [P, T, D])
        zb = [at(f"zb_{b}", 168 + 4 * b, [P, HT, P]) for b in range(2)]
        dv = [at(f"dv_{b}", 176 + 2 * b, [P, BANK]) for b in range(2)]
        diag3 = [at(f"diag3_{b}", 168 + 2 * b, [P, BANK]) for b in range(2)]
        cB3 = at("cB3", 180, [P, N])
        rB3 = at("rB3", 188, [P, N])
        dT = [at(f"dT_{b}", 196 + 2 * b, [P, BANK]) for b in range(2)]
        mx = [at(f"mx_{b}", 200 + 2 * b, [P, BANK]) for b in range(2)]
        XW = at("XW", 204, [P, T, D])
        uT = at("uT", 136, [P, N])
        Un = at("Un", 144, [P, T, D])
        acc3 = at("acc3", 152, [P, T, PC])
        pcs3 = at("pcs3", 176.5, [P, T, PW], BF16)
        s3 = [at("s3_0", 189, [P, T, D]), at("s3_1", 197, [P, T, D])]

        denc = [at(f"denc_{b}", 24 * b, [P, NC, N]) for b in range(2)]
        dTc = [at(f"dTc_{b}", 48 + 8 * b, [P, T, P]) for b in range(2)]
        G3 = [at(f"G3_{b}", 136 + 4 * b, [P, T, P], BF16) for b in range(2)]
        yc = [[at(f"yc_{b}{c}", 152 + 8 * b + 2 * c, [P, BANK]) for c in range(4)] for b in range(2)]
        E01 = at("E01", 168, [P, N])
        Eb = at("Eb", 176, [P, T, P], BF16)
        ATc3 = [at(f"ATc3_{b}", 196 + 1.5 * b, [P, NC, P]) for b in range(2)]
        tc = [at(f"tc_{b}", 199 + 2 * b, [P, BANK]) for b in range(2)]

        top = [(LOW + 212.5) * KB]

        def const(name, shape, dt=F32):
            size = 1
            for n in shape[1:]:
                size *= n
            size = -(-size * (2 if dt == BF16 else 4) // 32) * 32
            t = nc.alloc_sbuf_tensor_at(name, shape, dt, offset=int(top[0]))
            top[0] += size
            return t

        ident = const("ident", [P, P])
        identb = const("identb", [P, P], BF16)
        ones = const("ones", [P, P])
        zeros = const("zeros", [P, P], BF16)
        onesb = const("onesb", [P, P], BF16)
        slotb = const("slotb", [P, T, T], BF16)
        iota = const("iota", [P, P], BF16)
        rp = const("rp", [P, T, 3], BF16)
        rc = [const(f"rc_{b}", [P, NC]) for b in range(2)]
        er = [const(f"er_{b}", [P, NC]) for b in range(2)]
        mk = const("mk", [P, T])
        over3 = const("over3", [P, 1])
        dense3 = const("dense3", [P, 1], I32)
        over = const("over", [P, 1])
        dense = const("dense", [P, 1], I32)
        W3 = const("W3", [P, D])
        a3B = const("a3B", [P, 2, D])
        W2 = const("W2", [P, 3, D])
        stats = const("stats", [P, T, 6])
        mv = const("mv", [P, T, 2])
        var = const("var", [P, T])
        power = const("power", [P, T])
        rstd = const("rstd", [P, T])
        pcol = const("pcol", [P, T, H])
        ccol = const("ccol", [P, T, H])
        mcol = const("mcol", [P, T, H])
        tcol = const("tcol", [P, T, H])
        cmin = const("cmin", [P, H])
        ctop = const("ctop", [P, H])
        spread = const("spread", [P, H + 1])
        c1col = const("c1col", [P, H, T])
        cc = [const(f"cc_{e}", [P, T]) for e in range(2)]
        cc2 = [const(f"cc2_{e}", [P, T]) for e in range(2)]
        wsum = const("wsum", [P, H, F1])
        cmax = nc.alloc_sbuf_tensor_at("cmax", [P, T, H], F32, offset=int(top[0]))
        xwc = [const(f"xwc_{b}", [P, D]) for b in range(2)]
        c3 = const("c3", [P, T])
        c3s = const("c3s", [P, T])
        r3 = const("r3", [P, T])
        inv = const("inv", [P, T])
        deg = const("deg", [P, T])

        bank = [ctx.enter_context(nc.psum_tensor(f"bank{i}", [P, BANK], F32)) for i in range(8)]
        bankb = [b[:, :].bitcast(BF16) for b in bank]

        x_loaded = sem("x_loaded")
        w_loaded = sem("w_loaded")
        a_loaded = [sem(f"a_loaded{b}") for b in range(2)]
        a_ready = sem("a_ready")
        const_ready = sem("const_ready")
        vec = sem("vec")
        h_ready = sem("h_ready")
        var_ready = sem("var_ready")
        rstd_ready = sem("rstd_ready")
        hT_banks = sem("hT_banks")
        hT_ready = sem("hT_ready")
        w2T_banks = sem("w2T_banks")
        w2_ready = sem("w2_ready")
        proj_banks = sem("proj_banks")
        proj_ready = sem("proj_ready")
        wsum_bank = sem("wsum_bank")
        wsum_ready = sem("wsum_ready")
        logits_ready = sem("logits_ready")
        diag_ready = sem("diag_ready")
        bc_bank = sem("bc_bank")
        bc_copied = sem("bc_copied")
        at_bank = sem("at_bank")
        at_copied = sem("at_copied")
        pieces0_ready = sem("pieces0_ready")
        edge_bank = sem("edge_bank")
        some_ready = sem("some_ready")
        rank_bank = sem("rank_bank")
        iota_ready = sem("iota_ready")
        over_ready = sem("over_ready")
        over_bank = sem("over_bank")
        choice = sem("choice")
        g_ready = sem("g_ready")
        gathered = sem("gathered")
        w_copied = sem("w_copied")
        e_copied = sem("e_copied")
        rows_ready = sem("rows_ready")
        rows_bank = sem("rows_bank")
        m_copied = sem("m_copied")
        zc_ready = sem("zc_ready")
        zc_leaky = sem("zc_leaky")
        zc_less = sem("zc_less")
        zc_exp = sem("zc_exp")
        pc_ready = sem("pc_ready")
        pc_used = sem("pc_used")
        oc_copied = sem("oc_copied")
        e01_ready = sem("e01_ready")
        rp_ready = sem("rp_ready")
        g3_ready = sem("g3_ready")
        g3_used = sem("g3_used")
        rc_seq = sem("rc_seq")
        e3_copied = sem("e3_copied")
        er_ready = sem("er_ready")
        u3_ready = sem("u3_ready")
        denc_ready = sem("denc_ready")
        num3_bank = sem("num3_bank")
        ln_ready = sem("ln_ready")
        y_ready = sem("y_ready")
        t_ready = sem("t_ready")
        s_ready = sem("s_ready")
        z3_ready = sem("z3_ready")
        z3_leaky = sem("z3_leaky")
        dT3_ready = sem("dT3_ready")
        att3_ready = sem("att3_ready")
        att3_used = sem("att3_used")
        un3_kept = sem("un3_kept")
        ext_ready = sem("ext_ready")
        ext_bank = sem("ext_bank")
        guard_ready = sem("guard_ready")
        cur_ready = sem("cur_ready")
        uv_ready = sem("uv_ready")
        uv_free = sem("uv_free")
        p_ready = sem("p_ready")
        p_free = sem("p_free")
        oT_ready = sem("oT_ready")
        o_turned = sem("o_turned")
        o_kept = sem("o_kept")
        pieces_ready = sem("pieces_ready")
        mm_bank = sem("mm_bank")
        mm_copied = sem("mm_copied")
        atr_ready = sem("atr_ready")
        half_done = sem("half_done")
        xw_cur = sem("xw_cur")
        z_ready = sem("z_ready")
        den_ready = sem("den_ready")
        lo_ready = sem("lo_ready")
        num_bank = sem("num_bank")
        num_free = sem("num_free")
        dT_ready = sem("dT_ready")
        rec_ready = sem("rec_ready")
        att_ready = sem("att_ready")
        att_free = sem("att_free")
        u_bank = sem("u_bank")
        uT_ready = sem("uT_ready")
        u_turned = sem("u_turned")
        un_ready = sem("un_ready")
        pmax = sem("pmax")
        rec_seq = sem("rec_seq")
        act_seq = sem("act_seq")
        leaky_ready = sem("leaky_ready")
        dmax = sem("dmax")
        x_final = sem("x_final")
        passed = sem("passed")
        stored = sem("stored")

        CREDIT = {uv_free: 2, p_free: 2, oT_ready: 4, o_turned: 2, o_kept: 2, at_copied: 4, mm_copied: 2,
                  some_ready: 2, gathered: 2, w_copied: 2, e_copied: 2, rows_bank: 4, zc_less: 2, pc_ready: 4,
                  g3_used: 2, e3_copied: 2, num3_bank: 8, t_ready: 4, att3_ready: 8, att3_used: 8, un3_kept: 2,
                  pc_used: 4, zc_ready: 2, num_bank: 4, num_free: 4, att_ready: 2, att_free: 2}

        def apart(engine):
            engine.sem_inc(passed, 1)

        def choose(engine, layer, by_slots, over_all):
            first = layer == 0
            engine.wait_ge(choice, 2 if first else 3)
            flag = engine.alloc_register(f"dense_{layer}_" + str(engine.engine).split(".")[-1])
            engine.reg_load(flag, (dense if first else dense3)[0:1, 0:1])
            with engine.If_ne(flag, 0):
                over_all()
            with engine.Else():
                by_slots()

        def sweep(engine, tile_step):
            for it in range(2):
                tile_step(it, it)
            with engine.Fori(1, HT - 1) as g:
                for b in range(2):
                    tile_step(2 * g + b, b)
            for it in range(T - 2, T):
                tile_step(it, it % 2)

        def within(it, ahead):
            return not isinstance(it, int) or 0 <= it + ahead < T

        def rounds(engine, lead, follow):
            lead(0, 0)
            for it in range(2):
                lead(it + 1, it + 1)
                follow(it, it)
            with engine.Fori(0, T // 4 - 1) as g:
                for k in range(2, 6):
                    lead(4 * g + k + 1, (k + 1) % 4)
                    follow(4 * g + k, k % 4)
            lead(T - 1, 3)
            follow(T - 2, 2)
            follow(T - 1, 3)

        def steps(engine, lead, follow, turn=None):
            lead(0, 0, 0)
            for half in range(2):
                s0 = T * half
                with engine.Fori(0, HT - 1) as g:
                    for b in range(2):
                        lead(s0 + 2 * g + b + 1, 2 * g + b + 1, (b + 1) % 2)
                        follow(s0 + 2 * g + b, 2 * g + b, b, half)
                lead(s0 + T - 1, T - 1, 1)
                follow(s0 + T - 2, T - 2, 0, half)
                if half == 0:
                    if turn is not None:
                        turn()
                    lead(T, 0, 0)
                follow(s0 + T - 1, T - 1, 1, half)

        block = ctx.enter_context(nc.Block())

        @block.sync
        def _(sp):
            sp.dma_start(X[:, :, :], x.rearrange("(t p) f -> p t f", p=P)).then_inc(x_loaded, 16)

            def load(it, b):
                sp.dma_start(a32[b][:, :], adj[bass.ds(it * P, P), :]).then_inc(a_loaded[b], 16)

            load(0, 0)
            load(1, 1)
            with sp.Fori(1, HT) as g:
                for b in range(2):
                    sp.wait_ge(a_ready, 2 * g + b - 1)
                    load(2 * g + b, b)
            sp.wait_ge(x_final, 1)
            sp.dma_start(out.rearrange("(t p) f -> p t f", p=P), X[:, :, :]).then_inc(stored, 16)
            sp.wait_ge(stored, 16)

        @block.gpsimd
        def _(pool):
            for free, count in CREDIT.items():
                pool.sem_inc(free, count)
            nc.gpsimd.memset(ones[:, :], 1.0).then_inc(const_ready, 1)
            nc.gpsimd.memset(zeros[:, :], 0.0).then_inc(const_ready, 1)
            nc.gpsimd.memset(power[:, :], -0.5).then_inc(const_ready, 1)
            nc.gpsimd.memset(WH[:, :, :, F:F1], 1.0).then_inc(const_ready, 1)
            nc.gpsimd.memset(onesb[:, :], 1.0).then_inc(const_ready, 1)
            pool.wait_ge(const_ready, 5)
            nc.gpsimd.affine_select(out=ident[:, :], in_=ones[:, :], compare_op=ALU.is_equal, fill=0.0, base=0,
                                    pattern=[[-1, P]], channel_multiplier=1).then_inc(const_ready, 1)
            pool.wait_ge(const_ready, 6)
            nc.gpsimd.tensor_copy(identb[:, :], ident[:, :]).then_inc(const_ready, 1)

            def rstd_of(layer):
                pool.wait_ge(var_ready, layer + 1)
                nc.gpsimd.tensor_tensor(rstd[:, :], var[:, :], power[:, :], ALU.pow).then_inc(rstd_ready, 1)

            def diagonal(dst, col, n):
                if not isinstance(n, int) or n >= 2:
                    pool.wait_ge(bc_bank, n - 1)
                if not isinstance(n, int):
                    apart(pool)
                nc.gpsimd.tensor_tensor(dst[:, :].rearrange("p (t q) -> p t q", q=P),
                                        ident[:, :].unsqueeze(1).to_broadcast([P, 4, P]),
                                        col.unsqueeze(2).to_broadcast([P, 4, P]), ALU.mult).then_inc(diag_ready, 1)

            rstd_of(0)
            pool.wait_ge(logits_ready, 1)
            nc.gpsimd.affine_select(out=tri[:, :], in_=onesb[:, :], compare_op=ALU.is_ge, fill=0.0, base=0,
                                    pattern=[[1, P]], channel_multiplier=-1).then_inc(pieces0_ready, 1)
            count = 1
            for q in range(4):
                ts = slice(4 * q, 4 * q + 4)
                for k, (dst, x0, x1) in enumerate((
                        (whp[:, ts, 0, :], WX[:, ts, :], None),
                        (rest0[:, :, :], WX[:, ts, :], whp[:, ts, 0, :]),
                        (whp[:, ts, 1, :], rest0[:, :, :], None),
                        (whp[:, ts, 2, :], rest0[:, :, :], whp[:, ts, 1, :]))):
                    if x1 is None:
                        step = nc.gpsimd.tensor_copy(dst, x0)
                    else:
                        step = nc.gpsimd.tensor_tensor(dst, x0, x1, ALU.subtract)
                    step.then_inc(pieces0_ready, 1)
                    count += 1
                    pool.wait_ge(pieces0_ready, count)

            def over_all():
                for n in range(16):
                    diagonal(diag[n % 2], c1col[:, n // 4, 4 * (n % 4):4 * (n % 4) + 4], n)
                pool.wait_ge(guard_ready, 5)
                pool.wait_ge(bc_copied, 16)
                with pool.Fori(0, 2) as g:
                    for e in range(2):
                        h = 2 * g + e
                        pool.wait_ge(oT_ready, 4 * g + 2 * e + 2)
                        nc.gpsimd.tensor_copy(whc[e][:, :, :], WH[:, :, bass.ds(h, 1), :].rearrange("p t o f -> p t (o f)")).then_inc(cur_ready, 1)
                        nc.gpsimd.tensor_copy(cc[e][:, :], c1col[:, bass.ds(h, 1), :].rearrange("p o t -> p (o t)")).then_inc(cur_ready, 1)
                        nc.gpsimd.tensor_copy(cc2[e][:, :], c2col[:, bass.ds(h, 1), :].rearrange("p o t -> p (o t)")).then_inc(cur_ready, 1)
                        for half in range(2):
                            for k in range(4):
                                col = (pmcol, p2col)[k // 2]
                                t0 = HT * half + 4 * (k % 2)
                                diagonal(diag[k % 2], col[:, bass.ds(h, 1), t0:t0 + 4].rearrange("p o t -> p (o t)"),
                                         16 + 16 * g + 8 * e + 4 * half + k)
                pool.wait_ge(bc_bank, 48)

            def row_diagonals(it, b):
                for k, col in enumerate((pcol, mcol)):
                    pool.wait_ge(rows_bank, 2 * it + k + 1)
                    if not isinstance(it, int):
                        apart(pool)
                    nc.gpsimd.tensor_tensor(rows[b % 2][:, k, :, :],
                                            ident[:, :].unsqueeze(1).to_broadcast([P, H, P]),
                                            col[:, bass.ds(it, 1), :].rearrange("p o h -> p (o h)").unsqueeze(2)
                                            .to_broadcast([P, H, P]), ALU.mult).then_inc(rows_ready, 1)

            def next_diagonals(it, b):
                if not isinstance(it, int) or it < T - 1:
                    row_diagonals(it + 1, (b + 1) % 4)

            def less_m(it, b):
                pool.wait_ge(m_copied, it + 1)
                pool.wait_ge(zc_leaky, it + 1)
                z = zc[b][:, :, :, :].rearrange("p c h i -> p c (h i)")
                nc.gpsimd.tensor_tensor(z, z, mB[b % 2][:, :].unsqueeze(1).to_broadcast([P, NC, H * P]),
                                        ALU.subtract).then_inc(zc_less, 1)

            def by_slots():
                row_diagonals(0, 0)
                rounds(pool, next_diagonals, less_m)
                pool.sem_inc(diag_ready, 48)

            choose(pool, 0, by_slots, over_all)
            rstd_of(1)
            rstd_of(2)
            rstd_of(3)
            pool.wait_ge(logits_ready, 2)
            n0 = 48
            for k in range(8):
                diagonal(diag3[k % 2], (c3, r3)[k // 4][:, 4 * (k % 4):4 * (k % 4) + 4], n0 + k)
            pool.wait_ge(bc_bank, n0 + 8)
            pool.wait_ge(bc_copied, n0 + 8)

            def over_all3():
                def z_step(jt, s=None):
                    for q in range(2):
                        if s is not None:
                            pool.wait_ge(lo_ready, 2 * s + q + 1)
                            if not isinstance(s, int):
                                apart(pool)
                        nc.gpsimd.tensor_tensor(zb[q][:, :, :],
                                                cB3[:, bass.ds(jt * P, P)].unsqueeze(1).to_broadcast([P, HT, P]),
                                                r3[:, HT * q:HT * q + HT].unsqueeze(2).to_broadcast([P, HT, P]),
                                                ALU.add).then_inc(z_ready, 1)

                def lo_step(s, jt, b):
                    for q in range(2):
                        pool.wait_ge(den_ready, 2 * s + q + 1)
                        qs = slice(HT * q, HT * q + HT)
                        nc.gpsimd.tensor_tensor(den_lo[b][:, qs, :], zb[q][:, :, :], den_hi[b][:, qs, :].bitcast(F32),
                                                ALU.subtract).then_inc(lo_ready, 1)
                    if isinstance(jt, int) and jt == T - 1:
                        if s == T - 1:
                            z_step(0, s)
                    else:
                        z_step(jt + 1, s)

                def att_step(s, jt, b, half):
                    for c in range(2):
                        pool.wait_ge(rec_ready, 2 * s + c + 1)
                        nc.gpsimd.tensor_tensor(mx[c][:, :], dT[c][:, :], mx[c][:, :], ALU.mult).then_inc(att_ready, 1)

                z_step(0)
                steps(pool, lo_step, att_step)

            def z3(it, b):
                pool.wait_ge(att3_ready, 4 * it + 4)
                if not isinstance(it, int):
                    apart(pool)
                nc.gpsimd.tensor_tensor(dTc[b][:, :, :], rB3[:, bass.ds(it * P, P)].unsqueeze(1).to_broadcast([P, T, P]),
                                        c3[:, :].unsqueeze(2).to_broadcast([P, T, P]), ALU.add).then_inc(z3_ready, 1)

            def att3(it, b, c):
                pool.wait_ge(dT3_ready, it + 1)
                pool.wait_ge(s_ready, 4 * it + c + 1)
                nc.gpsimd.tensor_tensor(yc[b][c][:, :], yc[b][c][:, :],
                                        dTc[b][:, 4 * c:4 * c + 4, :].rearrange("p j i -> p (j i)"),
                                        ALU.mult).then_inc(att3_ready, 1)

            def tile3(it, b):
                if within(it, 1):
                    z3(it + 1, 1 - b)
                att3(it, b, 0)
                att3(it, b, 1)
                att3(it, b, 2)
                att3(it, b, 3)

            def by_slots3():
                z3(0, 0)
                sweep(pool, tile3)

            choose(pool, 3, by_slots3, over_all3)

        @block.scalar
        def _(act):
            act.dma_start(W0[:, :], w0).then_inc(w_loaded, 16)
            act.dma_start(attB[:, :, :].rearrange("p h f -> p (h f)"),
                          att0.rearrange("h f -> (h f)").partition_broadcast(P)).then_inc(w_loaded, 16)
            act.dma_start(W2[:, :, :], w2.rearrange("k o c -> o k c")).then_inc(w_loaded, 16)
            act.dma_start(W3[:, :], w3).then_inc(w_loaded, 16)
            act.dma_start(a3B[:, :, :].rearrange("p k f -> p (k f)"),
                          a3.rearrange("o f -> (o f)").partition_broadcast(P)).then_inc(w_loaded, 16)

            def turn_h(dst, use):
                for q in range(4):
                    act.wait_ge(hT_banks, 4 * use + q + 1)
                    nc.scalar.copy(dst[:, q * BANK:(q + 1) * BANK], bank[q][:, :]).then_inc(hT_ready, 1)

            def convert(g, b):
                act.wait_ge(a_loaded[b], 16 * g + 16)
                nc.scalar.copy(A[:, bass.ds(2 * g + b, 1), :].rearrange("p o n -> p (o n)"), a32[b][:, :]).then_inc(a_ready, 1)

            for it in range(4):
                convert(it // 2, it % 2)
            turn_h(hT0, 0)
            with act.Fori(2, HT) as g:
                for b in range(2):
                    convert(g, b)

            def over_all():
                for n in range(16):
                    act.wait_ge(bc_bank, n + 1)
                    nc.scalar.copy(cB[n // 4][:, (n % 4) * BANK:(n % 4 + 1) * BANK], bank[4 + n % 2][:, :]).then_inc(bc_copied, 1)
                with act.Fori(0, 2) as g:
                    for e in range(2):
                        for half in range(2):
                            u = 4 * g + 2 * e + half
                            for k in range(4):
                                n = 16 + 4 * u + k
                                lo = HALF * half + BANK * (k % 2)
                                act.wait_ge(bc_bank, n + 1)
                                nc.scalar.copy((pmB, p2B)[k // 2][:, lo:lo + BANK], bank[4 + k % 2][:, :]).then_inc(bc_copied, 1)
                            act.wait_ge(bc_copied, 16 + 4 * u + 4)
                            act.wait_ge(cur_ready, 6 * g + 3 * e + 3)
                            hs = slice(HALF * half, HALF * half + HALF)
                            for jt in range(T):
                                act.wait_ge(uv_free, T * u + jt + 1)
                                nc.scalar.activation(ub[jt % 2][:, :], pmB[:, hs], ACT.Exp, bias=cc[e][:, jt:jt + 1]).then_inc(uv_ready, 1)
                                nc.scalar.activation(vb[jt % 2][:, :], p2B[:, hs], ACT.Exp, bias=cc2[e][:, jt:jt + 1]).then_inc(uv_ready, 1)
                            act.wait_ge(p_free, T * u + T + 2)
                            act.wait_ge(o_turned, u + 1)
                            nc.scalar.copy(oT[half][:, 0:BANK], bank[2 * half][0:F1, :])
                            nc.scalar.copy(oT[half][:, BANK:HALF], bank[2 * half + 1][0:F1, :]).then_inc(oT_ready, 1)

            def slot_logits(it, b):
                act.wait_ge(gathered, it + 3)
                act.wait_ge(pc_used, it + 1)
                nc.scalar.copy(wc[b][:, :, :].rearrange("p c w -> p (c w)"), bank[b % 2][:, 0:NC * WC]).then_inc(w_copied, 1)
                act.wait_ge(rows_bank, 2 * it + 6)
                act.wait_ge(zc_less, it + 1)
                nc.scalar.copy(mB[b % 2][:, :], bank[5][:, :]).then_inc(m_copied, 1)
                act.wait_ge(w_copied, it + 3)
                for c in range(NC):
                    for h in range(H):
                        last = nc.scalar.activation(zc[b][:, c, h, :], bank[4 + 2 * (b % 2)][:, P * h:P * h + P], ACT.Identity,
                                                    bias=wc[b][:, c, H * F1 + h:H * F1 + h + 1])
                last.then_inc(zc_ready, 1)

            def copy_output(it):
                act.wait_ge(pc_used, it + 5)
                if not isinstance(it, int):
                    apart(act)
                nc.scalar.copy(Oc[:, bass.ds(it, 1), :, :].rearrange("p o h f -> p (o h f)"),
                               bank[7][:, 0:H * F1]).then_inc(oc_copied, 1)

            def slot_exp(it, b):
                act.wait_ge(zc_less, it + 3)
                z = zc[b][:, :, :, :].rearrange("p c h i -> p (c h i)")
                nc.scalar.activation(z, z, ACT.Exp).then_inc(zc_exp, 1)
                if not isinstance(it, int) or it > 0:
                    copy_output(it - 1)

            def by_slots():
                rounds(act, slot_logits, slot_exp)
                copy_output(T - 1)
                act.sem_inc(bc_copied, 48)

            choose(act, 0, by_slots, over_all)

            def products(dst, base):
                with act.Fori(0, HT) as g:
                    for b in range(2):
                        act.wait_ge(mm_bank, base + 2 * g + b + 1)
                        nc.scalar.copy(dst[:, bass.ds(2 * g + b, 1), :].rearrange("p o n -> p (o n)"),
                                       bank[b][:, 0:PC]).then_inc(mm_copied, 1)

            products(acc, 0)
            turn_h(hT2, 1)
            for t in range(T):
                act.wait_ge(proj_banks, 4 + t + 1)
                nc.scalar.copy(ys[:, t, :], bank[4 + t % 4][:, 0:3 * D]).then_inc(proj_ready, 1)
            products(acc, T)
            products(acc, 2 * T)
            turn_h(hT3, 2)
            for q in range(4):
                act.wait_ge(proj_banks, 4 + T + q + 1)
                nc.scalar.copy(XW[:, 4 * q:4 * q + 4, :].rearrange("p t f -> p (t f)"), bank[4 + q][:, :]).then_inc(proj_ready, 1)
            for k in range(8):
                act.wait_ge(bc_bank, 48 + k + 1)
                nc.scalar.copy((cB3, rB3)[k // 4][:, (k % 4) * BANK:(k % 4 + 1) * BANK], bank[4 + k % 2][:, :]).then_inc(bc_copied, 1)
            act.wait_ge(bc_copied, 56)

            def over_all3():
                def den_step(s, jt, b):
                    act.wait_ge(num_bank, 2 * s + 2)
                    for q in range(2):
                        z = zb[q][:, :, :]
                        act.wait_ge(leaky_ready, 2 * s + q + 1)
                        nc.scalar.activation(z, z, ACT.Exp).then_inc(act_seq, 1)
                        act.wait_ge(act_seq, 2 * s + q + 1)
                        nc.scalar.copy(den_hi[b][:, HT * q:HT * q + HT, :], z).then_inc(den_ready, 1)

                def dT_step(s, jt, b, half):
                    for c in range(2):
                        act.wait_ge(att_ready, 2 * s + c + 1)
                        apart(act)
                        lo = HALF * half + BANK * c
                        nc.scalar.activation(dT[c][:, :], rB3[:, lo:lo + BANK], ACT.Exp, bias=c3[:, bass.ds(jt, 1)])
                        nc.scalar.activation(dv[c][:, :], rB3[:, lo:lo + BANK], ACT.Exp, bias=c3s[:, bass.ds(jt, 1)],
                                             scale=0.01).then_inc(dT_ready, 1)
                    act.wait_ge(att_free, s + 1)
                    nc.scalar.copy(xwc[b][:, :], XW[:, bass.ds(jt, 1), :].rearrange("p o f -> p (o f)")).then_inc(xw_cur, 1)

                steps(act, den_step, dT_step)
                for q in range(4):
                    act.wait_ge(u_bank, q + 1)
                    nc.scalar.copy(uT[:, q * BANK:(q + 1) * BANK], bank[4 + q][:, :]).then_inc(uT_ready, 1)
                for q in range(4):
                    act.wait_ge(u_turned, q + 1)
                    nc.scalar.copy(Un[:, 4 * q:4 * q + 4, :].rearrange("p t f -> p (t f)"), bank[q][:, :]).then_inc(un_ready, 1)

            def exp_er(it, b):
                act.wait_ge(e3_copied, it + 3)
                if within(it, -2):
                    act.wait_ge(denc_ready, 3 * it - 3)
                nc.scalar.activation(er[b][:, :], rc[b][:, :], ACT.Exp, scale=0.01).then_inc(er_ready, 1)

            def exp_u(it, b, c):
                act.wait_ge(e3_copied, it + 3)
                act.wait_ge(num3_bank, 4 * it + 4)
                nc.scalar.activation(denc[b][:, c, :], cB3[:, :], ACT.Exp, bias=rc[b][:, c:c + 1]).then_inc(u3_ready, 1)

            def exp_ln(it, b, c):
                n = 4 * it + c
                act.wait_ge(num3_bank, n + 9)
                act.wait_ge(att3_used, n + 1)
                nc.scalar.activation(yc[b][c][:, :], bank[c][:, :], ACT.Ln).then_inc(ln_ready, 1)
                act.wait_ge(ln_ready, n + 1)
                nc.scalar.activation(yc[b][c][:, :], yc[b][c][:, :], ACT.Exp, scale=-1.0).then_inc(y_ready, 1)

            def exp_dT(it, b):
                act.wait_ge(z3_leaky, it + 1)
                z = dTc[b][:, :, :].rearrange("p j i -> p (j i)")
                nc.scalar.activation(z, z, ACT.Exp).then_inc(dT3_ready, 1)

            def tile3(it, b):
                if within(it, 1):
                    exp_er(it + 1, 1 - b)
                for c in range(4):
                    if within(it, 1) and c < NC:
                        exp_u(it + 1, 1 - b, c)
                    exp_ln(it, b, c)
                if within(it, 1):
                    exp_dT(it + 1, 1 - b)

            def by_slots3():
                nc.scalar.preload_act_table_set("natural_log_exp_and_others")
                nc.scalar.activation(E01[:, :], cB3[:, :], ACT.Exp, scale=0.01).then_inc(e01_ready, 1)
                exp_er(0, 0)
                for c in range(NC):
                    exp_u(0, 0, c)
                exp_dT(0, 0)
                sweep(act, tile3)

            choose(act, 3, by_slots3, over_all3)
            products(acc3, 3 * T)

        @block.tensor
        def _(pe):
            def turn_h(src, layer, use):
                pe.wait_ge(h_ready, layer + 1)
                for t in range(T):
                    last = nc.tensor.transpose(bank[t // 4][:, P * (t % 4):P * (t % 4) + P], src[:, t, :], ident[:, :])
                    if t % 4 == 3:
                        last.then_inc(hT_banks, 1)

            def broadcast(dg, n, b):
                pe.wait_ge(diag_ready, n + 1)
                if not isinstance(n, int) or n >= 2:
                    pe.wait_ge(bc_copied, n - 1)
                nc.tensor.matmul(bank[4 + b][:, :], ones[:, :], dg[b][:, :], start=True, stop=True).then_inc(bc_bank, 1)

            pe.wait_ge(const_ready, 7)
            turn_h(h0, 0, 0)
            pe.wait_ge(w_loaded, 80)
            for k in range(3):
                last = nc.tensor.transpose(bank[6][:, P * k:P * k + P], W2[:, k, :], ident[:, :])
            last.then_inc(w2T_banks, 1)
            pe.wait_ge(w2_ready, 1)
            for t in range(T):
                pe.wait_ge(hT_ready, t // 4 + 1)
                last = nc.tensor.matmul(bank[4 + t // 4][:, P * (t % 4):P * (t % 4) + P], hT0[:, P * t:P * t + P],
                                        W0[:, :], start=True, stop=True)
                if t % 4 == 3:
                    last.then_inc(proj_banks, 1)
            pe.wait_ge(proj_ready, 4)
            for t in range(T):
                last = nc.tensor.matmul(bank[7][:, 0:H * F1], ones[:, :], WH[:, t, :, :].rearrange("p h f -> p (h f)"),
                                        start=t == 0, stop=t == T - 1)
            last.then_inc(wsum_bank, 1)
            pe.wait_ge(ext_ready, 1)
            nc.tensor.matmul(bank[5][0:2 * H, 0:P], ext[:, :], ident[:, :], start=True, stop=True).then_inc(ext_bank, 1)
            pe.wait_ge(ext_ready, 2)
            nc.tensor.matmul(bank[5][:, 0:2 * H], ones[0:2 * H, :], exd[:, :], start=True, stop=True).then_inc(ext_bank, 1)

            pe.wait_ge(hT_ready, 4)
            pe.wait_ge(wsum_ready, 1)
            with pe.Fori(0, HT) as g:
                for b in range(2):
                    it = 2 * g + b
                    pe.wait_ge(a_ready, it + 1)
                    for grp in range(2):
                        pe.wait_ge(at_copied, 2 * it + grp + 1)
                        for k in range(8):
                            jt = 8 * grp + k
                            last = nc.tensor.transpose(
                                bankb[2 * b + grp][:, P * k:P * k + P],
                                A[:, bass.ds(it, 1), P * jt:P * jt + P].rearrange("p o n -> p (o n)"), identb[:, :])
                        last.then_inc(at_bank, 1)
                    pe.wait_ge(some_ready, it + 1)
                    for jt in range(T):
                        last = nc.tensor.matmul(bank[6 + b][:, jt:jt + 1],
                                                A[:, bass.ds(it, 1), P * jt:P * jt + P].rearrange("p o n -> p (o n)"),
                                                onesb[:, 0:1], start=True, stop=True)
                    last.then_inc(edge_bank, 1)
            pe.wait_ge(pieces0_ready, 1)
            pe.wait_ge(guard_ready, 1)
            nc.tensor.matmul(bank[5][:, 0:P], onesb[:, :], tri[:, :], start=True, stop=True).then_inc(rank_bank, 1)
            pe.wait_ge(some_ready, T + 2)
            someF = some[:, :, :].rearrange("p i j -> p (i j)")
            ranks = bank[4][:, 0:T * T].rearrange("p (i j) -> p i j", j=T)
            nc.tensor.matmul(bank[4][:, 0:T * T], tri[:, :], someF, start=True, stop=False)
            for first, end in CHUNKS:
                for jt in range(first, end - 1):
                    nc.tensor.matmul(ranks[:, :, jt + 1:end], onesb[:, :],
                                     some[:, :, jt:jt + 1].to_broadcast([P, T, end - 1 - jt]), start=False, stop=False)
            nc.tensor.matmul(bank[4][:, 0:T * T], zeros[:, :], someF, start=False, stop=True).then_inc(rank_bank, 1)
            pe.wait_ge(over_ready, 1)
            nc.tensor.matmul(bank[5][:, 0:1], ones[:, :], over[:, :], start=True, stop=True).then_inc(over_bank, 1)

            pe.wait_ge(at_copied, 2 * T + 4)

            def over_all():
                for n in range(16):
                    broadcast(diag, n, n % 2)
                with pe.Fori(0, 2) as g:
                    for e in range(2):
                        for half in range(2):
                            u = 4 * g + 2 * e + half
                            for k in range(4):
                                broadcast(diag, 16 + 4 * u + k, k % 2)
                            pe.wait_ge(cur_ready, 6 * g + 3 * e + 3)
                            pe.wait_ge(oT_ready, u + 3)
                            for jt in range(T):
                                pe.wait_ge(p_ready, T * u + jt + 1)
                                for c in range(2):
                                    last = nc.tensor.matmul(bank[2 * half + c][0:F1, :], whc[e][:, jt, :],
                                                            pb[jt % 2][:, BANK * c:BANK * c + BANK],
                                                            start=jt == 0, stop=jt == T - 1)
                                last.then_inc(p_free, 1)
                            pe.wait_ge(oT_ready, u + 5)
                            pe.wait_ge(o_kept, u + 1)
                            for t in range(HT):
                                last = nc.tensor.matmul(bank[6 + half][:, F1 * t:F1 * t + F1], oT[half][:, P * t:P * t + P],
                                                        ident[0:F1, 0:F1], start=True, stop=True)
                            last.then_inc(o_turned, 1)

            def gather(it, b):
                pe.wait_ge(g_ready, it + 1)
                pe.wait_ge(w_copied, it + 1)
                pe.wait_ge(e_copied, it + 1)
                for c, (first, end) in enumerate(CHUNKS):
                    for jt in range(first, end):
                        for k in range(3):
                            nc.tensor.matmul(bank[b % 2][:, WC * c:WC * c + WC], G[b % 2][:, jt, :], whp[:, jt, k, :],
                                             start=jt == first and k == 0, stop=jt == end - 1 and k == 2)
                        last = nc.tensor.matmul(bank[2 + b % 2][:, P * c:P * c + P], G[b % 2][:, jt, :],
                                                AT[:, jt, bass.ds(it * P, P)], start=jt == first, stop=jt == end - 1)
                last.then_inc(gathered, 1)

            def broadcast_rows(it, b):
                for k, target in enumerate((bank[4 + 2 * (b % 2)], bank[5])):
                    pe.wait_ge(rows_ready, 2 * it + k + 1)
                    if k == 0:
                        pe.wait_ge(zc_ready, it + 1)
                    elif not isinstance(it, int) or it > 0:
                        pe.wait_ge(m_copied, it)
                    nc.tensor.matmul(target[:, :], ones[:, :], rows[b % 2][:, k, :, :].rearrange("p h i -> p (h i)"),
                                     start=True, stop=True).then_inc(rows_bank, 1)

            def prepare(it, b):
                if not isinstance(it, int) or it < T - 1:
                    broadcast_rows(it + 1, (b + 1) % 4)
                    gather(it + 1, (b + 1) % 4)

            def slot_output(it, b):
                pe.wait_ge(pc_ready, it + 5)
                pe.wait_ge(w_copied, it + 3)
                if not isinstance(it, int) or it > 0:
                    pe.wait_ge(oc_copied, it)
                for h in range(H):
                    for c in range(NC):
                        last = nc.tensor.matmul(bank[7][:, F1 * h:F1 * h + F1], zc[b][:, c, h, :],
                                                wc[b][:, c, F1 * h:F1 * h + F1], start=c == 0, stop=c == NC - 1)
                last.then_inc(pc_used, 1)

            def by_slots():
                pe.wait_ge(pieces0_ready, 17)
                broadcast_rows(0, 0)
                gather(0, 0)
                rounds(pe, prepare, slot_output)
                pe.sem_inc(bc_bank, 48)

            choose(pe, 0, by_slots, over_all)

            def product(adjacency, pieces, number):
                pe.wait_ge(pieces_ready, number + 1)
                base = T * number
                with pe.Fori(0, HT) as g:
                    for b in range(2):
                        i = 2 * g + b
                        pe.wait_ge(mm_copied, base + i + 1)
                        for kt in range(T):
                            last = nc.tensor.matmul(bank[b][:, 0:PC], adjacency[:, kt, bass.ds(i * P, P)],
                                                    pieces[:, kt, 0:PC], start=kt == 0, stop=kt == T - 1)
                        last.then_inc(mm_bank, 1)

            product(A, pcs, 0)
            pe.wait_ge(mm_copied, T + 2)
            turn_h(h1, 2, 1)
            for t in range(T):
                pe.wait_ge(hT_ready, 4 + t // 4 + 1)
                if t >= 4:
                    pe.wait_ge(proj_ready, 4 + t - 3)
                nc.tensor.matmul(bank[4 + t % 4][:, 0:3 * D], hT2[:, P * t:P * t + P],
                                 W2[:, :, :].rearrange("p k o -> p (k o)"), start=True, stop=True).then_inc(proj_banks, 1)
            product(AT, pcs, 1)
            product(AT, pcs, 2)
            pe.wait_ge(mm_copied, 3 * T + 2)
            turn_h(h3, 3, 2)
            for t in range(T):
                pe.wait_ge(hT_ready, 8 + t // 4 + 1)
                last = nc.tensor.matmul(bank[4 + t // 4][:, P * (t % 4):P * (t % 4) + P], hT3[:, P * t:P * t + P],
                                        W3[:, :], start=True, stop=True)
                if t % 4 == 3:
                    last.then_inc(proj_banks, 1)
            pe.wait_ge(proj_ready, 8 + T)
            for k in range(8):
                broadcast(diag3, 48 + k, k % 2)
            pe.wait_ge(bc_copied, 56)
            pe.wait_ge(over_ready, 2)
            nc.tensor.matmul(bank[7][:, 0:1], ones[:, :], over3[:, :], start=True, stop=True).then_inc(over_bank, 1)

            def over_all3():
                for c in range(4):
                    last = nc.tensor.matmul(bank[4 + c][:, :], zeros[:, :], zeros[:, 0:1].to_broadcast([P, BANK]),
                                            start=True, stop=False)

                def num_step(s, jt, b):
                    pe.wait_ge(lo_ready, 2 * s + 2)
                    pe.wait_ge(num_free, 2 * s + 2)
                    for kt in range(T):
                        if isinstance(s, int) and s % T == 0:
                            pe.wait_ge(atr_ready, s + kt + 1)
                        for part, den in enumerate((den_hi, den_lo)):
                            for c in range(2):
                                last = nc.tensor.matmul(bank[2 * b + c][:, :], den[b][:, kt, :],
                                                        ATr[:, kt, BANK * c:BANK * c + BANK],
                                                        start=kt == 0 and part == 0, stop=kt == T - 1 and part == 1)
                                if kt == T - 1 and part == 1:
                                    last.then_inc(num_bank, 1)

                def u_step(s, jt, b, half):
                    pe.wait_ge(xw_cur, s + 1)
                    for c in range(2):
                        pe.wait_ge(att_ready, 2 * s + c + 3)
                        last = nc.tensor.matmul(bank[4 + 2 * half + c][:, :], xwc[b][:, :], mx[c][:, :], start=False,
                                                stop=False)
                    last.then_inc(att_free, 1)

                steps(pe, num_step, u_step)
                for c in range(4):
                    nc.tensor.matmul(bank[4 + c][:, :], zeros[:, :], zeros[:, 0:1].to_broadcast([P, BANK]),
                                     start=False, stop=True).then_inc(u_bank, 1)
                pe.wait_ge(num_free, 4 * T + 4)
                for t in range(T):
                    pe.wait_ge(uT_ready, t // 4 + 1)
                    last = nc.tensor.transpose(bank[t // 4][:, P * (t % 4):P * (t % 4) + P], uT[:, P * t:P * t + P],
                                               ident[:, :])
                    if t % 4 == 3:
                        last.then_inc(u_turned, 1)

            def gather3(it, b):
                pe.wait_ge(g3_ready, it + 1)
                pe.wait_ge(e3_copied, it + 1)
                for c, (first, end) in enumerate(CHUNKS):
                    for jt in range(first, end):
                        nc.tensor.matmul(bank[4 + b][:, P * c:P * c + P], G3[b][:, jt, :],
                                         AT[:, jt, bass.ds(it * P, P)], start=jt == first, stop=jt == end - 1 and c > 0)
                    if c == 0:
                        nc.tensor.matmul(bank[4 + b][:, 0:P], Eb[:, bass.ds(it, 1), :].rearrange("p o s -> p (o s)"),
                                         identb[:, :], start=False, stop=True)
                    for jt in range(first, end):
                        last = nc.tensor.matmul(bank[4 + b][:, P * NC + 3 * c:P * NC + 3 * c + 3], G3[b][:, jt, :],
                                                rp[:, jt, :], start=jt == first, stop=jt == end - 1)
                last.then_inc(g3_used, 1)

            def num3(it, b, c):
                pe.wait_ge(denc_ready, 3 * it + 3)
                pe.wait_ge(t_ready, 4 * it + c + 1)
                for k in range(4):
                    j0 = P * (4 * c + k)
                    for part in range(NC):
                        last = nc.tensor.matmul(bank[c][:, P * k:P * k + P], denc[b][:, part, j0:j0 + P],
                                                ATc3[b][:, part, :], start=part == 0, stop=part == NC - 1)
                last.then_inc(num3_bank, 1)

            def u3(it, b, c):
                pe.wait_ge(att3_ready, 4 * it + c + 9)
                if c == 0:
                    pe.wait_ge(un3_kept, it + 1)
                for k in range(4):
                    last = nc.tensor.matmul(bank[6 + b][:, 0:D], yc[b][c][:, P * k:P * k + P], XW[:, 4 * c + k, :],
                                            start=c == 0 and k == 0, stop=c == 3 and k == 3)
                last.then_inc(att3_used, 1)

            def tile3(it, b):
                for c in range(4):
                    num3(it, b, c)
                    if within(it, -1):
                        u3(it - 1, 1 - b, c)
                if within(it, 2):
                    gather3(it + 2, b)

            def by_slots3():
                pe.wait_ge(rp_ready, 5)
                gather3(0, 0)
                gather3(1, 1)
                sweep(pe, tile3)
                for c in range(4):
                    u3(T - 1, 1, c)

            choose(pe, 3, by_slots3, over_all3)
            product(AT, pcs3, 3)

        @block.vector
        def _(dve):
            done = [0]

            def then(instruction):
                done[0] += 1
                instruction.then_inc(vec, 1)
                dve.wait_ge(vec, done[0])

            def layernorm(layer, dst):
                for t in range(T):
                    last = nc.vector.bn_stats(stats[:, t, :], X[:, t, :])
                then(last)
                for t in range(T):
                    last = nc.vector.bn_aggr(mv[:, t, :], stats[:, t, :])
                then(last)
                nc.vector.tensor_scalar(var[:, :], mv[:, :, 1:2].rearrange("p t o -> p (t o)"), EPS, None,
                                        ALU.add).then_inc(var_ready, 1)
                dve.wait_ge(rstd_ready, layer + 1)
                for t in range(T):
                    last = nc.vector.tensor_scalar(dst[:, t, :], X[:, t, :], mv[:, t, 0:1], rstd[:, t:t + 1],
                                                   ALU.subtract, ALU.mult)
                then(last)
                done[0] += 1
                nc.vector.tensor_scalar(dst[:, :, :], dst[:, :, :], 0.0, None, ALU.max).then_inc(vec, 1)
                dve.wait_ge(vec, done[0])
                dve.sem_inc(h_ready, 1)

            def split(src, dst, rest):
                then(nc.vector.tensor_copy(dst[:, :, 0:D], src))
                then(nc.vector.tensor_tensor(rest[:, :, :], src, dst[:, :, 0:D], ALU.subtract))
                then(nc.vector.tensor_copy(dst[:, :, D:2 * D], rest[:, :, :]))
                nc.vector.tensor_tensor(dst[:, :, 2 * D:3 * D], rest[:, :, :], dst[:, :, D:2 * D],
                                        ALU.subtract).then_inc(pieces_ready, 1)

            def join(src, dst):
                then(nc.vector.tensor_tensor(dst[:, :, :], src[:, :, 2 * D:3 * D], src[:, :, D:2 * D], ALU.add))
                then(nc.vector.tensor_tensor(dst[:, :, :], dst[:, :, :], src[:, :, 0:D], ALU.add))

            dve.wait_ge(x_loaded, 16)
            layernorm(0, h0)
            dve.wait_ge(w2T_banks, 1)
            then(nc.vector.tensor_copy(W2[:, :, :].rearrange("p k o -> p (k o)"), bank[6][:, 0:3 * D]))
            nc.vector.tensor_tensor(W2[:, 0, :], W2[:, 0, :], W2[:, 2, :], ALU.subtract).then_inc(w2_ready, 1)
            for q in range(4):
                dve.wait_ge(proj_banks, q + 1)
                nc.vector.tensor_copy(WH[:, 4 * q:4 * q + 4, :, 0:F],
                                      bank[4 + q][:, :].rearrange("p (t h f) -> p t h f", t=4, h=H)).then_inc(proj_ready, 1)
            dve.wait_ge(proj_ready, 4)
            pr = h0[:, :, :].rearrange("p t (h f) -> p t h f", h=H)
            for k, col in enumerate((pcol, ccol)):
                then(nc.vector.tensor_tensor(pr, WH[:, :, :, 0:F],
                                             attB[:, :, F * k:F * k + F].unsqueeze(1).to_broadcast([P, T, H, F]), ALU.mult))
                then(nc.vector.tensor_reduce(col[:, :, :], pr, AX_X, ALU.add))
            then(nc.vector.tensor_copy(c1col[:, :, :].rearrange("p h t -> p t h"), ccol[:, :, :]))
            then(nc.vector.tensor_copy(WX[:, :, H * F1:WC], ccol[:, :, :]))
            dve.sem_inc(logits_ready, 1)
            dve.wait_ge(wsum_bank, 1)
            nc.vector.tensor_copy(wsum[:, :, :].rearrange("p h f -> p (h f)"), bank[7][:, 0:H * F1]).then_inc(wsum_ready, 1)
            then(nc.vector.tensor_reduce(ext[:, 0:H], c1col[:, :, :], AX_X, ALU.max))
            then(nc.vector.tensor_reduce(ext[:, H:2 * H], c1col[:, :, :], AX_X, ALU.min))
            nc.vector.tensor_scalar(ext[:, H:2 * H], ext[:, H:2 * H], -1.0, None, ALU.mult).then_inc(ext_ready, 1)
            dve.wait_ge(ext_bank, 1)
            then(nc.vector.tensor_reduce(exm[:, :], bank[5][0:2 * H, 0:P], AX_X, ALU.max))
            nc.vector.tensor_scalar(exd[:, :], ident[0:2 * H, 0:2 * H], exm[:, 0:1], None, ALU.mult).then_inc(ext_ready, 1)
            dve.wait_ge(ext_bank, 2)
            then(nc.vector.tensor_copy(ctop[:, :], bank[5][:, 0:H]))
            then(nc.vector.tensor_scalar(cmin[:, :], bank[5][:, H:2 * H], -1.0, None, ALU.mult))
            then(nc.vector.tensor_tensor(spread[:, 0:H], ctop[:, :], cmin[:, :], ALU.subtract))
            then(nc.vector.tensor_reduce(spread[:, H:H + 1], spread[:, 0:H], AX_X, ALU.max))
            then(nc.vector.tensor_scalar(spread[:, H:H + 1], spread[:, H:H + 1], 60.0, None, ALU.is_gt))

            def leaky_sum(c):
                then(nc.vector.tensor_tensor(cmax[:, :, :], pcol[:, :, :], c, ALU.add))
                then(nc.vector.tensor_scalar(tcol[:, :, :], cmax[:, :, :], 0.2, None, ALU.mult))
                then(nc.vector.tensor_tensor(mcol[:, :, :], cmax[:, :, :], tcol[:, :, :], ALU.max))

            leaky_sum(ctop[:, :].unsqueeze(1).to_broadcast([P, T, H]))
            dve.sem_inc(guard_ready, 1)

            for it in range(T):
                for grp in range(2):
                    dve.wait_ge(at_bank, 2 * it + grp + 1)
                    nc.vector.tensor_copy(AT[:, 8 * grp:8 * grp + 8, P * it:P * it + P],
                                          bankb[2 * (it % 2) + grp][:, :].rearrange("p (j i) -> p j i", j=8)
                                          ).then_inc(at_copied, 1)
                dve.wait_ge(edge_bank, it + 1)
                nc.vector.tensor_scalar(some[:, it, :], bank[6 + it % 2][:, 0:T], 0.0, None,
                                        ALU.is_gt).then_inc(some_ready, 1)

            dve.wait_ge(rank_bank, 1)
            nc.vector.tensor_copy(iota[:, :], bank[5][:, 0:P]).then_inc(iota_ready, 1)
            dve.wait_ge(iota_ready, 1)
            dve.wait_ge(rank_bank, 2)
            then(nc.vector.tensor_tensor(slots[:, :, :], bank[4][:, 0:T * T].rearrange("p (i j) -> p i j", j=T),
                                         some[:, :, :], ALU.mult))
            then(nc.vector.tensor_reduce(over[:, :], slots[:, :, :].rearrange("p i j -> p (i j)"), AX_X, ALU.max))
            then(nc.vector.tensor_scalar(over[:, :], over[:, :], float(P - 1), None, ALU.is_gt))
            then(nc.vector.tensor_tensor(over[:, :], over[:, :], spread[:, H:H + 1], ALU.max))
            dve.sem_inc(over_ready, 1)
            nc.vector.tensor_copy(slotb[:, :, :], slots[:, :, :]).then_inc(choice, 1)
            dve.wait_ge(over_bank, 1)
            nc.vector.tensor_scalar(dense[:, :], bank[5][:, 0:1], 0.0, None, ALU.is_gt).then_inc(choice, 1)

            def finish(o):
                Ow, Osw = (t[:, :, :, :].rearrange("p t h f -> p t (h f)") for t in (o, Os))
                then(nc.vector.tensor_scalar(tcol[:, :, :].unsqueeze(3), o[:, :, :, F:F1], 0.0, None, ALU.is_equal))
                then(nc.vector.tensor_scalar(mk[:, :], tcol[:, :, 0:1].rearrange("p t o -> p (t o)"), 1.0, None,
                                             ALU.subtract))
                then(nc.vector.tensor_tensor(Os[:, :, :, :], tcol[:, :, :].unsqueeze(3).to_broadcast([P, T, H, F1]),
                                             wsum[:, :, :].unsqueeze(1).to_broadcast([P, T, H, F1]), ALU.mult))
                then(nc.vector.tensor_tensor(Ow, Ow, Osw, ALU.add))
                then(nc.vector.reciprocal(tcol[:, :, :].unsqueeze(3), o[:, :, :, F:F1]))
                then(nc.vector.tensor_tensor(o[:, :, :, 0:F], o[:, :, :, 0:F],
                                             tcol[:, :, :].unsqueeze(3).to_broadcast([P, T, H, F]), ALU.mult))
                X4 = X[:, :, :].rearrange("p t (h f) -> p t h f", h=H)
                then(nc.vector.tensor_tensor(X4, X4, o[:, :, :, 0:F], ALU.add))

            def over_all():
                then(nc.vector.tensor_scalar(cmin[:, :], cmin[:, :], 1.0, None, ALU.subtract))
                for h in range(H):
                    dve.wait_ge(bc_copied, 4 * h + 4)
                    then(nc.vector.tensor_scalar(cB[h][:, :], cB[h][:, :], cmin[:, h:h + 1], None, ALU.subtract))
                for it in range(T):
                    for h in range(H):
                        then(nc.vector.tensor_tensor_reduce(out=junk[:, :], in0=A[:, it, :], in1=cB[h][:, :], scale=1.0,
                                                            scalar=0.0, op0=ALU.mult, op1=ALU.max,
                                                            accum_out=cmax[:, it, h:h + 1]))
                then(nc.vector.tensor_tensor(cmax[:, :, :], cmax[:, :, :],
                                             cmin[:, :].unsqueeze(1).to_broadcast([P, T, H]), ALU.add))
                leaky_sum(cmax[:, :, :])
                dve.wait_ge(pieces0_ready, 17)
                nc.vector.tensor_scalar(p2col[:, :, :].rearrange("p h t -> p t h"), pcol[:, :, :], 0.2, None,
                                        ALU.mult).then_inc(guard_ready, 1)
                nc.vector.tensor_tensor(pmcol[:, :, :].rearrange("p h t -> p t h"), pcol[:, :, :], mcol[:, :, :],
                                        ALU.subtract).then_inc(guard_ready, 1)
                nc.vector.tensor_scalar(c2col[:, :, :], c1col[:, :, :], 0.2, None, ALU.mult).then_inc(guard_ready, 1)
                dve.wait_ge(guard_ready, 4)
                nc.vector.tensor_tensor(p2col[:, :, :].rearrange("p h t -> p t h"),
                                        p2col[:, :, :].rearrange("p h t -> p t h"), mcol[:, :, :],
                                        ALU.subtract).then_inc(guard_ready, 1)
                dve.wait_ge(at_copied, 2 * T + 4)
                with dve.Fori(0, 2) as g:
                    for e in range(2):
                        for half in range(2):
                            u = 4 * g + 2 * e + half
                            for jt in range(T):
                                n = T * u + jt
                                b = jt % 2
                                dve.wait_ge(uv_ready, 2 * n + 2)
                                nc.vector.tensor_tensor(ub[b][:, :], ub[b][:, :], vb[b][:, :], ALU.max).then_inc(pmax, 1)
                                dve.wait_ge(pmax, n + 1)
                                dve.wait_ge(p_free, n + 1)
                                nc.vector.tensor_tensor(pb[b][:, :], ub[b][:, :], AT[:, jt, HALF * half:HALF * half + HALF],
                                                        ALU.min).then_inc(p_ready, 1)
                                dve.wait_ge(p_ready, n + 1)
                                dve.sem_inc(uv_free, 1)
                            dve.wait_ge(o_turned, u + 3)
                            nc.vector.tensor_copy(O[:, HT * half:HT * half + HT, bass.ds(2 * g + e, 1), :].rearrange("p t o f -> p t (o f)"),
                                                  bank[6 + half][:, 0:HT * F1].rearrange("p (t f) -> p t f", f=F1)
                                                  ).then_inc(o_kept, 1)
                dve.wait_ge(o_kept, 8 + 2)
                finish(O)

            def one_hot(it, b):
                dve.wait_ge(gathered, it + 1)
                if not isinstance(it, int):
                    apart(dve)
                nc.vector.tensor_tensor(G[b % 2][:, :, :], iota[:, :].unsqueeze(1).to_broadcast([P, T, P]),
                                        slotb[:, bass.ds(it, 1), :].rearrange("p o j -> p (o j)").unsqueeze(2)
                                        .to_broadcast([P, T, P]), ALU.is_equal).then_inc(g_ready, 1)

            def edges_and_leaky(it, b):
                if not isinstance(it, int) or it < T - 1:
                    one_hot(it + 1, (b + 1) % 4)
                dve.wait_ge(gathered, it + 3)
                dve.wait_ge(pc_ready, it + 3)
                nc.vector.tensor_copy(ATc[b % 2][:, :, :].rearrange("p c i -> p (c i)"),
                                      bank[2 + b % 2][:, 0:NC * P]).then_inc(e_copied, 1)
                dve.wait_ge(zc_ready, it + 3)
                z = zc[b][:, :, :, :].rearrange("p c h i -> p (c h i)")
                nc.vector.scalar_tensor_tensor(z, z, 0.2, z, ALU.mult, ALU.max).then_inc(zc_leaky, 1)

            def mask(it, b):
                dve.wait_ge(zc_exp, it + 1)
                dve.wait_ge(e_copied, it + 3)
                nc.vector.tensor_tensor(zc[b][:, :, :, :], zc[b][:, :, :, :],
                                        ATc[b % 2][:, :, :].unsqueeze(2).to_broadcast([P, NC, H, P]),
                                        ALU.min).then_inc(pc_ready, 1)

            def by_slots():
                one_hot(0, 0)
                rounds(dve, edges_and_leaky, mask)
                dve.wait_ge(oc_copied, T)
                finish(Oc)

            before, after = done[0], []

            def counted(part):
                def run():
                    done[0] = before
                    part()
                    after.append(done[0])
                    if done[0] < after[0]:
                        dve.sem_inc(vec, after[0] - done[0])
                    done[0] = after[0]
                return run

            choose(dve, 0, counted(by_slots), counted(over_all))

            layernorm(1, h1)
            then(nc.vector.memset(pcs[:, :, 3 * D:PW], 1.0))
            split(h1[:, :, :], pcs, s1)
            dve.wait_ge(mm_copied, T + 2)
            dg = acc[:, :, 3 * D:PC].rearrange("p t o -> p (t o)")
            then(nc.vector.tensor_scalar(inv[:, :], dg, 0.0, None, ALU.is_equal))
            then(nc.vector.tensor_tensor(deg[:, :], dg, inv[:, :], ALU.add))
            then(nc.vector.reciprocal(deg[:, :], deg[:, :]))
            then(nc.vector.tensor_scalar(inv[:, :], dg, 0.0, None, ALU.not_equal))
            then(nc.vector.tensor_tensor(inv[:, :], inv[:, :], deg[:, :], ALU.mult))
            join(acc, s1)
            then(nc.vector.tensor_tensor(s1[:, :, :], s1[:, :, :], inv[:, :].unsqueeze(2).to_broadcast([P, T, D]),
                                         ALU.mult))
            then(nc.vector.tensor_tensor(X[:, :, :], X[:, :, :], s1[:, :, :], ALU.add))

            layernorm(2, h1)

            def narrow(half, tiles):
                for kt in tiles:
                    nc.vector.tensor_copy(ATr[:, kt, :], AT[:, kt, HALF * half:HALF * half + HALF]).then_inc(atr_ready, 1)

            dve.wait_ge(proj_ready, 4 + T)
            split(ys[:, :, 2 * D:3 * D], pcs, s1)
            narrow(0, range(T))
            dve.wait_ge(mm_copied, 2 * T + 2)
            join(acc, s1)
            then(nc.vector.scalar_tensor_tensor(s1[:, :, :], s1[:, :, :], 2.0, ys[:, :, D:2 * D], ALU.mult, ALU.add))
            split(s1[:, :, :], pcs, h1)
            dve.wait_ge(mm_copied, 3 * T + 2)
            join(acc, s1)
            then(nc.vector.tensor_tensor(s1[:, :, :], s1[:, :, :], ys[:, :, 0:D], ALU.add))
            then(nc.vector.tensor_tensor(X[:, :, :], X[:, :, :], s1[:, :, :], ALU.add))

            layernorm(3, h3)
            dve.wait_ge(proj_ready, 8 + T)
            for k, col in enumerate((c3, r3)):
                then(nc.vector.tensor_tensor(pr3[:, :, :], XW[:, :, :],
                                             a3B[:, k:k + 1, :].to_broadcast([P, T, D]), ALU.mult))
                last = nc.vector.tensor_reduce(col[:, :], pr3[:, :, :], AX_X, ALU.add)
                then(last)
            nc.vector.tensor_scalar(c3s[:, :], c3[:, :], 0.01, None, ALU.mult).then_inc(logits_ready, 1)
            then(nc.vector.tensor_tensor(inv[:, :], c3[:, :], c3[:, :], ALU.mult))
            then(nc.vector.tensor_tensor(deg[:, :], r3[:, :], r3[:, :], ALU.mult))
            then(nc.vector.tensor_tensor(inv[:, :], inv[:, :], deg[:, :], ALU.max))
            then(nc.vector.tensor_reduce(over3[:, :], inv[:, :], AX_X, ALU.max))
            then(nc.vector.tensor_scalar(over3[:, :], over3[:, :], 100.0, None, ALU.is_gt))
            nc.vector.tensor_tensor(over3[:, :], over3[:, :], over[:, :], ALU.max).then_inc(over_ready, 1)
            dve.wait_ge(over_bank, 2)
            nc.vector.tensor_scalar(dense3[:, :], bank[7][:, 0:1], 0.0, None, ALU.is_gt).then_inc(choice, 1)

            def over_all3():
                def leaky_step(s, jt, b):
                    for q in range(2):
                        dve.wait_ge(z_ready, 2 * s + q + 1)
                        nc.vector.scalar_tensor_tensor(zb[q][:, :, :], zb[q][:, :, :], 0.01, zb[q][:, :, :], ALU.mult,
                                                       ALU.max).then_inc(leaky_ready, 1)

                def rec_step(s, jt, b, half):
                    dve.wait_ge(att_free, s + 2)
                    for c in range(2):
                        dve.wait_ge(num_bank, 2 * s + c + 5)
                        nc.vector.tensor_scalar(mx[c][:, :], bank[2 * b + c][:, :], TINY, None, ALU.max).then_inc(rec_seq, 1)
                        dve.wait_ge(dT_ready, 2 * s + c + 1)
                        nc.vector.tensor_tensor(dT[c][:, :], dT[c][:, :], dv[c][:, :], ALU.max).then_inc(dmax, 1)
                        dve.wait_ge(dmax, 2 * s + c + 1)
                        nc.vector.scalar_tensor_tensor(dT[c][:, :], bank[2 * b + c][:, :], 0.0, dT[c][:, :],
                                                       ALU.not_equal, ALU.mult).then_inc(num_free, 1)
                        dve.wait_ge(rec_seq, 2 * s + c + 1)
                        dve.wait_ge(num_free, 2 * s + c + 5)
                        nc.vector.reciprocal(mx[c][:, :], mx[c][:, :]).then_inc(rec_ready, 1)

                def second_half():
                    dve.wait_ge(num_bank, 2 * T + 4)
                    narrow(1, range(T))

                steps(dve, leaky_step, rec_step, second_half)
                dve.wait_ge(un_ready, 4)

            def one_hot3(it, b):
                dve.wait_ge(g3_used, it + 1)
                if not isinstance(it, int):
                    apart(dve)
                nc.vector.tensor_tensor(G3[b][:, :, :], iota[:, :].unsqueeze(1).to_broadcast([P, T, P]),
                                        slotb[:, bass.ds(it, 1), :].rearrange("p o j -> p (o j)").unsqueeze(2)
                                        .to_broadcast([P, T, P]), ALU.is_equal).then_inc(g3_ready, 1)

            def edges3(it, b):
                dve.wait_ge(g3_used, it + 3)
                dve.wait_ge(num3_bank, 4 * it + 4)
                nc.vector.tensor_copy(ATc3[b][:, :, :].rearrange("p c i -> p (c i)"), bank[4 + b][:, 0:NC * P])
                pieces = bank[4 + b][:, NC * P:NC * P + 3 * NC].rearrange("p (c k) -> p c k", k=3)
                r_of = rc[b][:, :].unsqueeze(2)
                if within(it, -2):
                    dve.wait_ge(u3_ready, 3 * it - 3)
                nc.vector.tensor_copy(r_of, pieces[:, :, 2:3]).then_inc(rc_seq, 1)
                dve.wait_ge(rc_seq, 3 * it + 1)
                nc.vector.tensor_tensor(r_of, r_of, pieces[:, :, 1:2], ALU.add).then_inc(rc_seq, 1)
                dve.wait_ge(rc_seq, 3 * it + 2)
                nc.vector.tensor_tensor(r_of, r_of, pieces[:, :, 0:1], ALU.add).then_inc(rc_seq, 1)
                dve.wait_ge(rc_seq, 3 * it + 3)
                dve.sem_inc(e3_copied, 1)

            def den3(it, b, c):
                dve.wait_ge(er_ready, it + 1)
                dve.wait_ge(u3_ready, 3 * it + c + 1)
                nc.vector.scalar_tensor_tensor(denc[b][:, c, :], E01[:, :], er[b][:, c:c + 1], denc[b][:, c, :],
                                               ALU.mult, ALU.max).then_inc(denc_ready, 1)

            def newton3(it, b, c):
                n = 4 * it + c
                dve.wait_ge(y_ready, n + 1)
                if not isinstance(n, int) or n >= 2:
                    dve.wait_ge(s_ready, n - 1)
                nc.vector.tensor_tensor(tc[c % 2][:, :], bank[c][:, :], yc[b][c][:, :], ALU.mult).then_inc(t_ready, 1)
                dve.wait_ge(t_ready, n + 5)
                nc.vector.scalar_tensor_tensor(yc[b][c][:, :], tc[c % 2][:, :], 2.0, yc[b][c][:, :], ALU.subtract,
                                               ALU.mult).then_inc(s_ready, 1)

            def leaky3(it, b):
                dve.wait_ge(z3_ready, it + 1)
                z = dTc[b][:, :, :].rearrange("p j i -> p (j i)")
                nc.vector.scalar_tensor_tensor(z, z, 0.01, z, ALU.mult, ALU.max).then_inc(z3_leaky, 1)

            def keep3(it, b):
                dve.wait_ge(att3_used, 4 * it + 12)
                if not isinstance(it, int):
                    apart(dve)
                nc.vector.tensor_tensor(Un[:, bass.ds(it, 1), :].rearrange("p o f -> p (o f)"), bank[6 + b][:, 0:D],
                                        mk[:, bass.ds(it, 1)].to_broadcast([P, D]), ALU.mult).then_inc(un3_kept, 1)

            def tile3(it, b):
                if within(it, 1):
                    edges3(it + 1, 1 - b)
                if within(it, 2):
                    one_hot3(it + 2, b)
                for c in range(4):
                    if within(it, 1):
                        if c < NC:
                            den3(it + 1, 1 - b, c)
                        else:
                            leaky3(it + 1, 1 - b)
                    newton3(it, b, c)
                if within(it, -1):
                    keep3(it - 1, 1 - b)

            def by_slots3():
                nc.vector.tensor_copy(rp[:, :, 0:1], r3[:, :].unsqueeze(2)).then_inc(rp_ready, 1)
                nc.vector.memset(Eb[:, :, :], 0.0).then_inc(rp_ready, 1)
                dve.wait_ge(rp_ready, 2)
                nc.vector.tensor_tensor(r3[:, :].unsqueeze(2), r3[:, :].unsqueeze(2), rp[:, :, 0:1],
                                        ALU.subtract).then_inc(rp_ready, 1)
                dve.wait_ge(rp_ready, 3)
                nc.vector.tensor_copy(rp[:, :, 1:2], r3[:, :].unsqueeze(2)).then_inc(rp_ready, 1)
                nc.vector.tensor_scalar(Eb[:, :, P - 1:P], mk[:, :].unsqueeze(2), 1.0, None, ALU.add)
                dve.wait_ge(rp_ready, 4)
                nc.vector.tensor_tensor(rp[:, :, 2:3], r3[:, :].unsqueeze(2), rp[:, :, 1:2],
                                        ALU.subtract).then_inc(rp_ready, 1)
                one_hot3(0, 0)
                one_hot3(1, 1)
                edges3(0, 0)
                dve.wait_ge(e01_ready, 1)
                for c in range(NC):
                    den3(0, 0, c)
                leaky3(0, 0)
                sweep(dve, tile3)
                keep3(T - 1, 1)
                dve.wait_ge(un3_kept, T + 2)

            choose(dve, 3, by_slots3, over_all3)
            then(nc.vector.memset(pcs3[:, :, 3 * D:PW], 1.0))
            split(Un[:, :, :], pcs3, s3[0])
            dve.wait_ge(mm_copied, 4 * T + 2)
            join(acc3, s3[1])
            nc.vector.tensor_tensor(X[:, :, :], X[:, :, :], s3[1][:, :, :], ALU.add).then_inc(x_final, 1)


_INS = ["x", "adj", "L0_gnn_weight", "L0_gnn_att_weight", "L2_gnn_W", "L3_gnn_W", "L3_gnn_a"]


def kernel(**inputs):
    import numpy as np
    import concourse.bacc as bacc
    from concourse import mybir as mb
    from concourse.bass_utils import run_bass_kernel_spmd

    nc = bacc.Bacc("TRN2", target_bir_lowering=False, num_devices=1, dynamic_dma_scratch_size=1024)
    arrays, args = {}, []
    for name in _INS:
        a = np.ascontiguousarray(inputs[name])
        arrays[f"in_{name}"] = a
        args.append(nc.dram_tensor(f"in_{name}", a.shape, mb.dt.from_np(a.dtype), kind="ExternalInput").ap())
    args.append(nc.dram_tensor("out_0", (N, D), mb.dt.float32, kind="ExternalOutput").ap())
    gnn_stack(nc, *args)
    r = run_bass_kernel_spmd(nc, [arrays], core_ids=[0])
    return r.results[0]["out_0"]
```

```python
import concourse.bass as bass
from concourse import mybir
from contextlib import ExitStack

F32 = mybir.dt.float32
F32R = mybir.dt.float32r
I32 = mybir.dt.int32
BF16 = mybir.dt.bfloat16
ALU = mybir.AluOpType
ACT = mybir.ActivationFunctionType
AX_X = mybir.AxisListType.X

P = 128
N = 2048
T = N // P
D = 128
H = 4
F = D // H
F1 = F + 1
HALF = N // 2
HT = T // 2
GT = 4
NG = T // GT
BANK = 512
PW = 3 * D + 2
PC = 3 * D + 1
WC = H * F1 + H
CHUNKS = ((0, 5), (5, 10), (10, 16))
NC = len(CHUNKS)
EPS = 1e-5
TINY = 1.2e-38
KB = 1024
LOW = 1.25


def gnn_stack(nc, x, adj, w0, att0, w2, w3, a3, out):
    ctx = ExitStack()
    with ctx:
        def at(name, kb, shape, dt=F32):
            return nc.alloc_sbuf_tensor_at(name, shape, dt, offset=int((kb + LOW) * KB))

        def sem(name):
            return ctx.enter_context(nc.semaphore(name))

        A = at("A", 0, [P, T, N], BF16)
        ATr = at("ATr", 0, [P, T, HALF], F32R)
        AT = at("AT", 64, [P, T, N], BF16)
        X = at("X", 128, [P, T, D])
        WX = at("WX", 136, [P, T, WC])
        WH = WX[:, :, 0:H * F1].rearrange("p t (h f) -> p t h f", f=F1)
        B = 144.5
        a32 = [at(f"a32_{b}", B + 8 * b, [P, N]) for b in range(2)]
        cB = [at(f"cB_{h}", B + 16 + 8 * h, [P, N]) for h in range(H)]
        junk = at("junk", B + 48, [P, N], BF16)
        attB = at("attB", B + 48, [P, H, 2 * F])
        W0 = at("W0", B + 49, [P, D])
        h0 = at("h0", B + 52, [P, T, D])
        hT0 = at("hT0", B + 60, [P, N])
        ext = at("ext", B + 50, [P, 2 * H])
        exm = at("exm", B + 50.125, [2 * H, 1])
        exd = at("exd", B + 50.25, [2 * H, 2 * H])
        whc = [at(f"whc_{e}", B + 2.25 * e, [P, T, F1]) for e in range(2)]
        oT = [at(f"oT_{e}", B + 5 + 4 * e, [F1, HALF]) for e in range(2)]
        pmB = at("pmB", B + 13, [P, N])
        p2B = at("p2B", B + 21, [P, N])
        ub = [at(f"ub_{b}", B + 29 + 4 * b, [P, HALF]) for b in range(2)]
        vb = [at(f"vb_{b}", B + 37 + 4 * b, [P, HALF]) for b in range(2)]
        pb = [at(f"pb_{b}", B + 45 + 4 * b, [P, HALF]) for b in range(2)]
        diag = [at(f"diag_{b}", B + 53 + 2 * b, [P, BANK]) for b in range(2)]
        O = at("O", B + 57, [P, T, H, F1])
        pmcol, p2col, c2col = (at(name, B + 65.5 + 0.25 * k, [P, H, T]) for k, name in enumerate(("pmcol", "p2col", "c2col")))
        Oc = at("Oc", 136, [P, T, H, F1])
        slots = at("slots", B + 48, [P, T, T])
        G = [at(f"G_{b}", B + 4 * b, [P, T, P], BF16) for b in range(2)]
        zc = [at(f"zc_{b}", B + 8 + 6 * b, [P, NC, H, P]) for b in range(4)]
        wc = [at(f"wc_{b}", B + 32 + 1.75 * b, [P, NC, WC]) for b in range(4)]
        ATc = [at(f"ATc_{b}", B + 39 + 0.75 * b, [P, NC, P], BF16) for b in range(2)]
        mB = [at(f"mB_{b}", [B + 42, B + 52][b], [P, H * P]) for b in range(2)]
        rows = [at(f"rows_{b}", B + 44 + 4 * b, [P, H, P]) for b in range(2)]
        rest0 = at("rest0", B + 52, [P, 4, WC])
        tri = at("tri", B + 54.25, [P, P], BF16)
        some = at("some", B + 54.75, [P, T, T], BF16)
        whp = at("whp", B + 55.25, [P, T, 3, WC], BF16)
        Os = at("Os", B + 29, [P, T, H, F1])
        accs = [at(f"accs_{b}", B + 15.375 + 6.03125 * b, [P, GT, PC]) for b in range(2)]
        pcs2 = at("pcs2", B + 27.4375, [P, T, 3 * D], BF16)
        pcs = at("pcs", B + 39.4375, [P, T, PW], BF16)
        h1 = at("h1", B + 51.5, [P, T, D])
        ys = at("ys", 136, [P, T, 3 * D])
        sg = at("sg", B + 60, [P, GT, D])
        rest = at("rest", B + 62, [P, GT, D])
        hTs = [at(f"hTs_{b}", B + 64 + 2 * b, [P, BANK]) for b in range(2)]
        sg3 = at("sg3", B + 27.75, [P, GT, D])
        hTs3 = [at(f"hTs3_{b}", B + 29.75 + 2 * b, [P, BANK]) for b in range(2)]
        pr3 = at("pr3", B + 33.75, [P, GT, D])
        den_hi = [at(f"den_hi_{b}", 136 + 8 * b, [P, T, P], F32R) for b in range(2)]
        den_lo = [at(f"den_lo_{b}", 152 + 8 * b, [P, T, P], F32R) for b in range(2)]
        zb = [at(f"zb_{b}", 168 + 4 * b, [P, HT, P]) for b in range(2)]
        dv = [at(f"dv_{b}", 176 + 2 * b, [P, BANK]) for b in range(2)]
        diag3 = [at(f"diag3_{b}", 168 + 2 * b, [P, BANK]) for b in range(2)]
        cB3 = at("cB3", 180, [P, N])
        rB3 = at("rB3", 188, [P, N])
        dT = [at(f"dT_{b}", 196 + 2 * b, [P, BANK]) for b in range(2)]
        mx = [at(f"mx_{b}", 200 + 2 * b, [P, BANK]) for b in range(2)]
        XW = at("XW", 204, [P, T, D])
        uT = at("uT", 136, [P, N])
        Un = at("Un", 144, [P, T, D])
        accs3 = [at(f"accs3_{b}", 152 + 6.03125 * b, [P, GT, PC]) for b in range(2)]
        pcs3 = at("pcs3", 176.5, [P, T, PW], BF16)
        s3 = at("s3", 189, [P, GT, D])
        rest3 = at("rest3", 191, [P, GT, D])

        denc = [at(f"denc_{b}", 24 * b, [P, NC, N]) for b in range(2)]
        dTc = [at(f"dTc_{b}", 48 + 8 * b, [P, T, P]) for b in range(2)]
        G3 = [at(f"G3_{b}", 136 + 4 * b, [P, T, P], BF16) for b in range(2)]
        yc = [[at(f"yc_{b}{c}", 152 + 8 * b + 2 * c, [P, BANK]) for c in range(4)] for b in range(2)]
        E01 = at("E01", 168, [P, N])
        Eb = at("Eb", 176, [P, T, P], BF16)
        ATc3 = [at(f"ATc3_{b}", 196 + 1.5 * b, [P, NC, P]) for b in range(2)]
        tc = [at(f"tc_{b}", 199 + 2 * b, [P, BANK]) for b in range(2)]

        top = [(LOW + 212.5) * KB]

        def const(name, shape, dt=F32):
            size = 1
            for n in shape[1:]:
                size *= n
            size = -(-size * (2 if dt == BF16 else 4) // 32) * 32
            t = nc.alloc_sbuf_tensor_at(name, shape, dt, offset=int(top[0]))
            top[0] += size
            return t

        ident = const("ident", [P, P])
        identb = const("identb", [P, P], BF16)
        ones = const("ones", [P, P])
        zeros = const("zeros", [P, P], BF16)
        onesb = const("onesb", [P, P], BF16)
        slotb = const("slotb", [P, T, T], BF16)
        iota = const("iota", [P, P], BF16)
        rp = const("rp", [P, T, 3], BF16)
        rc = [const(f"rc_{b}", [P, NC]) for b in range(2)]
        er = [const(f"er_{b}", [P, NC]) for b in range(2)]
        minus2 = const("minus2", [P, 1])
        mk = const("mk", [P, T])
        over3 = const("over3", [P, 1])
        dense3 = const("dense3", [P, 1], I32)
        over = const("over", [P, 1])
        dense = const("dense", [P, 1], I32)
        W3 = const("W3", [P, D])
        a3B = const("a3B", [P, 2, D])
        W2 = const("W2", [P, 3, D])
        stats = const("stats", [P, T, 6])
        mv = const("mv", [P, T, 2])
        var = const("var", [P, T])
        power = const("power", [P, T])
        rstd = const("rstd", [P, T])
        pcol = const("pcol", [P, T, H])
        ccol = const("ccol", [P, T, H])
        mcol = const("mcol", [P, T, H])
        qcol = mcol
        tcol = const("tcol", [P, T, H])
        cmin = const("cmin", [P, H])
        ctop = const("ctop", [P, H])
        spread = const("spread", [P, H + 1])
        c1col = const("c1col", [P, H, T])
        cc = [const(f"cc_{e}", [P, T]) for e in range(2)]
        cc2 = [const(f"cc2_{e}", [P, T]) for e in range(2)]
        wsum = const("wsum", [P, H, F1])
        cmax = nc.alloc_sbuf_tensor_at("cmax", [P, T, H], F32, offset=int(top[0]))
        xwc = [const(f"xwc_{b}", [P, D]) for b in range(2)]
        c3 = const("c3", [P, T])
        c3s = const("c3s", [P, T])
        r3 = const("r3", [P, T])
        inv = const("inv", [P, T])
        deg = const("deg", [P, T])

        bank = [ctx.enter_context(nc.psum_tensor(f"bank{i}", [P, BANK], F32)) for i in range(8)]
        bankb = [b[:, :].bitcast(BF16) for b in bank]

        x_loaded = sem("x_loaded")
        w_loaded = sem("w_loaded")
        a_loaded = [sem(f"a_loaded{b}") for b in range(2)]
        a_ready = sem("a_ready")
        const_ready = sem("const_ready")
        vec = sem("vec")
        h_ready = sem("h_ready")
        var_ready = sem("var_ready")
        rstd_ready = sem("rstd_ready")
        hT_banks = sem("hT_banks")
        hT_ready = sem("hT_ready")
        w2T_banks = sem("w2T_banks")
        w2_ready = sem("w2_ready")
        proj_banks = sem("proj_banks")
        proj_ready = sem("proj_ready")
        wsum_bank = sem("wsum_bank")
        wsum_ready = sem("wsum_ready")
        logits_ready = sem("logits_ready")
        diag_ready = sem("diag_ready")
        bc_bank = sem("bc_bank")
        bc_copied = sem("bc_copied")
        at_bank = sem("at_bank")
        at_copied = sem("at_copied")
        pieces0_ready = sem("pieces0_ready")
        edge_bank = sem("edge_bank")
        some_ready = sem("some_ready")
        rank_bank = sem("rank_bank")
        iota_ready = sem("iota_ready")
        over_ready = sem("over_ready")
        over_bank = sem("over_bank")
        choice = sem("choice")
        g_ready = sem("g_ready")
        gathered = sem("gathered")
        w_copied = sem("w_copied")
        e_copied = sem("e_copied")
        rows_ready = sem("rows_ready")
        rows_bank = sem("rows_bank")
        q_copied = sem("q_copied")
        mB_ready = sem("mB_ready")
        zc_ready = sem("zc_ready")
        zc_leaky = sem("zc_leaky")
        zc_less = sem("zc_less")
        zc_exp = sem("zc_exp")
        pc_ready = sem("pc_ready")
        pc_used = sem("pc_used")
        oc_copied = sem("oc_copied")
        e01_ready = sem("e01_ready")
        rp_ready = sem("rp_ready")
        g3_ready = sem("g3_ready")
        g3_used = sem("g3_used")
        rc_seq = sem("rc_seq")
        e3_copied = sem("e3_copied")
        er_ready = sem("er_ready")
        u3_ready = sem("u3_ready")
        denc_ready = sem("denc_ready")
        num3_bank = sem("num3_bank")
        ln_ready = sem("ln_ready")
        y_ready = sem("y_ready")
        t_ready = sem("t_ready")
        less2_ready = sem("less2_ready")
        deny_ready = sem("deny_ready")
        z3_ready = sem("z3_ready")
        z3_leaky = sem("z3_leaky")
        dT3_ready = sem("dT3_ready")
        att3_ready = sem("att3_ready")
        att3_used = sem("att3_used")
        un3_kept = sem("un3_kept")
        ext_ready = sem("ext_ready")
        ext_bank = sem("ext_bank")
        guard_ready = sem("guard_ready")
        cur_ready = sem("cur_ready")
        uv_ready = sem("uv_ready")
        uv_free = sem("uv_free")
        p_ready = sem("p_ready")
        p_free = sem("p_free")
        oT_ready = sem("oT_ready")
        o_turned = sem("o_turned")
        o_kept = sem("o_kept")
        pieces_ready = sem("pieces_ready")
        mm_bank = sem("mm_bank")
        mm_copied = sem("mm_copied")
        shift_ready = sem("shift_ready")
        h1_ready = sem("h1_ready")
        acc_used = sem("acc_used")
        atr_ready = sem("atr_ready")
        xw_cur = sem("xw_cur")
        z_ready = sem("z_ready")
        den_ready = sem("den_ready")
        lo_ready = sem("lo_ready")
        num_bank = sem("num_bank")
        num_free = sem("num_free")
        dT_ready = sem("dT_ready")
        rec_ready = sem("rec_ready")
        att_ready = sem("att_ready")
        att_free = sem("att_free")
        u_bank = sem("u_bank")
        uT_ready = sem("uT_ready")
        u_turned = sem("u_turned")
        un_ready = sem("un_ready")
        pmax = sem("pmax")
        rec_seq = sem("rec_seq")
        act_seq = sem("act_seq")
        leaky_ready = sem("leaky_ready")
        dmax = sem("dmax")
        x_final = sem("x_final")
        passed = sem("passed")
        stored = sem("stored")

        CREDIT = {uv_free: 2, p_free: 2, oT_ready: 4, o_turned: 2, o_kept: 2, at_copied: 4, mm_copied: 2,
                  some_ready: 2, gathered: 2, w_copied: 2, e_copied: 2, rows_bank: 2, zc_less: 2, pc_ready: 4,
                  g3_used: 2, e3_copied: 2, num3_bank: 8, acc_used: 2, t_ready: 4, att3_ready: 8, att3_used: 8, un3_kept: 2,
                  pc_used: 4, zc_ready: 2, num_bank: 4, num_free: 4, att_ready: 2, att_free: 2}

        def apart(engine):
            engine.sem_inc(passed, 1)

        def choose(engine, layer, by_slots, over_all):
            first = layer == 0
            engine.wait_ge(choice, 2 if first else 3)
            flag = engine.alloc_register(f"dense_{layer}_" + str(engine.engine).split(".")[-1])
            engine.reg_load(flag, (dense if first else dense3)[0:1, 0:1])
            with engine.If_ne(flag, 0):
                over_all()
            with engine.Else():
                by_slots()

        def sweep(engine, tile_step):
            for it in range(2):
                tile_step(it, it)
            with engine.Fori(1, HT - 1) as g:
                for b in range(2):
                    tile_step(2 * g + b, b)
            for it in range(T - 2, T):
                tile_step(it, it % 2)

        def within(it, ahead):
            return not isinstance(it, int) or 0 <= it + ahead < T

        def rounds(engine, lead, follow):
            lead(0, 0)
            for it in range(2):
                lead(it + 1, it + 1)
                follow(it, it)
            with engine.Fori(0, T // 4 - 1) as g:
                for k in range(2, 6):
                    lead(4 * g + k + 1, (k + 1) % 4)
                    follow(4 * g + k, k % 4)
            lead(T - 1, 3)
            follow(T - 2, 2)
            follow(T - 1, 3)

        def steps(engine, lead, follow, turn=None):
            lead(0, 0, 0)
            for half in range(2):
                s0 = T * half
                with engine.Fori(0, HT - 1) as g:
                    for b in range(2):
                        lead(s0 + 2 * g + b + 1, 2 * g + b + 1, (b + 1) % 2)
                        follow(s0 + 2 * g + b, 2 * g + b, b, half)
                lead(s0 + T - 1, T - 1, 1)
                follow(s0 + T - 2, T - 2, 0, half)
                if half == 0:
                    if turn is not None:
                        turn()
                    lead(T, 0, 0)
                follow(s0 + T - 1, T - 1, 1, half)

        block = ctx.enter_context(nc.Block())

        @block.sync
        def _(sp):
            sp.dma_start(X[:, :, :], x.rearrange("(t p) f -> p t f", p=P)).then_inc(x_loaded, 16)

            def load(it, b):
                sp.dma_start(a32[b][:, :], adj[bass.ds(it * P, P), :]).then_inc(a_loaded[b], 16)

            load(0, 0)
            load(1, 1)
            with sp.Fori(1, HT) as g:
                for b in range(2):
                    sp.wait_ge(a_ready, 2 * g + b - 1)
                    load(2 * g + b, b)
            outT = out.rearrange("(t p) f -> p t f", p=P)
            for q in range(NG):
                ts = slice(GT * q, GT * q + GT)
                sp.wait_ge(x_final, q + 1)
                sp.dma_start(outT[:, ts, :], X[:, ts, :]).then_inc(stored, 16)
            sp.wait_ge(stored, 16 * NG)

        @block.gpsimd
        def _(pool):
            for free, count in CREDIT.items():
                pool.sem_inc(free, count)
            nc.gpsimd.memset(ones[:, :], 1.0).then_inc(const_ready, 1)
            nc.gpsimd.memset(zeros[:, :], 0.0).then_inc(const_ready, 1)
            nc.gpsimd.memset(power[:, :], -0.5).then_inc(const_ready, 1)
            nc.gpsimd.memset(WH[:, :, :, F:F1], 1.0).then_inc(const_ready, 1)
            nc.gpsimd.memset(onesb[:, :], 1.0).then_inc(const_ready, 1)
            nc.gpsimd.memset(minus2[:, :], -2.0)
            pool.wait_ge(const_ready, 5)
            nc.gpsimd.affine_select(out=ident[:, :], in_=ones[:, :], compare_op=ALU.is_equal, fill=0.0, base=0,
                                    pattern=[[-1, P]], channel_multiplier=1).then_inc(const_ready, 1)
            pool.wait_ge(const_ready, 6)
            nc.gpsimd.tensor_copy(identb[:, :], ident[:, :]).then_inc(const_ready, 1)

            def rstd_of(layer):
                for q in range(NG):
                    ts = slice(GT * q, GT * q + GT)
                    pool.wait_ge(var_ready, NG * layer + q + 1)
                    nc.gpsimd.tensor_tensor(rstd[:, ts], var[:, ts], power[:, ts], ALU.pow).then_inc(rstd_ready, 1)

            def diagonal(dst, col, n):
                if not isinstance(n, int) or n >= 2:
                    pool.wait_ge(bc_bank, n - 1)
                if not isinstance(n, int):
                    apart(pool)
                nc.gpsimd.tensor_tensor(dst[:, :].rearrange("p (t q) -> p t q", q=P),
                                        ident[:, :].unsqueeze(1).to_broadcast([P, 4, P]),
                                        col.unsqueeze(2).to_broadcast([P, 4, P]), ALU.mult).then_inc(diag_ready, 1)

            rstd_of(0)
            pool.wait_ge(logits_ready, 1)
            pool.wait_ge(guard_ready, 1)
            nc.gpsimd.affine_select(out=tri[:, :], in_=onesb[:, :], compare_op=ALU.is_ge, fill=0.0, base=0,
                                    pattern=[[1, P]], channel_multiplier=-1).then_inc(pieces0_ready, 1)
            count = 1
            for q in range(4):
                ts = slice(4 * q, 4 * q + 4)
                for k, (dst, x0, x1) in enumerate((
                        (whp[:, ts, 0, :], WX[:, ts, :], None),
                        (rest0[:, :, :], WX[:, ts, :], whp[:, ts, 0, :]),
                        (whp[:, ts, 1, :], rest0[:, :, :], None),
                        (whp[:, ts, 2, :], rest0[:, :, :], whp[:, ts, 1, :]))):
                    if x1 is None:
                        step = nc.gpsimd.tensor_copy(dst, x0)
                    else:
                        step = nc.gpsimd.tensor_tensor(dst, x0, x1, ALU.subtract)
                    step.then_inc(pieces0_ready, 1)
                    count += 1
                    pool.wait_ge(pieces0_ready, count)

            def over_all():
                for n in range(16):
                    diagonal(diag[n % 2], c1col[:, n // 4, 4 * (n % 4):4 * (n % 4) + 4], n)
                pool.wait_ge(guard_ready, 5)
                pool.wait_ge(bc_copied, 16)
                with pool.Fori(0, 2) as g:
                    for e in range(2):
                        h = 2 * g + e
                        pool.wait_ge(oT_ready, 4 * g + 2 * e + 2)
                        nc.gpsimd.tensor_copy(whc[e][:, :, :], WH[:, :, bass.ds(h, 1), :].rearrange("p t o f -> p t (o f)")).then_inc(cur_ready, 1)
                        nc.gpsimd.tensor_copy(cc[e][:, :], c1col[:, bass.ds(h, 1), :].rearrange("p o t -> p (o t)")).then_inc(cur_ready, 1)
                        nc.gpsimd.tensor_copy(cc2[e][:, :], c2col[:, bass.ds(h, 1), :].rearrange("p o t -> p (o t)")).then_inc(cur_ready, 1)
                        for half in range(2):
                            for k in range(4):
                                col = (pmcol, p2col)[k // 2]
                                t0 = HT * half + 4 * (k % 2)
                                diagonal(diag[k % 2], col[:, bass.ds(h, 1), t0:t0 + 4].rearrange("p o t -> p (o t)"),
                                         16 + 16 * g + 8 * e + 4 * half + k)
                pool.wait_ge(bc_bank, 48)

            def row_diagonals(it, b):
                pool.wait_ge(rows_bank, it + 1)
                if not isinstance(it, int):
                    apart(pool)
                nc.gpsimd.tensor_tensor(rows[b % 2][:, :, :], ident[:, :].unsqueeze(1).to_broadcast([P, H, P]),
                                        qcol[:, bass.ds(it, 1), :].rearrange("p o h -> p (o h)").unsqueeze(2)
                                        .to_broadcast([P, H, P]), ALU.mult).then_inc(rows_ready, 1)

            def next_diagonals(it, b):
                if not isinstance(it, int) or it < T - 1:
                    row_diagonals(it + 1, (b + 1) % 4)

            def less_m(it, b):
                pool.wait_ge(mB_ready, it + 1)
                pool.wait_ge(zc_leaky, it + 1)
                z = zc[b][:, :, :, :].rearrange("p c h i -> p c (h i)")
                nc.gpsimd.tensor_tensor(z, z, mB[b % 2][:, :].unsqueeze(1).to_broadcast([P, NC, H * P]),
                                        ALU.subtract).then_inc(zc_less, 1)

            def by_slots():
                row_diagonals(0, 0)
                rounds(pool, next_diagonals, less_m)
                pool.sem_inc(diag_ready, 48)

            choose(pool, 0, by_slots, over_all)
            rstd_of(1)
            rstd_of(2)
            rstd_of(3)
            pool.wait_ge(logits_ready, 2)
            n0 = 48
            for k in range(8):
                diagonal(diag3[k % 2], (c3, r3)[k // 4][:, 4 * (k % 4):4 * (k % 4) + 4], n0 + k)
            pool.wait_ge(bc_bank, n0 + 8)
            pool.wait_ge(bc_copied, n0 + 8)

            def over_all3():
                def z_step(jt, s=None):
                    for q in range(2):
                        if s is not None:
                            pool.wait_ge(lo_ready, 2 * s + q + 1)
                            if not isinstance(s, int):
                                apart(pool)
                        nc.gpsimd.tensor_tensor(zb[q][:, :, :],
                                                cB3[:, bass.ds(jt * P, P)].unsqueeze(1).to_broadcast([P, HT, P]),
                                                r3[:, HT * q:HT * q + HT].unsqueeze(2).to_broadcast([P, HT, P]),
                                                ALU.add).then_inc(z_ready, 1)

                def lo_step(s, jt, b):
                    for q in range(2):
                        pool.wait_ge(den_ready, 2 * s + q + 1)
                        qs = slice(HT * q, HT * q + HT)
                        nc.gpsimd.tensor_tensor(den_lo[b][:, qs, :], zb[q][:, :, :], den_hi[b][:, qs, :].bitcast(F32),
                                                ALU.subtract).then_inc(lo_ready, 1)
                    if isinstance(jt, int) and jt == T - 1:
                        if s == T - 1:
                            z_step(0, s)
                    else:
                        z_step(jt + 1, s)

                def att_step(s, jt, b, half):
                    for c in range(2):
                        pool.wait_ge(rec_ready, 2 * s + c + 1)
                        nc.gpsimd.tensor_tensor(mx[c][:, :], dT[c][:, :], mx[c][:, :], ALU.mult).then_inc(att_ready, 1)

                z_step(0)
                steps(pool, lo_step, att_step)

            def z3(it, b):
                pool.wait_ge(att3_ready, 4 * it + 4)
                if not isinstance(it, int):
                    apart(pool)
                nc.gpsimd.tensor_tensor(dTc[b][:, :, :], rB3[:, bass.ds(it * P, P)].unsqueeze(1).to_broadcast([P, T, P]),
                                        c3[:, :].unsqueeze(2).to_broadcast([P, T, P]), ALU.add).then_inc(z3_ready, 1)

            def att3(it, b, c):
                n = 4 * it + c
                if c == 0:
                    pool.wait_ge(dT3_ready, it + 1)
                pool.wait_ge(t_ready, n + 5)
                nc.gpsimd.tensor_tensor(yc[b][c][:, :], yc[b][c][:, :],
                                        dTc[b][:, 4 * c:4 * c + 4, :].rearrange("p j i -> p (j i)"),
                                        ALU.mult).then_inc(deny_ready, 1)
                pool.wait_ge(deny_ready, n + 1)
                pool.wait_ge(less2_ready, n + 1)
                nc.gpsimd.tensor_tensor(yc[b][c][:, :], yc[b][c][:, :], tc[c % 2][:, :], ALU.mult).then_inc(att3_ready, 1)

            def tile3(it, b):
                if within(it, 1):
                    z3(it + 1, 1 - b)
                att3(it, b, 0)
                att3(it, b, 1)
                att3(it, b, 2)
                att3(it, b, 3)

            def by_slots3():
                z3(0, 0)
                sweep(pool, tile3)

            choose(pool, 3, by_slots3, over_all3)

        @block.scalar
        def _(act):
            act.dma_start(W0[:, :], w0).then_inc(w_loaded, 16)
            act.dma_start(attB[:, :, :].rearrange("p h f -> p (h f)"),
                          att0.rearrange("h f -> (h f)").partition_broadcast(P)).then_inc(w_loaded, 16)
            act.dma_start(W2[:, :, :], w2.rearrange("k o c -> o k c")).then_inc(w_loaded, 16)
            act.dma_start(W3[:, :], w3).then_inc(w_loaded, 16)
            act.dma_start(a3B[:, :, :].rearrange("p k f -> p (k f)"),
                          a3.rearrange("o f -> (o f)").partition_broadcast(P)).then_inc(w_loaded, 16)

            def turn_h(dst, use):
                for q in range(4):
                    act.wait_ge(hT_banks, 4 * use + q + 1)
                    nc.scalar.copy(dst[:, q * BANK:(q + 1) * BANK], bank[q][:, :]).then_inc(hT_ready, 1)

            def convert(g, b):
                act.wait_ge(a_loaded[b], 16 * g + 16)
                nc.scalar.copy(A[:, bass.ds(2 * g + b, 1), :].rearrange("p o n -> p (o n)"), a32[b][:, :]).then_inc(a_ready, 1)

            for it in range(4):
                convert(it // 2, it % 2)
            turn_h(hT0, 0)
            with act.Fori(2, HT) as g:
                for b in range(2):
                    convert(g, b)

            def over_all():
                for n in range(16):
                    act.wait_ge(bc_bank, n + 1)
                    nc.scalar.copy(cB[n // 4][:, (n % 4) * BANK:(n % 4 + 1) * BANK], bank[4 + n % 2][:, :]).then_inc(bc_copied, 1)
                with act.Fori(0, 2) as g:
                    for e in range(2):
                        for half in range(2):
                            u = 4 * g + 2 * e + half
                            for k in range(4):
                                n = 16 + 4 * u + k
                                lo = HALF * half + BANK * (k % 2)
                                act.wait_ge(bc_bank, n + 1)
                                nc.scalar.copy((pmB, p2B)[k // 2][:, lo:lo + BANK], bank[4 + k % 2][:, :]).then_inc(bc_copied, 1)
                            act.wait_ge(bc_copied, 16 + 4 * u + 4)
                            act.wait_ge(cur_ready, 6 * g + 3 * e + 3)
                            hs = slice(HALF * half, HALF * half + HALF)
                            for jt in range(T):
                                act.wait_ge(uv_free, T * u + jt + 1)
                                nc.scalar.activation(ub[jt % 2][:, :], pmB[:, hs], ACT.Exp, bias=cc[e][:, jt:jt + 1]).then_inc(uv_ready, 1)
                                nc.scalar.activation(vb[jt % 2][:, :], p2B[:, hs], ACT.Exp, bias=cc2[e][:, jt:jt + 1]).then_inc(uv_ready, 1)
                            act.wait_ge(p_free, T * u + T + 2)
                            act.wait_ge(o_turned, u + 1)
                            nc.scalar.copy(oT[half][:, 0:BANK], bank[2 * half][0:F1, :])
                            nc.scalar.copy(oT[half][:, BANK:HALF], bank[2 * half + 1][0:F1, :]).then_inc(oT_ready, 1)

            def slot_logits(it, b):
                act.wait_ge(gathered, it + 3)
                act.wait_ge(pc_used, it + 1)
                nc.scalar.copy(wc[b][:, :, :].rearrange("p c w -> p (c w)"), bank[b % 2][:, 0:NC * WC]).then_inc(w_copied, 1)
                act.wait_ge(rows_bank, it + 3)
                act.wait_ge(zc_less, it + 1)
                nc.scalar.copy(mB[b % 2][:, :], bank[4 + 2 * (b % 2)][:, :]).then_inc(q_copied, 1)
                act.wait_ge(w_copied, it + 3)
                for c in range(NC):
                    for h in range(H):
                        last = nc.scalar.activation(zc[b][:, c, h, :], bank[4 + 2 * (b % 2)][:, P * h:P * h + P], ACT.Identity,
                                                    bias=wc[b][:, c, H * F1 + h:H * F1 + h + 1])
                last.then_inc(zc_ready, 1)

            def copy_output(it):
                act.wait_ge(pc_used, it + 5)
                if not isinstance(it, int):
                    apart(act)
                nc.scalar.copy(Oc[:, bass.ds(it, 1), :, :].rearrange("p o h f -> p (o h f)"),
                               bank[7][:, 0:H * F1]).then_inc(oc_copied, 1)

            def slot_exp(it, b):
                act.wait_ge(zc_less, it + 3)
                z = zc[b][:, :, :, :].rearrange("p c h i -> p (c h i)")
                nc.scalar.activation(z, z, ACT.Exp).then_inc(zc_exp, 1)
                if not isinstance(it, int) or it > 0:
                    copy_output(it - 1)

            def by_slots():
                rounds(act, slot_logits, slot_exp)
                copy_output(T - 1)
                act.sem_inc(bc_copied, 48)

            choose(act, 0, by_slots, over_all)

            def products(dst, number, columns, turned=None, projected=None):
                for q in range(NG):
                    act.wait_ge(acc_used, NG * number + q + 1)
                    with act.Fori(0, GT // 2) as g:
                        for b in range(2):
                            act.wait_ge(mm_bank, T * number + GT * q + 2 * g + b + 1)
                            nc.scalar.copy(dst[q % 2][:, bass.ds(2 * g + b, 1), 0:columns].rearrange("p o n -> p (o n)"),
                                           bank[b][:, 0:columns]).then_inc(mm_copied, 1)
                    if turned is not None and q >= 1:
                        turned(q - 1)
                    if turned is not None and q >= 2:
                        projected(q - 2)
                if turned is not None:
                    projected(NG - 2)
                    turned(NG - 1)
                    projected(NG - 1)

            def turned_group(dst, use):
                def run(q):
                    act.wait_ge(hT_banks, 4 * use + q + 1)
                    if q >= 2:
                        act.wait_ge(proj_banks, (4 + GT * (q - 1)) if use == 1 else (4 + T + q - 1))
                    nc.scalar.copy(dst[q % 2][:, :], bank[2 + q % 2][:, :]).then_inc(hT_ready, 1)
                return run

            def projected2(q):
                for t in range(GT * q, GT * q + GT):
                    act.wait_ge(proj_banks, 4 + t + 1)
                    nc.scalar.copy(ys[:, t, :], bank[4 + t % 4][:, 0:3 * D]).then_inc(proj_ready, 1)

            def projected3(q):
                act.wait_ge(proj_banks, 4 + T + q + 1)
                nc.scalar.copy(XW[:, GT * q:GT * q + GT, :].rearrange("p t f -> p (t f)"), bank[4 + q][:, :]).then_inc(proj_ready, 1)

            for q in range(NG):
                act.wait_ge(shift_ready, q + 1)
                for t in range(GT * q, GT * q + GT):
                    last = nc.scalar.activation(h1[:, t, :], X[:, t, :], ACT.Relu, scale=rstd[:, t:t + 1],
                                                bias=var[:, t:t + 1])
                last.then_inc(h1_ready, 1)
            products(accs, 0, PC, turned_group(hTs, 1), projected2)
            products(accs, 1, 3 * D)
            products(accs, 2, 3 * D, turned_group(hTs3, 2), projected3)
            for k in range(8):
                act.wait_ge(bc_bank, 48 + k + 1)
                nc.scalar.copy((cB3, rB3)[k // 4][:, (k % 4) * BANK:(k % 4 + 1) * BANK], bank[4 + k % 2][:, :]).then_inc(bc_copied, 1)
            act.wait_ge(bc_copied, 56)

            def over_all3():
                def den_step(s, jt, b):
                    act.wait_ge(num_bank, 2 * s + 2)
                    for q in range(2):
                        z = zb[q][:, :, :]
                        act.wait_ge(leaky_ready, 2 * s + q + 1)
                        nc.scalar.activation(z, z, ACT.Exp).then_inc(act_seq, 1)
                        act.wait_ge(act_seq, 2 * s + q + 1)
                        nc.scalar.copy(den_hi[b][:, HT * q:HT * q + HT, :], z).then_inc(den_ready, 1)

                def dT_step(s, jt, b, half):
                    for c in range(2):
                        act.wait_ge(att_ready, 2 * s + c + 1)
                        apart(act)
                        lo = HALF * half + BANK * c
                        nc.scalar.activation(dT[c][:, :], rB3[:, lo:lo + BANK], ACT.Exp, bias=c3[:, bass.ds(jt, 1)])
                        nc.scalar.activation(dv[c][:, :], rB3[:, lo:lo + BANK], ACT.Exp, bias=c3s[:, bass.ds(jt, 1)],
                                             scale=0.01).then_inc(dT_ready, 1)
                    act.wait_ge(att_free, s + 1)
                    nc.scalar.copy(xwc[b][:, :], XW[:, bass.ds(jt, 1), :].rearrange("p o f -> p (o f)")).then_inc(xw_cur, 1)

                steps(act, den_step, dT_step)
                for q in range(4):
                    act.wait_ge(u_bank, q + 1)
                    nc.scalar.copy(uT[:, q * BANK:(q + 1) * BANK], bank[4 + q][:, :]).then_inc(uT_ready, 1)
                for q in range(4):
                    act.wait_ge(u_turned, q + 1)
                    nc.scalar.copy(Un[:, 4 * q:4 * q + 4, :].rearrange("p t f -> p (t f)"), bank[q][:, :]).then_inc(un_ready, 1)

            def exp_er(it, b):
                act.wait_ge(e3_copied, it + 3)
                if within(it, -2):
                    act.wait_ge(denc_ready, 3 * it - 3)
                nc.scalar.activation(er[b][:, :], rc[b][:, :], ACT.Exp, scale=0.01).then_inc(er_ready, 1)

            def exp_u(it, b, c):
                act.wait_ge(e3_copied, it + 3)
                act.wait_ge(num3_bank, 4 * it + 4)
                nc.scalar.activation(denc[b][:, c, :], cB3[:, :], ACT.Exp, bias=rc[b][:, c:c + 1]).then_inc(u3_ready, 1)

            def exp_ln(it, b, c):
                n = 4 * it + c
                act.wait_ge(num3_bank, n + 9)
                act.wait_ge(att3_used, n + 1)
                nc.scalar.activation(yc[b][c][:, :], bank[c][:, :], ACT.Ln).then_inc(ln_ready, 1)
                act.wait_ge(ln_ready, n + 1)
                nc.scalar.activation(yc[b][c][:, :], yc[b][c][:, :], ACT.Exp, scale=-1.0).then_inc(y_ready, 1)

            def less2(it, c):
                act.wait_ge(t_ready, 4 * it + c + 5)
                nc.scalar.activation(tc[c % 2][:, :], tc[c % 2][:, :], ACT.Identity, bias=minus2[:, :]).then_inc(less2_ready, 1)

            def exp_dT(it, b):
                act.wait_ge(z3_leaky, it + 1)
                z = dTc[b][:, :, :].rearrange("p j i -> p (j i)")
                nc.scalar.activation(z, z, ACT.Exp).then_inc(dT3_ready, 1)

            def tile3(it, b):
                if within(it, 1):
                    exp_er(it + 1, 1 - b)
                for c in range(4):
                    if within(it, 1) and c < NC:
                        exp_u(it + 1, 1 - b, c)
                    if c == 0:
                        if within(it, -1):
                            less2(it - 1, 3)
                        exp_dT(it, b)
                    exp_ln(it, b, c)
                    if c > 0:
                        less2(it, c - 1)

            def by_slots3():
                nc.scalar.preload_act_table_set("natural_log_exp_and_others")
                nc.scalar.activation(E01[:, :], cB3[:, :], ACT.Exp, scale=0.01).then_inc(e01_ready, 1)
                exp_er(0, 0)
                for c in range(NC):
                    exp_u(0, 0, c)
                sweep(act, tile3)
                less2(T - 1, 3)

            choose(act, 3, by_slots3, over_all3)
            products(accs3, 3, 3 * D)

        @block.tensor
        def _(pe):
            def turn_h(src, layer, use):
                for t in range(T):
                    pe.wait_ge(h_ready, NG * layer + t // GT + 1)
                    last = nc.tensor.transpose(bank[t // 4][:, P * (t % 4):P * (t % 4) + P], src[:, t, :], ident[:, :])
                    if t % 4 == 3:
                        last.then_inc(hT_banks, 1)

            def broadcast(dg, n, b):
                pe.wait_ge(diag_ready, n + 1)
                if not isinstance(n, int) or n >= 2:
                    pe.wait_ge(bc_copied, n - 1)
                nc.tensor.matmul(bank[4 + b][:, :], ones[:, :], dg[b][:, :], start=True, stop=True).then_inc(bc_bank, 1)

            pe.wait_ge(const_ready, 7)
            turn_h(h0, 0, 0)
            pe.wait_ge(w_loaded, 80)
            for k in range(3):
                last = nc.tensor.transpose(bank[6][:, P * k:P * k + P], W2[:, k, :], ident[:, :])
            last.then_inc(w2T_banks, 1)
            pe.wait_ge(w2_ready, 1)
            for t in range(T):
                pe.wait_ge(hT_ready, t // 4 + 1)
                last = nc.tensor.matmul(bank[4 + t // 4][:, P * (t % 4):P * (t % 4) + P], hT0[:, P * t:P * t + P],
                                        W0[:, :], start=True, stop=True)
                if t % 4 == 3:
                    last.then_inc(proj_banks, 1)
            pe.wait_ge(proj_ready, 4)
            for t in range(T):
                last = nc.tensor.matmul(bank[7][:, 0:H * F1], ones[:, :], WH[:, t, :, :].rearrange("p h f -> p (h f)"),
                                        start=t == 0, stop=t == T - 1)
            last.then_inc(wsum_bank, 1)
            pe.wait_ge(ext_ready, 1)
            nc.tensor.matmul(bank[5][0:2 * H, 0:P], ext[:, :], ident[:, :], start=True, stop=True).then_inc(ext_bank, 1)
            pe.wait_ge(ext_ready, 2)
            nc.tensor.matmul(bank[5][:, 0:2 * H], ones[0:2 * H, :], exd[:, :], start=True, stop=True).then_inc(ext_bank, 1)

            pe.wait_ge(hT_ready, 4)
            pe.wait_ge(wsum_ready, 1)
            with pe.Fori(0, HT) as g:
                for b in range(2):
                    it = 2 * g + b
                    pe.wait_ge(a_ready, it + 1)
                    for grp in range(2):
                        pe.wait_ge(at_copied, 2 * it + grp + 1)
                        for k in range(8):
                            jt = 8 * grp + k
                            last = nc.tensor.transpose(
                                bankb[2 * b + grp][:, P * k:P * k + P],
                                A[:, bass.ds(it, 1), P * jt:P * jt + P].rearrange("p o n -> p (o n)"), identb[:, :])
                        last.then_inc(at_bank, 1)
                    pe.wait_ge(some_ready, it + 1)
                    for jt in range(T):
                        last = nc.tensor.matmul(bank[6 + b][:, jt:jt + 1],
                                                A[:, bass.ds(it, 1), P * jt:P * jt + P].rearrange("p o n -> p (o n)"),
                                                onesb[:, 0:1], start=True, stop=True)
                    last.then_inc(edge_bank, 1)
            pe.wait_ge(pieces0_ready, 1)
            pe.wait_ge(guard_ready, 1)
            nc.tensor.matmul(bank[5][:, 0:P], onesb[:, :], tri[:, :], start=True, stop=True).then_inc(rank_bank, 1)
            pe.wait_ge(some_ready, T + 2)
            someF = some[:, :, :].rearrange("p i j -> p (i j)")
            ranks = bank[4][:, 0:T * T].rearrange("p (i j) -> p i j", j=T)
            nc.tensor.matmul(bank[4][:, 0:T * T], tri[:, :], someF, start=True, stop=False)
            for first, end in CHUNKS:
                for jt in range(first, end - 1):
                    nc.tensor.matmul(ranks[:, :, jt + 1:end], onesb[:, :],
                                     some[:, :, jt:jt + 1].to_broadcast([P, T, end - 1 - jt]), start=False, stop=False)
            nc.tensor.matmul(bank[4][:, 0:T * T], zeros[:, :], someF, start=False, stop=True).then_inc(rank_bank, 1)
            pe.wait_ge(over_ready, 1)
            nc.tensor.matmul(bank[5][:, 0:1], ones[:, :], over[:, :], start=True, stop=True).then_inc(over_bank, 1)

            pe.wait_ge(at_copied, 2 * T + 4)

            def over_all():
                for n in range(16):
                    broadcast(diag, n, n % 2)
                with pe.Fori(0, 2) as g:
                    for e in range(2):
                        for half in range(2):
                            u = 4 * g + 2 * e + half
                            for k in range(4):
                                broadcast(diag, 16 + 4 * u + k, k % 2)
                            pe.wait_ge(cur_ready, 6 * g + 3 * e + 3)
                            pe.wait_ge(oT_ready, u + 3)
                            for jt in range(T):
                                pe.wait_ge(p_ready, T * u + jt + 1)
                                for c in range(2):
                                    last = nc.tensor.matmul(bank[2 * half + c][0:F1, :], whc[e][:, jt, :],
                                                            pb[jt % 2][:, BANK * c:BANK * c + BANK],
                                                            start=jt == 0, stop=jt == T - 1)
                                last.then_inc(p_free, 1)
                            pe.wait_ge(oT_ready, u + 5)
                            pe.wait_ge(o_kept, u + 1)
                            for t in range(HT):
                                last = nc.tensor.matmul(bank[6 + half][:, F1 * t:F1 * t + F1], oT[half][:, P * t:P * t + P],
                                                        ident[0:F1, 0:F1], start=True, stop=True)
                            last.then_inc(o_turned, 1)

            def gather(it, b):
                pe.wait_ge(g_ready, it + 1)
                pe.wait_ge(w_copied, it + 1)
                pe.wait_ge(e_copied, it + 1)
                for c, (first, end) in enumerate(CHUNKS):
                    for jt in range(first, end):
                        for k in range(3):
                            nc.tensor.matmul(bank[b % 2][:, WC * c:WC * c + WC], G[b % 2][:, jt, :], whp[:, jt, k, :],
                                             start=jt == first and k == 0, stop=jt == end - 1 and k == 2)
                        last = nc.tensor.matmul(bank[2 + b % 2][:, P * c:P * c + P], G[b % 2][:, jt, :],
                                                AT[:, jt, bass.ds(it * P, P)], start=jt == first, stop=jt == end - 1)
                last.then_inc(gathered, 1)

            def broadcast_rows(it, b):
                pe.wait_ge(rows_ready, it + 1)
                pe.wait_ge(zc_ready, it + 1)
                nc.tensor.matmul(bank[4 + 2 * (b % 2)][:, :], ones[:, :], rows[b % 2][:, :, :].rearrange("p h i -> p (h i)"),
                                 start=True, stop=True).then_inc(rows_bank, 1)

            def prepare(it, b):
                if not isinstance(it, int) or it < T - 1:
                    broadcast_rows(it + 1, (b + 1) % 4)
                    gather(it + 1, (b + 1) % 4)

            def slot_output(it, b):
                pe.wait_ge(pc_ready, it + 5)
                pe.wait_ge(w_copied, it + 3)
                if not isinstance(it, int) or it > 0:
                    pe.wait_ge(oc_copied, it)
                for h in range(H):
                    for c in range(NC):
                        last = nc.tensor.matmul(bank[7][:, F1 * h:F1 * h + F1], zc[b][:, c, h, :],
                                                wc[b][:, c, F1 * h:F1 * h + F1], start=c == 0, stop=c == NC - 1)
                last.then_inc(pc_used, 1)

            def by_slots():
                pe.wait_ge(pieces0_ready, 17)
                broadcast_rows(0, 0)
                gather(0, 0)
                rounds(pe, prepare, slot_output)
                pe.sem_inc(bc_bank, 48)

            choose(pe, 0, by_slots, over_all)

            def product(adjacency, pieces, number, columns, turn=None, project=None):
                pe.wait_ge(pieces_ready, NG * number + NG)
                for q in range(NG):
                    with pe.Fori(0, GT // 2) as g:
                        for b in range(2):
                            pe.wait_ge(mm_copied, T * number + GT * q + 2 * g + b + 1)
                            for kt in range(T):
                                last = nc.tensor.matmul(bank[b][:, 0:columns],
                                                        adjacency[:, kt, bass.ds((GT * q + 2 * g + b) * P, P)],
                                                        pieces[:, kt, 0:columns], start=kt == 0, stop=kt == T - 1)
                            last.then_inc(mm_bank, 1)
                    if turn is not None and q >= 1:
                        turn(q - 1)
                    if turn is not None and q >= 2:
                        project(q - 2)
                if turn is not None:
                    project(NG - 2)
                    turn(NG - 1)
                    project(NG - 1)

            def turn_group(layer, use):
                def run(q):
                    pe.wait_ge(h_ready, NG * layer + q + 1)
                    if q >= 2:
                        pe.wait_ge(hT_ready, 4 * use + q - 1)
                    for k in range(GT):
                        last = nc.tensor.transpose(bank[2 + q % 2][:, P * k:P * k + P], h1[:, GT * q + k, :], ident[:, :])
                    last.then_inc(hT_banks, 1)
                return run

            def project2(q):
                pe.wait_ge(hT_ready, 4 + q + 1)
                for t in range(GT * q, GT * q + GT):
                    if t >= 4:
                        pe.wait_ge(proj_ready, 4 + t - 3)
                    k = t % GT
                    nc.tensor.matmul(bank[4 + t % 4][:, 0:3 * D], hTs[q % 2][:, P * k:P * k + P],
                                     W2[:, :, :].rearrange("p k o -> p (k o)"), start=True, stop=True).then_inc(proj_banks, 1)

            def project3(q):
                pe.wait_ge(hT_ready, 8 + q + 1)
                for k in range(GT):
                    last = nc.tensor.matmul(bank[4 + q][:, P * k:P * k + P], hTs3[q % 2][:, P * k:P * k + P],
                                            W3[:, :], start=True, stop=True)
                last.then_inc(proj_banks, 1)

            product(A, pcs, 0, PC, turn_group(2, 1), project2)
            product(AT, pcs2, 1, 3 * D)
            pe.wait_ge(proj_ready, 4 + T)
            product(AT, pcs, 2, 3 * D, turn_group(3, 2), project3)
            pe.wait_ge(proj_ready, 8 + T)
            pe.wait_ge(over_ready, 2)
            nc.tensor.matmul(bank[7][:, 0:1], ones[:, :], over3[:, :], start=True, stop=True).then_inc(over_bank, 1)
            for k in range(8):
                broadcast(diag3, 48 + k, k % 2)
            pe.wait_ge(bc_copied, 56)

            def over_all3():
                for c in range(4):
                    last = nc.tensor.matmul(bank[4 + c][:, :], zeros[:, :], zeros[:, 0:1].to_broadcast([P, BANK]),
                                            start=True, stop=False)

                def num_step(s, jt, b):
                    pe.wait_ge(lo_ready, 2 * s + 2)
                    pe.wait_ge(num_free, 2 * s + 2)
                    for kt in range(T):
                        if isinstance(s, int) and s % T == 0:
                            pe.wait_ge(atr_ready, s + kt + 1)
                        for part, den in enumerate((den_hi, den_lo)):
                            for c in range(2):
                                last = nc.tensor.matmul(bank[2 * b + c][:, :], den[b][:, kt, :],
                                                        ATr[:, kt, BANK * c:BANK * c + BANK],
                                                        start=kt == 0 and part == 0, stop=kt == T - 1 and part == 1)
                                if kt == T - 1 and part == 1:
                                    last.then_inc(num_bank, 1)

                def u_step(s, jt, b, half):
                    pe.wait_ge(xw_cur, s + 1)
                    for c in range(2):
                        pe.wait_ge(att_ready, 2 * s + c + 3)
                        last = nc.tensor.matmul(bank[4 + 2 * half + c][:, :], xwc[b][:, :], mx[c][:, :], start=False,
                                                stop=False)
                    last.then_inc(att_free, 1)

                steps(pe, num_step, u_step)
                for c in range(4):
                    nc.tensor.matmul(bank[4 + c][:, :], zeros[:, :], zeros[:, 0:1].to_broadcast([P, BANK]),
                                     start=False, stop=True).then_inc(u_bank, 1)
                pe.wait_ge(num_free, 4 * T + 4)
                for t in range(T):
                    pe.wait_ge(uT_ready, t // 4 + 1)
                    last = nc.tensor.transpose(bank[t // 4][:, P * (t % 4):P * (t % 4) + P], uT[:, P * t:P * t + P],
                                               ident[:, :])
                    if t % 4 == 3:
                        last.then_inc(u_turned, 1)

            def gather3(it, b):
                pe.wait_ge(g3_ready, it + 1)
                pe.wait_ge(e3_copied, it + 1)
                for c, (first, end) in enumerate(CHUNKS):
                    for jt in range(first, end):
                        nc.tensor.matmul(bank[4 + b][:, P * c:P * c + P], G3[b][:, jt, :],
                                         AT[:, jt, bass.ds(it * P, P)], start=jt == first, stop=jt == end - 1 and c > 0)
                    if c == 0:
                        nc.tensor.matmul(bank[4 + b][:, 0:P], Eb[:, bass.ds(it, 1), :].rearrange("p o s -> p (o s)"),
                                         identb[:, :], start=False, stop=True)
                    for jt in range(first, end):
                        last = nc.tensor.matmul(bank[4 + b][:, P * NC + 3 * c:P * NC + 3 * c + 3], G3[b][:, jt, :],
                                                rp[:, jt, :], start=jt == first, stop=jt == end - 1)
                last.then_inc(g3_used, 1)

            def num3(it, b, c):
                pe.wait_ge(denc_ready, 3 * it + 3)
                pe.wait_ge(t_ready, 4 * it + c + 1)
                for k in range(4):
                    j0 = P * (4 * c + k)
                    for part in range(NC):
                        last = nc.tensor.matmul(bank[c][:, P * k:P * k + P], denc[b][:, part, j0:j0 + P],
                                                ATc3[b][:, part, :], start=part == 0, stop=part == NC - 1)
                last.then_inc(num3_bank, 1)

            def u3(it, b, c):
                pe.wait_ge(att3_ready, 4 * it + c + 9)
                if c == 0:
                    pe.wait_ge(un3_kept, it + 1)
                for k in range(4):
                    last = nc.tensor.matmul(bank[6 + b][:, 0:D], yc[b][c][:, P * k:P * k + P], XW[:, 4 * c + k, :],
                                            start=c == 0 and k == 0, stop=c == 3 and k == 3)
                last.then_inc(att3_used, 1)

            def tile3(it, b):
                for c in range(4):
                    num3(it, b, c)
                    if within(it, -1):
                        u3(it - 1, 1 - b, c)
                if within(it, 2):
                    gather3(it + 2, b)

            def by_slots3():
                pe.wait_ge(rp_ready, 5)
                gather3(0, 0)
                gather3(1, 1)
                sweep(pe, tile3)
                for c in range(4):
                    u3(T - 1, 1, c)

            choose(pe, 3, by_slots3, over_all3)
            product(AT, pcs3, 3, 3 * D)

        @block.vector
        def _(dve):
            done = [0]

            def then(instruction):
                done[0] += 1
                instruction.then_inc(vec, 1)
                dve.wait_ge(vec, done[0])

            def counted(by_slots, over_all):
                before, after = done[0], []

                def run(part):
                    done[0] = before
                    part()
                    after.append(done[0])
                    if done[0] < after[0]:
                        dve.sem_inc(vec, after[0] - done[0])
                    done[0] = after[0]

                return lambda: run(by_slots), lambda: run(over_all)

            def group(q):
                return slice(GT * q, GT * q + GT)

            def moments(q):
                for t in range(GT * q, GT * q + GT):
                    last = nc.vector.bn_stats(stats[:, t, :], X[:, t, :])
                then(last)
                for t in range(GT * q, GT * q + GT):
                    last = nc.vector.bn_aggr(mv[:, t, :], stats[:, t, :])
                then(last)
                nc.vector.tensor_scalar(var[:, group(q)], mv[:, group(q), 1:2].rearrange("p t o -> p (t o)"), EPS, None,
                                        ALU.add).then_inc(var_ready, 1)

            def normal(layer, q, dst):
                dve.wait_ge(rstd_ready, NG * layer + q + 1)
                for t in range(GT * q, GT * q + GT):
                    last = nc.vector.tensor_scalar(dst[:, t, :], X[:, t, :], mv[:, t, 0:1], rstd[:, t:t + 1],
                                                   ALU.subtract, ALU.mult)
                then(last)
                then(nc.vector.tensor_scalar(dst[:, group(q), :], dst[:, group(q), :], 0.0, None, ALU.max))
                dve.sem_inc(h_ready, 1)

            def split(src, dst, q, tmp):
                d = dst[:, group(q), :]
                then(nc.vector.tensor_copy(d[:, :, 0:D], src))
                then(nc.vector.tensor_tensor(tmp[:, :, :], src, d[:, :, 0:D], ALU.subtract))
                then(nc.vector.tensor_copy(d[:, :, D:2 * D], tmp[:, :, :]))
                then(nc.vector.tensor_tensor(d[:, :, 2 * D:3 * D], tmp[:, :, :], d[:, :, D:2 * D], ALU.subtract))
                dve.sem_inc(pieces_ready, 1)

            def join(src, number, q, dst):
                a = src[q % 2]
                then(nc.vector.tensor_tensor(dst[:, :, :], a[:, :, 2 * D:3 * D], a[:, :, D:2 * D], ALU.add))
                then(nc.vector.tensor_tensor(dst[:, :, :], dst[:, :, :], a[:, :, 0:D], ALU.add))
                dve.sem_inc(acc_used, 1)

            dve.wait_ge(x_loaded, 16)
            for q in range(NG):
                moments(q)
            for q in range(NG):
                normal(0, q, h0)
            dve.wait_ge(w2T_banks, 1)
            then(nc.vector.tensor_copy(W2[:, :, :].rearrange("p k o -> p (k o)"), bank[6][:, 0:3 * D]))
            nc.vector.tensor_tensor(W2[:, 0, :], W2[:, 0, :], W2[:, 2, :], ALU.subtract).then_inc(w2_ready, 1)
            for q in range(4):
                dve.wait_ge(proj_banks, q + 1)
                nc.vector.tensor_copy(WH[:, 4 * q:4 * q + 4, :, 0:F],
                                      bank[4 + q][:, :].rearrange("p (t h f) -> p t h f", t=4, h=H)).then_inc(proj_ready, 1)
            dve.wait_ge(proj_ready, 4)
            pr = h0[:, :, :].rearrange("p t (h f) -> p t h f", h=H)
            for k, col in enumerate((pcol, ccol)):
                then(nc.vector.tensor_tensor(pr, WH[:, :, :, 0:F],
                                             attB[:, :, F * k:F * k + F].unsqueeze(1).to_broadcast([P, T, H, F]), ALU.mult))
                then(nc.vector.tensor_reduce(col[:, :, :], pr, AX_X, ALU.add))
            then(nc.vector.tensor_copy(c1col[:, :, :].rearrange("p h t -> p t h"), ccol[:, :, :]))
            dve.sem_inc(logits_ready, 1)
            dve.wait_ge(wsum_bank, 1)
            nc.vector.tensor_copy(wsum[:, :, :].rearrange("p h f -> p (h f)"), bank[7][:, 0:H * F1]).then_inc(wsum_ready, 1)
            then(nc.vector.tensor_reduce(ext[:, 0:H], c1col[:, :, :], AX_X, ALU.max))
            then(nc.vector.tensor_reduce(ext[:, H:2 * H], c1col[:, :, :], AX_X, ALU.min))
            nc.vector.tensor_scalar(ext[:, H:2 * H], ext[:, H:2 * H], -1.0, None, ALU.mult).then_inc(ext_ready, 1)
            dve.wait_ge(ext_bank, 1)
            then(nc.vector.tensor_reduce(exm[:, :], bank[5][0:2 * H, 0:P], AX_X, ALU.max))
            nc.vector.tensor_scalar(exd[:, :], ident[0:2 * H, 0:2 * H], exm[:, 0:1], None, ALU.mult).then_inc(ext_ready, 1)
            dve.wait_ge(ext_bank, 2)
            then(nc.vector.tensor_copy(ctop[:, :], bank[5][:, 0:H]))
            then(nc.vector.tensor_scalar(cmin[:, :], bank[5][:, H:2 * H], -1.0, None, ALU.mult))
            then(nc.vector.tensor_tensor(spread[:, 0:H], ctop[:, :], cmin[:, :], ALU.subtract))
            then(nc.vector.tensor_reduce(spread[:, H:H + 1], spread[:, 0:H], AX_X, ALU.max))
            then(nc.vector.tensor_scalar(spread[:, H:H + 1], spread[:, H:H + 1], 60.0, None, ALU.is_gt))

            def leaky_sum(c):
                then(nc.vector.tensor_tensor(cmax[:, :, :], pcol[:, :, :], c, ALU.add))
                then(nc.vector.tensor_scalar(tcol[:, :, :], cmax[:, :, :], 0.2, None, ALU.mult))
                then(nc.vector.tensor_tensor(mcol[:, :, :], cmax[:, :, :], tcol[:, :, :], ALU.max))

            Cs = ctop[:, :].unsqueeze(1).to_broadcast([P, T, H])
            then(nc.vector.tensor_tensor(qcol[:, :, :], pcol[:, :, :], Cs, ALU.add))
            then(nc.vector.tensor_tensor(WX[:, :, H * F1:WC], ccol[:, :, :], Cs, ALU.subtract))
            dve.sem_inc(guard_ready, 1)

            for it in range(T):
                for grp in range(2):
                    dve.wait_ge(at_bank, 2 * it + grp + 1)
                    nc.vector.tensor_copy(AT[:, 8 * grp:8 * grp + 8, P * it:P * it + P],
                                          bankb[2 * (it % 2) + grp][:, :].rearrange("p (j i) -> p j i", j=8)
                                          ).then_inc(at_copied, 1)
                dve.wait_ge(edge_bank, it + 1)
                nc.vector.tensor_scalar(some[:, it, :], bank[6 + it % 2][:, 0:T], 0.0, None,
                                        ALU.is_gt).then_inc(some_ready, 1)

            dve.wait_ge(rank_bank, 1)
            nc.vector.tensor_copy(iota[:, :], bank[5][:, 0:P]).then_inc(iota_ready, 1)
            dve.wait_ge(iota_ready, 1)
            dve.wait_ge(rank_bank, 2)
            then(nc.vector.tensor_tensor(slots[:, :, :], bank[4][:, 0:T * T].rearrange("p (i j) -> p i j", j=T),
                                         some[:, :, :], ALU.mult))
            then(nc.vector.tensor_reduce(over[:, :], slots[:, :, :].rearrange("p i j -> p (i j)"), AX_X, ALU.max))
            then(nc.vector.tensor_scalar(over[:, :], over[:, :], float(P - 1), None, ALU.is_gt))
            then(nc.vector.tensor_tensor(over[:, :], over[:, :], spread[:, H:H + 1], ALU.max))
            dve.sem_inc(over_ready, 1)
            nc.vector.tensor_copy(slotb[:, :, :], slots[:, :, :]).then_inc(choice, 1)
            dve.wait_ge(over_bank, 1)
            nc.vector.tensor_scalar(dense[:, :], bank[5][:, 0:1], 0.0, None, ALU.is_gt).then_inc(choice, 1)

            def finish(o):
                Ow, Osw = (t[:, :, :, :].rearrange("p t h f -> p t (h f)") for t in (o, Os))
                then(nc.vector.tensor_scalar(tcol[:, :, :].unsqueeze(3), o[:, :, :, F:F1], 0.0, None, ALU.is_equal))
                then(nc.vector.tensor_scalar(mk[:, :], tcol[:, :, 0:1].rearrange("p t o -> p (t o)"), 1.0, None,
                                             ALU.subtract))
                then(nc.vector.tensor_tensor(Os[:, :, :, :], tcol[:, :, :].unsqueeze(3).to_broadcast([P, T, H, F1]),
                                             wsum[:, :, :].unsqueeze(1).to_broadcast([P, T, H, F1]), ALU.mult))
                then(nc.vector.tensor_tensor(Ow, Ow, Osw, ALU.add))
                then(nc.vector.reciprocal(tcol[:, :, :].unsqueeze(3), o[:, :, :, F:F1]))
                then(nc.vector.tensor_tensor(o[:, :, :, 0:F], o[:, :, :, 0:F],
                                             tcol[:, :, :].unsqueeze(3).to_broadcast([P, T, H, F]), ALU.mult))
                X4 = X[:, :, :].rearrange("p t (h f) -> p t h f", h=H)
                then(nc.vector.tensor_tensor(X4, X4, o[:, :, :, 0:F], ALU.add))

            def over_all():
                then(nc.vector.tensor_scalar(cmin[:, :], cmin[:, :], 1.0, None, ALU.subtract))
                for h in range(H):
                    dve.wait_ge(bc_copied, 4 * h + 4)
                    then(nc.vector.tensor_scalar(cB[h][:, :], cB[h][:, :], cmin[:, h:h + 1], None, ALU.subtract))
                for it in range(T):
                    for h in range(H):
                        then(nc.vector.tensor_tensor_reduce(out=junk[:, :], in0=A[:, it, :], in1=cB[h][:, :], scale=1.0,
                                                            scalar=0.0, op0=ALU.mult, op1=ALU.max,
                                                            accum_out=cmax[:, it, h:h + 1]))
                then(nc.vector.tensor_tensor(cmax[:, :, :], cmax[:, :, :],
                                             cmin[:, :].unsqueeze(1).to_broadcast([P, T, H]), ALU.add))
                leaky_sum(cmax[:, :, :])
                dve.wait_ge(pieces0_ready, 17)
                nc.vector.tensor_scalar(p2col[:, :, :].rearrange("p h t -> p t h"), pcol[:, :, :], 0.2, None,
                                        ALU.mult).then_inc(guard_ready, 1)
                nc.vector.tensor_tensor(pmcol[:, :, :].rearrange("p h t -> p t h"), pcol[:, :, :], mcol[:, :, :],
                                        ALU.subtract).then_inc(guard_ready, 1)
                nc.vector.tensor_scalar(c2col[:, :, :], c1col[:, :, :], 0.2, None, ALU.mult).then_inc(guard_ready, 1)
                dve.wait_ge(guard_ready, 4)
                nc.vector.tensor_tensor(p2col[:, :, :].rearrange("p h t -> p t h"),
                                        p2col[:, :, :].rearrange("p h t -> p t h"), mcol[:, :, :],
                                        ALU.subtract).then_inc(guard_ready, 1)
                dve.wait_ge(at_copied, 2 * T + 4)
                with dve.Fori(0, 2) as g:
                    for e in range(2):
                        for half in range(2):
                            u = 4 * g + 2 * e + half
                            for jt in range(T):
                                n = T * u + jt
                                b = jt % 2
                                dve.wait_ge(uv_ready, 2 * n + 2)
                                nc.vector.tensor_tensor(ub[b][:, :], ub[b][:, :], vb[b][:, :], ALU.max).then_inc(pmax, 1)
                                dve.wait_ge(pmax, n + 1)
                                dve.wait_ge(p_free, n + 1)
                                nc.vector.tensor_tensor(pb[b][:, :], ub[b][:, :], AT[:, jt, HALF * half:HALF * half + HALF],
                                                        ALU.min).then_inc(p_ready, 1)
                                dve.wait_ge(p_ready, n + 1)
                                dve.sem_inc(uv_free, 1)
                            dve.wait_ge(o_turned, u + 3)
                            nc.vector.tensor_copy(O[:, HT * half:HT * half + HT, bass.ds(2 * g + e, 1), :].rearrange("p t o f -> p t (o f)"),
                                                  bank[6 + half][:, 0:HT * F1].rearrange("p (t f) -> p t f", f=F1)
                                                  ).then_inc(o_kept, 1)
                dve.wait_ge(o_kept, 8 + 2)
                finish(O)

            def one_hot(it, b):
                dve.wait_ge(gathered, it + 1)
                if not isinstance(it, int):
                    apart(dve)
                nc.vector.tensor_tensor(G[b % 2][:, :, :], iota[:, :].unsqueeze(1).to_broadcast([P, T, P]),
                                        slotb[:, bass.ds(it, 1), :].rearrange("p o j -> p (o j)").unsqueeze(2)
                                        .to_broadcast([P, T, P]), ALU.is_equal).then_inc(g_ready, 1)

            def edges_and_leaky(it, b):
                if not isinstance(it, int) or it < T - 1:
                    one_hot(it + 1, (b + 1) % 4)
                dve.wait_ge(gathered, it + 3)
                dve.wait_ge(pc_ready, it + 3)
                nc.vector.tensor_copy(ATc[b % 2][:, :, :].rearrange("p c i -> p (c i)"),
                                      bank[2 + b % 2][:, 0:NC * P]).then_inc(e_copied, 1)
                dve.wait_ge(q_copied, it + 1)
                m = mB[b % 2][:, :]
                nc.vector.scalar_tensor_tensor(m, m, 0.2, m, ALU.mult, ALU.max).then_inc(mB_ready, 1)
                dve.wait_ge(zc_ready, it + 3)
                z = zc[b][:, :, :, :].rearrange("p c h i -> p (c h i)")
                nc.vector.scalar_tensor_tensor(z, z, 0.2, z, ALU.mult, ALU.max).then_inc(zc_leaky, 1)

            def mask(it, b):
                dve.wait_ge(zc_exp, it + 1)
                dve.wait_ge(e_copied, it + 3)
                nc.vector.tensor_tensor(zc[b][:, :, :, :], zc[b][:, :, :, :],
                                        ATc[b % 2][:, :, :].unsqueeze(2).to_broadcast([P, NC, H, P]),
                                        ALU.min).then_inc(pc_ready, 1)

            def by_slots():
                one_hot(0, 0)
                rounds(dve, edges_and_leaky, mask)
                dve.wait_ge(oc_copied, T)
                finish(Oc)

            choose(dve, 0, *counted(by_slots, over_all))

            for q in range(NG):
                moments(q)
            then(nc.vector.memset(pcs[:, :, 3 * D:PW], 1.0))
            for q in range(NG):
                dve.wait_ge(rstd_ready, NG + q + 1)
                nc.vector.scalar_tensor_tensor(var[:, group(q)].unsqueeze(2), mv[:, group(q), 0:1], -1.0,
                                               rstd[:, group(q)].unsqueeze(2), ALU.mult, ALU.mult).then_inc(shift_ready, 1)
                dve.sem_inc(h_ready, 1)
            for q in range(NG):
                dve.wait_ge(h1_ready, q + 1)
                split(h1[:, group(q), :], pcs, q, rest)

            def layer1(q):
                dve.wait_ge(mm_copied, GT * q + GT + 2)
                gq = group(q)
                dg = accs[q % 2][:, :, 3 * D:PC].rearrange("p t o -> p (t o)")
                then(nc.vector.tensor_scalar(inv[:, gq], dg, 0.0, None, ALU.is_equal))
                then(nc.vector.tensor_tensor(deg[:, gq], dg, inv[:, gq], ALU.add))
                then(nc.vector.reciprocal(deg[:, gq], deg[:, gq]))
                then(nc.vector.tensor_scalar(inv[:, gq], dg, 0.0, None, ALU.not_equal))
                then(nc.vector.tensor_tensor(inv[:, gq], inv[:, gq], deg[:, gq], ALU.mult))
                join(accs, 0, q, sg)
                then(nc.vector.tensor_tensor(sg[:, :, :], sg[:, :, :], inv[:, gq].unsqueeze(2).to_broadcast([P, GT, D]),
                                             ALU.mult))
                then(nc.vector.tensor_tensor(X[:, gq, :], X[:, gq, :], sg[:, :, :], ALU.add))
                moments(q)
                normal(2, q, h1)

            def first_pieces(q):
                dve.wait_ge(proj_ready, 4 + GT * q + GT)
                split(ys[:, group(q), 2 * D:3 * D], pcs2, q, rest)

            for q in range(NG):
                layer1(q)
                if q >= 2:
                    first_pieces(q - 2)
            for q in range(NG - 2, NG):
                first_pieces(q)
            for q in range(NG):
                dve.wait_ge(mm_copied, T + GT * q + GT + 2)
                join(accs, 1, q, sg)
                then(nc.vector.scalar_tensor_tensor(sg[:, :, :], sg[:, :, :], 2.0, ys[:, group(q), D:2 * D], ALU.mult,
                                                    ALU.add))
                split(sg[:, :, :], pcs, q, rest)

            def layer2(q):
                dve.wait_ge(mm_copied, 2 * T + GT * q + GT + 2)
                join(accs, 2, q, sg3)
                then(nc.vector.tensor_tensor(sg3[:, :, :], sg3[:, :, :], ys[:, group(q), 0:D], ALU.add))
                then(nc.vector.tensor_tensor(X[:, group(q), :], X[:, group(q), :], sg3[:, :, :], ALU.add))
                moments(q)
                normal(3, q, h1)

            def logits3(q):
                dve.wait_ge(proj_ready, 4 + T + q + 1)
                for k, col in enumerate((c3, r3)):
                    then(nc.vector.tensor_tensor(pr3[:, :, :], XW[:, group(q), :],
                                                 a3B[:, k:k + 1, :].to_broadcast([P, GT, D]), ALU.mult))
                    then(nc.vector.tensor_reduce(col[:, group(q)], pr3[:, :, :], AX_X, ALU.add))

            for q in range(NG):
                layer2(q)
                if q >= 2:
                    logits3(q - 2)
            for q in range(NG - 2, NG):
                logits3(q)
            nc.vector.tensor_scalar(c3s[:, :], c3[:, :], 0.01, None, ALU.mult).then_inc(logits_ready, 1)
            then(nc.vector.tensor_tensor(inv[:, :], c3[:, :], c3[:, :], ALU.mult))
            then(nc.vector.tensor_tensor(deg[:, :], r3[:, :], r3[:, :], ALU.mult))
            then(nc.vector.tensor_tensor(inv[:, :], inv[:, :], deg[:, :], ALU.max))
            then(nc.vector.tensor_reduce(over3[:, :], inv[:, :], AX_X, ALU.max))
            then(nc.vector.tensor_scalar(over3[:, :], over3[:, :], 100.0, None, ALU.is_gt))
            nc.vector.tensor_tensor(over3[:, :], over3[:, :], over[:, :], ALU.max).then_inc(over_ready, 1)
            dve.wait_ge(over_bank, 2)
            nc.vector.tensor_scalar(dense3[:, :], bank[7][:, 0:1], 0.0, None, ALU.is_gt).then_inc(choice, 1)

            def over_all3():
                def narrow(half, tiles):
                    for kt in tiles:
                        nc.vector.tensor_copy(ATr[:, kt, :], AT[:, kt, HALF * half:HALF * half + HALF]).then_inc(atr_ready, 1)

                narrow(0, range(T))

                def leaky_step(s, jt, b):
                    for q in range(2):
                        dve.wait_ge(z_ready, 2 * s + q + 1)
                        nc.vector.scalar_tensor_tensor(zb[q][:, :, :], zb[q][:, :, :], 0.01, zb[q][:, :, :], ALU.mult,
                                                       ALU.max).then_inc(leaky_ready, 1)

                def rec_step(s, jt, b, half):
                    dve.wait_ge(att_free, s + 2)
                    for c in range(2):
                        dve.wait_ge(num_bank, 2 * s + c + 5)
                        nc.vector.tensor_scalar(mx[c][:, :], bank[2 * b + c][:, :], TINY, None, ALU.max).then_inc(rec_seq, 1)
                        dve.wait_ge(dT_ready, 2 * s + c + 1)
                        nc.vector.tensor_tensor(dT[c][:, :], dT[c][:, :], dv[c][:, :], ALU.max).then_inc(dmax, 1)
                        dve.wait_ge(dmax, 2 * s + c + 1)
                        nc.vector.scalar_tensor_tensor(dT[c][:, :], bank[2 * b + c][:, :], 0.0, dT[c][:, :],
                                                       ALU.not_equal, ALU.mult).then_inc(num_free, 1)
                        dve.wait_ge(rec_seq, 2 * s + c + 1)
                        dve.wait_ge(num_free, 2 * s + c + 5)
                        nc.vector.reciprocal(mx[c][:, :], mx[c][:, :]).then_inc(rec_ready, 1)

                def second_half():
                    dve.wait_ge(num_bank, 2 * T + 4)
                    narrow(1, range(T))

                steps(dve, leaky_step, rec_step, second_half)
                dve.wait_ge(un_ready, 4)
                for q in range(NG - 1):
                    split(Un[:, group(q), :], pcs3, q, rest3)

            def one_hot3(it, b):
                dve.wait_ge(g3_used, it + 1)
                if not isinstance(it, int):
                    apart(dve)
                nc.vector.tensor_tensor(G3[b][:, :, :], iota[:, :].unsqueeze(1).to_broadcast([P, T, P]),
                                        slotb[:, bass.ds(it, 1), :].rearrange("p o j -> p (o j)").unsqueeze(2)
                                        .to_broadcast([P, T, P]), ALU.is_equal).then_inc(g3_ready, 1)

            def edges3(it, b):
                dve.wait_ge(g3_used, it + 3)
                dve.wait_ge(num3_bank, 4 * it + 4)
                nc.vector.tensor_copy(ATc3[b][:, :, :].rearrange("p c i -> p (c i)"), bank[4 + b][:, 0:NC * P])
                pieces = bank[4 + b][:, NC * P:NC * P + 3 * NC].rearrange("p (c k) -> p c k", k=3)
                r_of = rc[b][:, :].unsqueeze(2)
                if within(it, -2):
                    dve.wait_ge(u3_ready, 3 * it - 3)
                nc.vector.tensor_copy(r_of, pieces[:, :, 2:3]).then_inc(rc_seq, 1)
                dve.wait_ge(rc_seq, 3 * it + 1)
                nc.vector.tensor_tensor(r_of, r_of, pieces[:, :, 1:2], ALU.add).then_inc(rc_seq, 1)
                dve.wait_ge(rc_seq, 3 * it + 2)
                nc.vector.tensor_tensor(r_of, r_of, pieces[:, :, 0:1], ALU.add).then_inc(rc_seq, 1)
                dve.wait_ge(rc_seq, 3 * it + 3)
                dve.sem_inc(e3_copied, 1)

            def den3(it, b, c):
                dve.wait_ge(er_ready, it + 1)
                dve.wait_ge(u3_ready, 3 * it + c + 1)
                nc.vector.scalar_tensor_tensor(denc[b][:, c, :], E01[:, :], er[b][:, c:c + 1], denc[b][:, c, :],
                                               ALU.mult, ALU.max).then_inc(denc_ready, 1)

            def times_y(it, b, c):
                n = 4 * it + c
                dve.wait_ge(y_ready, n + 1)
                dve.wait_ge(att3_ready, n + 7)
                nc.vector.tensor_tensor(tc[c % 2][:, :], bank[c][:, :], yc[b][c][:, :], ALU.mult).then_inc(t_ready, 1)

            def leaky3(it, b):
                dve.wait_ge(z3_ready, it + 1)
                z = dTc[b][:, :, :].rearrange("p j i -> p (j i)")
                nc.vector.scalar_tensor_tensor(z, z, 0.01, z, ALU.mult, ALU.max).then_inc(z3_leaky, 1)

            def keep3(it, b):
                dve.wait_ge(att3_used, 4 * it + 12)
                if not isinstance(it, int):
                    apart(dve)
                nc.vector.tensor_tensor(Un[:, bass.ds(it, 1), :].rearrange("p o f -> p (o f)"), bank[6 + b][:, 0:D],
                                        mk[:, bass.ds(it, 1)].to_broadcast([P, D]), ALU.mult).then_inc(un3_kept, 1)

            def tile3(it, b):
                if within(it, 2):
                    one_hot3(it + 2, b)
                for c in range(4):
                    if within(it, 1):
                        if c < NC:
                            den3(it + 1, 1 - b, c)
                        else:
                            leaky3(it + 1, 1 - b)
                    times_y(it, b, c)
                    if c == 2 and within(it, 2):
                        edges3(it + 2, b)
                    if not within(it, 1) and c < NG - 1:
                        if c == 0:
                            dve.wait_ge(un3_kept, GT * (NG - 1) + 2)
                        split(Un[:, group(c), :], pcs3, c, rest3)
                if within(it, -1):
                    keep3(it - 1, 1 - b)

            def by_slots3():
                one_hot3(0, 0)
                nc.vector.tensor_copy(rp[:, :, 0:1], r3[:, :].unsqueeze(2)).then_inc(rp_ready, 1)
                nc.vector.memset(Eb[:, :, :], 0.0).then_inc(rp_ready, 1)
                dve.wait_ge(rp_ready, 2)
                nc.vector.tensor_tensor(deg[:, :].unsqueeze(2), r3[:, :].unsqueeze(2), rp[:, :, 0:1],
                                        ALU.subtract).then_inc(rp_ready, 1)
                dve.wait_ge(rp_ready, 3)
                nc.vector.tensor_copy(rp[:, :, 1:2], deg[:, :].unsqueeze(2)).then_inc(rp_ready, 1)
                nc.vector.tensor_scalar(Eb[:, :, P - 1:P], mk[:, :].unsqueeze(2), 1.0, None, ALU.add)
                dve.wait_ge(rp_ready, 4)
                nc.vector.tensor_tensor(rp[:, :, 2:3], deg[:, :].unsqueeze(2), rp[:, :, 1:2],
                                        ALU.subtract).then_inc(rp_ready, 1)
                one_hot3(1, 1)
                edges3(0, 0)
                dve.wait_ge(e01_ready, 1)
                for c in range(NC):
                    den3(0, 0, c)
                edges3(1, 1)
                leaky3(0, 0)
                sweep(dve, tile3)
                keep3(T - 1, 1)
                dve.wait_ge(un3_kept, T + 2)

            choose(dve, 3, *counted(by_slots3, over_all3))
            split(Un[:, group(NG - 1), :], pcs3, NG - 1, rest3)
            for q in range(NG):
                dve.wait_ge(mm_copied, 3 * T + GT * q + GT + 2)
                join(accs3, 3, q, s3)
                nc.vector.tensor_tensor(X[:, group(q), :], X[:, group(q), :], s3[:, :, :], ALU.add).then_inc(x_final, 1)
                dve.wait_ge(x_final, q + 1)


_INS = ["x", "adj", "L0_gnn_weight", "L0_gnn_att_weight", "L2_gnn_W", "L3_gnn_W", "L3_gnn_a"]


def kernel(**inputs):
    import numpy as np
    import concourse.bacc as bacc
    from concourse import mybir as mb
    from concourse.bass_utils import run_bass_kernel_spmd

    nc = bacc.Bacc("TRN2", target_bir_lowering=False, num_devices=1, dynamic_dma_scratch_size=1024)
    arrays, args = {}, []
    for name in _INS:
        a = np.ascontiguousarray(inputs[name])
        arrays[f"in_{name}"] = a
        args.append(nc.dram_tensor(f"in_{name}", a.shape, mb.dt.from_np(a.dtype), kind="ExternalInput").ap())
    args.append(nc.dram_tensor("out_0", (N, D), mb.dt.float32, kind="ExternalOutput").ap())
    gnn_stack(nc, *args)
    r = run_bass_kernel_spmd(nc, [arrays], core_ids=[0])
    return r.results[0]["out_0"]
```
